# Optimizing a Trainium2 kernel written in Bass

```python
import numpy as np
import jax
import jax.numpy as jnp

def _softmax(x, axis=-1):
    return jax.nn.softmax(x, axis=axis)

def _gelu(x):
    return jax.nn.gelu(x, approximate=True)

def _silu(x):
    return jax.nn.silu(x)

def _sigmoid(x):
    return jax.nn.sigmoid(x)

def _layernorm(x, axis=-1, eps=1e-05):
    m = jnp.mean(x, axis=axis, keepdims=True)
    v = jnp.var(x, axis=axis, keepdims=True)
    return (x - m) / jnp.sqrt(v + eps)

def _scatter_add(tgt, idx, src, axis=0):
    return tgt.at[idx].add(src)

def _segment_sum(src, seg, n):
    return jax.ops.segment_sum(src, seg, n)
kernel_name = 'mk_sandwich_d1_jaxref_r4_22767d'

def setup_inputs(seed: int=0):
    np.random.seed(seed)
    _w = jnp.asarray

    def _L0_attn_setup():
        import jax, jax.numpy as jnp
        import numpy as np
        B, T, C = (1, 1024, 512)
        H = 16
        D = C // H
        BLOCK = 64
        WINDOW = 256
        DILATION = 64
        GLOBAL_TOKENS = 128
        ROPE_BASE = 10000.0
        SCALE = 1.0 / np.sqrt(D)

        def _rope(x):
            t = jnp.arange(x.shape[2], dtype=jnp.float32)
            inv_freq = 1.0 / ROPE_BASE ** (jnp.arange(0, D, 2, dtype=jnp.float32) / D)
            freqs = jnp.outer(t, inv_freq)
            emb = jnp.concatenate([freqs, freqs], axis=-1)
            cos = jnp.cos(emb)[None, None].astype(x.dtype)
            sin = jnp.sin(emb)[None, None].astype(x.dtype)
            x1, x2 = jnp.split(x, 2, axis=-1)
            rot = jnp.concatenate([-x2, x1], axis=-1)
            return x * cos + rot * sin

        def _token_mask(seq_len):
            nb = (seq_len + BLOCK - 1) // BLOCK
            bp = jnp.arange(nb)
            qb, kb = (bp[:, None], bp[None, :])
            dist = qb - kb
            window_blocks = WINDOW // BLOCK
            window_mask = (dist >= 0) & (dist <= window_blocks)
            global_blocks = max(1, GLOBAL_TOKENS // BLOCK)
            global_mask = kb < global_blocks
            dilation_blocks = max(1, DILATION // BLOCK)
            dilated_mask = kb % dilation_blocks == 0
            causal_mask = kb <= qb
            block_mask = (window_mask | global_mask | dilated_mask) & causal_mask
            tok = jnp.repeat(jnp.repeat(block_mask, BLOCK, axis=0), BLOCK, axis=1)
            return tok[:seq_len, :seq_len]
        key = jax.random.key(seed)
        ks = jax.random.split(key, 5)
        x = jax.random.normal(ks[0], (B, T, C), dtype=jnp.float32)
        w_q = jax.random.normal(ks[1], (C, C), dtype=jnp.float32) * 0.02
        w_k = jax.random.normal(ks[2], (C, C), dtype=jnp.float32) * 0.02
        w_v = jax.random.normal(ks[3], (C, C), dtype=jnp.float32) * 0.02
        w_o = jax.random.normal(ks[4], (C, C), dtype=jnp.float32) * 0.02
        return {'x': x, 'w_q': w_q, 'w_k': w_k, 'w_v': w_v, 'w_o': w_o}
    _L0_attn_in = _L0_attn_setup()

    def _L0_ffn_setup():
        import jax, jax.numpy as jnp
        import numpy as np
        B, S, H = (2, 512, 512)
        E, K, F = (32, 4, 352)
        FS = 1408
        EPS = 1e-06
        CAP = 256
        key = jax.random.key(seed)
        ks = jax.random.split(key, 10)
        s = 0.02
        return {'hidden_states': jax.random.normal(ks[0], (B, S, H), jnp.float32), 'w_norm': 1.0 + 0.02 * jax.random.normal(ks[1], (H,), jnp.float32), 'w_router': s * jax.random.normal(ks[2], (H, E), jnp.float32), 'w_gate': s * jax.random.normal(ks[3], (E, H, F), jnp.float32), 'w_up': s * jax.random.normal(ks[4], (E, H, F), jnp.float32), 'w_down': s * jax.random.normal(ks[5], (E, F, H), jnp.float32), 'sw_gate': s * jax.random.normal(ks[6], (H, FS), jnp.float32), 'sw_up': s * jax.random.normal(ks[7], (H, FS), jnp.float32), 'sw_down': s * jax.random.normal(ks[8], (FS, H), jnp.float32), 'w_shared_gate': s * jax.random.normal(ks[9], (H, 1), jnp.float32)}
    _L0_ffn_in = _L0_ffn_setup()
    _d = {'L0_attn_x': _L0_attn_in['x'], 'L0_attn_w_q': _L0_attn_in['w_q'], 'L0_attn_w_k': _L0_attn_in['w_k'], 'L0_attn_w_v': _L0_attn_in['w_v'], 'L0_attn_w_o': _L0_attn_in['w_o'], 'L0_ffn_w_norm': _L0_ffn_in['w_norm'], 'L0_ffn_w_router': _L0_ffn_in['w_router'], 'L0_ffn_w_gate': _L0_ffn_in['w_gate'], 'L0_ffn_w_up': _L0_ffn_in['w_up'], 'L0_ffn_w_down': _L0_ffn_in['w_down'], 'L0_ffn_sw_gate': _L0_ffn_in['sw_gate'], 'L0_ffn_sw_up': _L0_ffn_in['sw_up'], 'L0_ffn_sw_down': _L0_ffn_in['sw_down'], 'L0_ffn_w_shared_gate': _L0_ffn_in['w_shared_gate']}
    _x0 = _d['L0_attn_x']
    _d['L0_attn_x'] = jax.random.normal(jax.random.fold_in(jax.random.key(seed), 1), (1, 2048, 512), dtype=_x0.dtype)
    del _x0
    return _d

def reference(L0_attn_x, L0_attn_w_q, L0_attn_w_k, L0_attn_w_v, L0_attn_w_o, L0_ffn_w_norm, L0_ffn_w_router, L0_ffn_w_gate, L0_ffn_w_up, L0_ffn_w_down, L0_ffn_sw_gate, L0_ffn_sw_up, L0_ffn_sw_down, L0_ffn_w_shared_gate):

    def _L0_attn_ref(x, w_q, w_k, w_v, w_o):
        import jax, jax.numpy as jnp
        import numpy as np
        B, T, C = (1, 1024, 512)
        H = 16
        D = C // H
        BLOCK = 64
        WINDOW = 256
        DILATION = 64
        GLOBAL_TOKENS = 128
        ROPE_BASE = 10000.0
        SCALE = 1.0 / np.sqrt(D)

        def _rope(x):
            t = jnp.arange(x.shape[2], dtype=jnp.float32)
            inv_freq = 1.0 / ROPE_BASE ** (jnp.arange(0, D, 2, dtype=jnp.float32) / D)
            freqs = jnp.outer(t, inv_freq)
            emb = jnp.concatenate([freqs, freqs], axis=-1)
            cos = jnp.cos(emb)[None, None].astype(x.dtype)
            sin = jnp.sin(emb)[None, None].astype(x.dtype)
            x1, x2 = jnp.split(x, 2, axis=-1)
            rot = jnp.concatenate([-x2, x1], axis=-1)
            return x * cos + rot * sin

        def _token_mask(seq_len):
            nb = (seq_len + BLOCK - 1) // BLOCK
            bp = jnp.arange(nb)
            qb, kb = (bp[:, None], bp[None, :])
            dist = qb - kb
            window_blocks = WINDOW // BLOCK
            window_mask = (dist >= 0) & (dist <= window_blocks)
            global_blocks = max(1, GLOBAL_TOKENS // BLOCK)
            global_mask = kb < global_blocks
            dilation_blocks = max(1, DILATION // BLOCK)
            dilated_mask = kb % dilation_blocks == 0
            causal_mask = kb <= qb
            block_mask = (window_mask | global_mask | dilated_mask) & causal_mask
            tok = jnp.repeat(jnp.repeat(block_mask, BLOCK, axis=0), BLOCK, axis=1)
            return tok[:seq_len, :seq_len]
        Bc, Tc, Cc = x.shape
        q = (x @ w_q.T).reshape(Bc, Tc, H, D).transpose(0, 2, 1, 3)
        k = (x @ w_k.T).reshape(Bc, Tc, H, D).transpose(0, 2, 1, 3)
        v = (x @ w_v.T).reshape(Bc, Tc, H, D).transpose(0, 2, 1, 3)
        q = _rope(q)
        k = _rope(k)
        scores = jnp.einsum('bhqd,bhkd->bhqk', q, k) * SCALE
        tok_mask = _token_mask(Tc)
        scores = jnp.where(tok_mask[None, None], scores, -jnp.inf)
        attn = jax.nn.softmax(scores, axis=-1)
        ctx = jnp.einsum('bhqk,bhkd->bhqd', attn, v)
        ctx = ctx.transpose(0, 2, 1, 3).reshape(Bc, Tc, Cc)
        return ctx @ w_o.T

    def _L0_ffn_ref(hidden_states, w_norm, w_router, w_gate, w_up, w_down, sw_gate, sw_up, sw_down, w_shared_gate):
        import jax, jax.numpy as jnp
        import numpy as np
        B, S, H = (2, 512, 512)
        E, K, F = (32, 4, 352)
        FS = 1408
        EPS = 1e-06
        CAP = 256
        inp = hidden_states
        xf = inp.astype(jnp.float32)
        var = jnp.mean(xf * xf, axis=-1, keepdims=True)
        x = (w_norm * (xf * jax.lax.rsqrt(var + EPS))).astype(inp.dtype)
        Bq, Sq, Hq = x.shape
        x = x.reshape(-1, Hq)
        T = Bq * Sq
        logits = x @ w_router
        probs = jax.nn.softmax(logits.astype(jnp.float32), axis=-1)
        w_topk, sel = jax.lax.top_k(probs, K)
        w_topk = w_topk.astype(x.dtype)
        flat_e = sel.reshape(-1)
        order = jnp.argsort(flat_e)
        sorted_e = flat_e[order]
        counts = jnp.zeros((E,), jnp.int32).at[flat_e].add(1)
        starts = jnp.cumsum(counts) - counts
        pos = jnp.arange(T * K) - starts[sorted_e]
        tok = order // K
        valid = pos < CAP
        dest = jnp.where(valid, pos, CAP)
        buf = jnp.zeros((E, CAP + 1, Hq), x.dtype).at[sorted_e, dest].set(x[tok])
        buf = buf[:, :CAP]
        g = jnp.einsum('ech,ehf->ecf', buf, w_gate)
        u = jnp.einsum('ech,ehf->ecf', buf, w_up)
        y = jnp.einsum('ecf,efh->ech', jax.nn.silu(g) * u, w_down)
        wv = w_topk.reshape(-1)[order] * valid.astype(x.dtype)
        gath = y[sorted_e, jnp.minimum(pos, CAP - 1)]
        out = jnp.zeros((T, Hq), x.dtype).at[tok].add(gath * wv[:, None])
        sh = jax.nn.silu(x @ sw_gate) * (x @ sw_up) @ sw_down
        sh = jax.nn.sigmoid(x @ w_shared_gate) * sh
        out = out + sh
        return inp + out.reshape(Bq, Sq, Hq)
    x = L0_attn_x
    x = x + _layernorm(_L0_attn_ref(_layernorm(x, axis=-1), L0_attn_w_q, L0_attn_w_k, L0_attn_w_v, L0_attn_w_o), axis=-1)
    x = x + _layernorm(_L0_ffn_ref(_layernorm(x, axis=-1), L0_ffn_w_norm, L0_ffn_w_router, L0_ffn_w_gate, L0_ffn_w_up, L0_ffn_w_down, L0_ffn_sw_gate, L0_ffn_sw_up, L0_ffn_sw_down, L0_ffn_w_shared_gate), axis=-1)
    return x

_drawn_inputs = setup_inputs


def setup_inputs(seed=0):
    import zlib

    import numpy as np

    out = dict(_drawn_inputs(seed))
    spreads = {}
    factors = {'L0_ffn_w_norm': 8.0,
     'L0_ffn_w_router': 8.0,
     'L0_ffn_w_gate': 8.0,
     'L0_ffn_w_up': 8.0,
     'L0_ffn_w_down': 8.0,
     'L0_ffn_sw_gate': 3.537,
     'L0_ffn_sw_up': 3.52,
     'L0_ffn_sw_down': 3.51,
     'L0_ffn_w_shared_gate': 8.0}
    for name, (base, spread) in spreads.items():
        noise = np.random.default_rng([zlib.crc32(name.encode()), seed]).standard_normal(out[name].shape)
        drawn = base * np.exp(spread * noise) if base else spread * noise
        out[name] = jnp.asarray(drawn.astype(out[name].dtype))
    for name, factor in factors.items():
        out[name] = (out[name] * factor).astype(out[name].dtype)
    return out
```

```python
from contextlib import ExitStack

import concourse.bass as bass
from concourse import mybir

P = 128
F32 = mybir.dt.float32
F32R = mybir.dt.float32r
BF16 = mybir.dt.bfloat16
I32 = mybir.dt.int32
U32 = mybir.dt.uint32
ALU = mybir.AluOpType
ACT = mybir.ActivationFunctionType
AX = mybir.AxisListType
ds = bass.ds

T, C = 2048, 512
NT, KC = T // P, C // P
H, D = 16, 32
HG = P // D
NG = H // HG
QC = 512
NQ = T // QC
QT = QC // P
HALF = 64
BIG = -1.0e30
LN_EPS, RMS_EPS = 1e-5, 1e-6
E, K, F, CAP = 32, 4, 352, 256
FS = 1408
NFS = FS // P
FT = [(0, 128), (128, 128), (256, 96)]
SLOTS = E * CAP


class Chain:

    def __init__(self, eng, sem, base=0):
        self.eng, self.sem, self.base, self.n = eng, sem, base, 0

    def link(self, ins):
        ins.then_inc(self.sem, 1)
        self.n += 1
        self.eng.wait_ge(self.sem, self.base + self.n)

    def done(self, per):
        assert self.n == per, (self.n, per)


def hold(eng, held):
    eng.sem_inc(held, 1)


class Mem:

    def __init__(self, nc, ctx):
        self.nc, self.ctx = nc, ctx

    def sb(self, name, shape, dt=F32):
        return self.ctx.enter_context(self.nc.sbuf_tensor(name, shape, dt))

    def ps(self, name, shape, dt=F32):
        return self.ctx.enter_context(self.nc.psum_tensor(name, shape, dt))

    def sem(self, name):
        return self.ctx.enter_context(self.nc.semaphore(name))


def norm_and_transpose(nc, x_dram, identity_dram, ident, neg_half, xnT):
    with ExitStack() as ctx:
        m = Mem(nc, ctx)
        xt = m.sb("a_x", [P, 2, C])
        xn = m.sb("a_xn", [P, 2, C])
        stats = m.sb("a_stats", [P, 2, 6])
        mv = m.sb("a_mean_var", [P, 2, 2])
        veps = m.sb("a_var_eps", [P, 2])
        rstd = m.sb("a_rstd", [P, 2])
        held = m.sem("a_held")
        tp = m.ps("a_tp", [P, 2, KC, P])
        ident_ready, consts_ready = m.sem("a_ident_ready"), m.sem("a_consts_ready")
        x_ready = [m.sem(f"a_x_ready{b}") for b in range(2)]
        xn_done = m.sem("a_xn_done")
        var_ready, rstd_ready = m.sem("a_var_ready"), m.sem("a_rstd_ready")
        tp_ready = m.sem("a_tp_ready")
        tp_copied = m.sem("a_tp_copied")
        chain = m.sem("a_dve_chain")
        block = ctx.enter_context(nc.Block())

        @block.sync
        def _(sp):
            sp.dma_start(ident[:], identity_dram).then_inc(ident_ready, 16)
            with sp.Fori(0, NT // 2) as i:
                row = [sp.snap(i * (2 * P) + b * P) for b in range(2)]
                for b in range(2):
                    sp.wait_ge(xn_done, i * 2 + (b + 1))
                    sp.dma_start(xt[:, b], x_dram[ds(row[b], P), :]).then_inc(x_ready[b], 16)

        @block.vector
        def _(dve):
            dve.sem_inc(xn_done, 2)
            dve.memset(neg_half[:], -0.5).then_inc(consts_ready, 1)
            with dve.Fori(0, NT // 2) as i:
                c = Chain(dve, chain, i * 4)
                for b in range(2):
                    dve.wait_ge(x_ready[b], i * 16 + 16)
                    c.link(dve.bn_stats(stats[:, b], xt[:, b]))
                    hold(dve, held)
                    c.link(dve.bn_aggr(mv[:, b], stats[:, b]))
                    dve.tensor_scalar(veps[:, b:b + 1], mv[:, b, 1:2], LN_EPS, None,
                                      ALU.add).then_inc(var_ready, 1)
                for b in range(2):
                    dve.wait_ge(rstd_ready, i * 2 + (b + 1))
                    dve.wait_ge(tp_ready, i * 2 + (b + 1))
                    dve.tensor_scalar(xn[:, b], xt[:, b], mv[:, b, 0:1], rstd[:, b:b + 1],
                                      ALU.subtract, ALU.mult).then_inc(xn_done, 1)
                c.done(4)

        @block.gpsimd
        def _(pool):
            pool.wait_ge(consts_ready, 1)
            with pool.Fori(0, NT // 2) as i:
                for b in range(2):
                    pool.wait_ge(var_ready, i * 2 + (b + 1))
                    pool.tensor_tensor(rstd[:, b:b + 1], veps[:, b:b + 1], neg_half[:],
                                       ALU.pow).then_inc(rstd_ready, 1)

        @block.tensor
        def _(pe):
            pe.sem_inc(tp_ready, 2)
            pe.wait_ge(ident_ready, 16)
            with pe.Fori(0, NT // 2) as i:
                for b in range(2):
                    pe.wait_ge(xn_done, i * 2 + (b + 3))
                    pe.wait_ge(tp_copied, i * 2 + (b + 1))
                    for k in range(KC):
                        last = pe.transpose(tp[:, b, k], xn[:, b, k * P:(k + 1) * P], ident[:])
                    last.then_inc(tp_ready, 1)

        @block.scalar
        def _(act):
            act.sem_inc(tp_copied, 2)
            with act.Fori(0, NT // 2) as i:
                for b in range(2):
                    act.wait_ge(tp_ready, i * 2 + (b + 3))
                    act.copy(xnT[:, :, ds(i * (2 * P) + b * P, P)], tp[:, b]).then_inc(tp_copied, 1)


def attention(nc, wq_t, wk_t, wv_t, cos_dram, sin_dram, rotate_dram, ctx_dram, ident, xnT):
    scale = float(D) ** -0.5
    steps = [[(kt, max(0, kt - QT * qc) * P) for kt in range(QT * (qc + 1))] for qc in range(NQ)]
    n_steps = sum(map(len, steps))
    first_step = [sum(map(len, steps[:qc])) for qc in range(NQ)]
    units = [[(qt, kc, j, min(QC, (qt + 1) * P - kc * QC))
              for qt in range(QT * qc, QT * (qc + 1)) for kc in range(qc + 1) for j in range(HG)]
             for qc in range(NQ)]
    n_mx = sum(map(len, units)) + NQ
    n_rope = 2 * NQ
    M_ROW = 3 * D

    with ExitStack() as ctx:
        m = Mem(nc, ctx)
        cos, sin = m.sb("rope_cos", [P, T]), m.sb("rope_sin", [P, T])
        rotate = m.sb("rope_rotate", [P, P])
        wq, wk = m.sb("wq_g", [P, KC, P]), m.sb("wk_g", [P, KC, P])
        wv = m.sb("wv_g", [P, KC, P])
        raw = m.sb("rope_raw", [P, 2, QC])
        by_cos, by_sin = m.sb("rope_by_cos", [P, 2, QC]), m.sb("rope_by_sin", [P, 2, QC])
        hilo = [m.sb(f"hilo_{s}", [P, 2, T], F32R) for s in "qk"]
        stack = [[m.sb(f"stack_{s}{j}", [P, T], F32R) for j in range(HG)] for s in "qk"]
        v = m.sb("v_g", [P, NT, P])
        probs = [m.sb(f"probs{b}", [P, HG, QC]) for b in range(2)]
        rden = m.sb("rden", [P, QC])
        ctxs = [m.sb(f"ctx{b}", [P, QC]) for b in range(2)]
        tops = m.sb("tops", [P, NT, HG, NQ])
        negmax = m.sb("negmax", [P, QT, HG])
        negmax_hi = m.sb("negmax_hi", [P, QT, HG], F32R)
        spread = m.sb("negmax_spread", [P, QT, P])
        max_rows = m.sb("max_rows", [P, QC], F32R)
        ones = m.sb("ones_d", [P, D])
        first_half = m.sb("first_half", [P, P], BF16)
        second_half = m.sb("second_half", [P, P], BF16)
        first_big = m.sb("first_big", [P, P], BF16)
        second_big = m.sb("second_big", [P, P], BF16)
        out_banks = [m.ps("pv", [P, QC]), m.ps("den", [P, QC])]
        pv, den = out_banks
        mx = m.ps("mx", [P, 2, QC])
        st = m.ps("st", [P, HG, QC])

        consts_in, w_in, masks_set = m.sem("b_consts_in"), m.sem("b_w_in"), m.sem("b_masks_set")
        zeros_set, held = m.sem("b_zeros_set"), m.sem("b_held")
        qk_projected, v_projected = m.sem("b_qk_projected"), m.sem("b_v_projected")
        raw_copied, v_copied = m.sem("b_raw_copied"), m.sem("b_v_copied")
        rotated, cos_done, split_done = m.sem("b_rotated"), m.sem("b_cos_done"), m.sem("b_split_done")
        added = m.sem("b_added")
        stack_in = [m.sem("b_stack_q_in"), m.sem("b_stack_k_in")]
        mx_ready, negmax_split = m.sem("b_mx_ready"), m.sem("b_negmax_split")
        mx_free = m.sem("b_mx_free")
        max_rows_set, max_rows_in = m.sem("b_max_rows_set"), m.sem("b_max_rows_in")
        st_ready, exp_done, pv_done = m.sem("b_st_ready"), m.sem("b_exp_done"), m.sem("b_pv_done")
        ctx_ready = m.sem("b_ctx_ready")
        ctx_stored = [m.sem(f"b_ctx_stored{b}") for b in range(2)]
        chain = m.sem("b_dve_chain")
        block = ctx.enter_context(nc.Block())

        @block.sync
        def _(sp):
            sp.dma_start(cos[:], cos_dram).then_inc(consts_in, 16)
            sp.dma_start(sin[:], sin_dram).then_inc(consts_in, 16)
            sp.dma_start(rotate[:], rotate_dram).then_inc(consts_in, 16)
            with sp.Fori(0, NG) as g:
                channel, steps_before = sp.snap(g * P), sp.snap(g * n_steps)
                sp.wait_ge(v_projected, g * NQ + 1)
                for w, w_dram in ((wq, wq_t), (wk, wk_t), (wv, wv_t)):
                    sp.dma_start(w[:], w_dram.rearrange("(k p) n -> p k n", p=P)[:, :, ds(channel, P)])\
                        .then_inc(w_in, 16)
                for s in range(2):
                    sp.wait_ge(split_done, g * n_rope + NQ * (s + 1))
                    if s == 0:
                        hold(sp, held)
                        sp.wait_ge(pv_done, steps_before + 1)
                    for r, part in enumerate(((0, 0, 1), (0, 1, 0))[s]):
                        for j in range(HG):
                            sp.dma_start(stack[s][j][r * D:(r + 1) * D, :].bitcast(F32),
                                         hilo[s][j * D:(j + 1) * D, part, :].bitcast(F32)).then_inc(stack_in[s], 16)

                def max_rows_of(qc):
                    sp.wait_ge(max_rows_set, g * NQ + (qc + 1))
                    for j in range(HG):
                        sp.dma_start(stack[0][j][M_ROW:M_ROW + 2, qc * QC:(qc + 1) * QC].bitcast(F32),
                                     max_rows[j * D:j * D + 2, :].bitcast(F32)).then_inc(max_rows_in, 16)

                max_rows_of(0)
                for qc in range(NQ):
                    if qc + 1 < NQ:
                        max_rows_of(qc + 1)
                    sp.wait_ge(ctx_ready, g * NQ + (qc + 2))
                    sp.dma_start(ctx_dram[ds(channel, P), qc * QC:(qc + 1) * QC],
                                 ctxs[qc % 2][:]).then_inc(ctx_stored[qc % 2], 16)
            for b in range(2):
                sp.wait_ge(ctx_stored[b], 16 * NG * NQ // 2 + 1)

        @block.gpsimd
        def _(pool):
            setup = Chain(pool, masks_set)
            for t in (first_half, second_half, first_big, second_big):
                setup.link(pool.memset(t[:], 0.0))
            setup.link(pool.memset(ones[:], 1.0))
            setup.link(pool.memset(first_half[0:1, 0:HALF], 1.0))
            setup.link(pool.memset(second_half[0:1, HALF:P], 1.0))
            setup.link(pool.memset(first_big[0:1, 0:HALF], BIG))
            setup.link(pool.memset(second_big[0:1, HALF:P], BIG))
            for j in range(HG):
                setup.link(pool.memset(stack[1][j][M_ROW:P, :].bitcast(F32), 1.0))
            pool.wait_ge(consts_in, 48)
            with pool.Fori(0, NG) as g:
                for u in range(n_rope):
                    b, tc = u % 2, u % NQ
                    pool.wait_ge(raw_copied, g * n_rope + (u + 1))
                    if u >= 2:
                        pool.wait_ge(added, g * n_rope + (u - 1))
                    pool.tensor_tensor(by_cos[:, b], raw[:, b], cos[:, tc * QC:(tc + 1) * QC],
                                       ALU.mult).then_inc(cos_done, 1)

        @block.tensor
        def _(pe):
            pe.wait_ge(consts_in, 48)
            pe.wait_ge(masks_set, 9 + HG)

            with pe.Fori(0, NG) as g:
                def project(u):
                    s, tc = u // NQ, u % NQ
                    if u >= 2:
                        pe.wait_ge(raw_copied, g * n_rope + (u - 1))
                    for k in range(KC):
                        last = pe.matmul(out_banks[u % 2][:], (wq, wk)[s][:, k], xnT[:, k, tc * QC:(tc + 1) * QC],
                                         start=(k == 0), stop=(k == KC - 1))
                    last.then_inc(qk_projected, 1)

                def rotate_pairs(u):
                    pe.wait_ge(raw_copied, g * n_rope + (u + 1))
                    if u >= 2:
                        pe.wait_ge(split_done, g * n_rope + (u - 1))
                    pe.matmul(st[:, u % 2], rotate[:], raw[:, u % 2], start=True, stop=True)\
                        .then_inc(rotated, 1)

                def project_v(n):
                    if n >= 2:
                        pe.wait_ge(v_copied, g * NQ + (n - 1))
                    for t in range(QT):
                        for k in range(KC):
                            tok = (n * QT + t) * P
                            last = pe.matmul(st[:, 2 + n % 2, t * P:(t + 1) * P], xnT[:, k, tok:tok + P], wv[:, k],
                                             start=(k == 0), stop=(k == KC - 1))
                    last.then_inc(v_projected, 1)

                def max_unit(qc, n, use):
                    qt, kc, j, w = units[qc][n]
                    pe.wait_ge(mx_free, g * n_mx + (use + 1))
                    diagonal = (qt + 1) * P <= (kc + 1) * QC
                    last = pe.matmul(mx[:, use % 2, 0:w], stack[0][j][0:M_ROW, qt * P:(qt + 1) * P],
                                     stack[1][j][0:M_ROW, kc * QC:kc * QC + w], start=True, stop=not diagonal)
                    if diagonal:
                        last = pe.matmul(mx[:, use % 2, w - P:w], first_half[:], second_big[:],
                                         start=False, stop=True)
                    last.then_inc(mx_ready, 1)

                def turn_max(use):
                    pe.wait_ge(mx_free, g * n_mx + (use + 1))
                    pe.wait_ge(negmax_split, g * NQ + max_turned[0] + 1)
                    for t in range(QT):
                        last = pe.transpose(mx[:, use % 2, t * P:(t + 1) * P], spread[:, t], ident[:])
                    last.then_inc(mx_ready, 1)
                    max_turned[0] += 1

                def scores(qc, i):
                    kt, q0 = steps[qc][i]
                    s = first_step[qc] + i
                    diagonal = kt >= QT * qc
                    if i == 0:
                        pe.wait_ge(max_rows_in, g * (64 * NQ) + (64 * (qc + 1) + 1))
                    for pair in range(2):
                        if s:
                            pe.wait_ge(exp_done, g * (2 * n_steps) + (2 * s + pair - 1))
                        for j in (2 * pair, 2 * pair + 1):
                            last = pe.matmul(st[:, j, q0:QC], stack[1][j][0:M_ROW + 2, kt * P:(kt + 1) * P],
                                             stack[0][j][0:M_ROW + 2, qc * QC + q0:(qc + 1) * QC],
                                             start=True, stop=not diagonal)
                            if diagonal:
                                last = pe.matmul(st[:, j, q0:q0 + P], second_half[:], first_big[:],
                                                 start=False, stop=True)
                        last.then_inc(st_ready, 1)

                def weigh_values(qc, i):
                    kt, q0 = steps[qc][i]
                    s = first_step[qc] + i
                    pe.wait_ge(exp_done, g * (2 * n_steps) + (2 * s + 2))
                    if i == 0:
                        pe.wait_ge(ctx_ready, g * NQ + (qc + 1))
                    flags = dict(start=(i == 0), stop=(i == len(steps[qc]) - 1))
                    for j in range(HG):
                        pe.matmul(pv[j * D:(j + 1) * D, q0:QC], v[:, kt, j * D:(j + 1) * D],
                                  probs[s % 2][:, j, q0:QC], **flags)
                    for j in range(HG):
                        last = pe.matmul(den[j * D:(j + 1) * D, q0:QC], ones[:],
                                         probs[s % 2][:, j, q0:QC], **flags)
                    last.then_inc(pv_done, 1)

                pe.wait_ge(w_in, g * 48 + 48)
                pe.wait_ge(ctx_ready, g * NQ + 1)
                project(0)
                for u in range(1, n_rope):
                    project(u)
                    rotate_pairs(u - 1)
                rotate_pairs(n_rope - 1)
                for n in range(NQ):
                    project_v(n)
                max_turned = [0]
                use = 0
                pe.wait_ge(stack_in[0], g * (16 * 3 * HG) + (16 * 3 * HG + 1))
                pe.wait_ge(stack_in[1], g * (16 * 3 * HG) + (16 * 3 * HG + 1))
                for n in range(len(units[0])):
                    max_unit(0, n, use)
                    use += 1
                turn_max(use)
                use += 1
                pe.wait_ge(v_copied, g * NQ + NQ)
                before = None
                for qc in range(NQ):
                    n_i, n_u, done = len(steps[qc]), len(units[qc + 1]) if qc + 1 < NQ else 0, 0
                    for i in range(n_i):
                        scores(qc, i)
                        if i == n_i - 1 and n_u:
                            turn_max(use)
                            use += 1
                        if before:
                            weigh_values(*before)
                        before = (qc, i)
                        upto = n_u * min(i + 1, n_i - 2) // (n_i - 2)
                        while done < upto:
                            max_unit(qc + 1, done, use)
                            done, use = done + 1, use + 1
                weigh_values(*before)
                assert use == n_mx

        @block.scalar
        def _(act):
            with act.Fori(0, NG) as g:
                for u in range(n_rope):
                    act.wait_ge(qk_projected, g * n_rope + (u + 1))
                    if u >= 2:
                        act.wait_ge(rotated, g * n_rope + (u - 1))
                        act.wait_ge(cos_done, g * n_rope + (u - 1))
                    act.copy(raw[:, u % 2], out_banks[u % 2][:]).then_inc(raw_copied, 1)
                for n in range(NQ):
                    act.wait_ge(v_projected, g * NQ + (n + 2))
                    act.copy(v[:, n * QT:(n + 1) * QT, :],
                             st[:, 2 + n % 2].rearrange("p (t c) -> p t c", t=QT)).then_inc(v_copied, 1)
                for qc in range(NQ):
                    for i, (kt, q0) in enumerate(steps[qc]):
                        s = first_step[qc] + i
                        for pair in range(2):
                            heads = slice(2 * pair, 2 * pair + 2)
                            act.wait_ge(st_ready, g * (2 * n_steps) + (2 * s + pair + 1))
                            if s >= 2:
                                act.wait_ge(pv_done, g * n_steps + s)
                            act.activation(probs[s % 2][:, heads, q0:QC], st[:, heads, q0:QC], ACT.Exp,
                                           scale=scale).then_inc(exp_done, 1)

        @block.vector
        def _(dve):
            dve.memset(tops[:], -3.0e38).then_inc(zeros_set, 1)
            dve.memset(spread[:], 0.0).then_inc(zeros_set, 1)
            dve.wait_ge(zeros_set, 2)
            dve.wait_ge(consts_in, 48)
            dve.sem_inc(mx_free, 2)
            for started in (v_projected, pv_done, ctx_ready, max_rows_in, *stack_in, *ctx_stored):
                dve.sem_inc(started, 1)
            per = 2 * n_rope + 3 * NQ
            with dve.Fori(0, NG) as g:
                c = Chain(dve, chain, g * per)
                for u in range(n_rope):
                    s, b, tc = u // NQ, u % 2, u % NQ
                    cols = slice(tc * QC, (tc + 1) * QC)
                    dve.wait_ge(rotated, g * n_rope + (u + 1))
                    c.link(dve.tensor_tensor(by_sin[:, b], st[:, b], sin[:, cols], ALU.mult))
                    dve.wait_ge(cos_done, g * n_rope + (u + 1))
                    dve.tensor_tensor(by_sin[:, b], by_sin[:, b], by_cos[:, b], ALU.add).then_inc(added, 1)
                    dve.wait_ge(added, g * n_rope + (u + 1))
                    dve.wait_ge(stack_in[s], g * (16 * 3 * HG) + 1)
                    c.link(dve.tensor_copy(hilo[s][:, 0, cols], by_sin[:, b]))
                    dve.tensor_tensor(hilo[s][:, 1, cols], by_sin[:, b], hilo[s][:, 0, cols].bitcast(F32),
                                      ALU.subtract).then_inc(split_done, 1)

                state = {"use": 0}

                def max_of_units(qc):
                    for qt, kc, j, w in units[qc]:
                        dve.wait_ge(mx_ready, g * n_mx + (state["use"] + 1))
                        dve.tensor_reduce(tops[:, qt, j, kc:kc + 1], mx[:, state["use"] % 2, 0:w], AX.X,
                                          ALU.max).then_inc(mx_free, 1)
                        state["use"] += 1
                    dve.wait_ge(mx_free, g * n_mx + (state["use"] + 2))
                    lo_hi = spread[:].rearrange("p t (j r) -> p t j r", r=D)
                    c.link(dve.tensor_reduce(negmax[:], tops[:, QT * qc:QT * (qc + 1)], AX.X, ALU.max,
                                             negate=True))
                    c.link(dve.tensor_copy(negmax_hi[:], negmax[:]))
                    dve.tensor_copy(lo_hi[:, :, :, 0], negmax_hi[:].bitcast(F32))
                    dve.tensor_tensor(lo_hi[:, :, :, 1], negmax[:], negmax_hi[:].bitcast(F32),
                                      ALU.subtract).then_inc(negmax_split, 1)
                    dve.wait_ge(mx_ready, g * n_mx + (state["use"] + 1))
                    dve.wait_ge(max_rows_in, g * (64 * NQ) + (64 * qc + 1))
                    dve.tensor_copy(max_rows[:], mx[:, state["use"] % 2]).then_inc(mx_free, 1)
                    dve.wait_ge(mx_free, g * n_mx + (state["use"] + 3))
                    dve.sem_inc(max_rows_set, 1)
                    state["use"] += 1

                def normalise(qc):
                    dve.wait_ge(pv_done, g * n_steps + (first_step[qc] + len(steps[qc]) + 1))
                    c.link(dve.reciprocal(rden[:], den[:]))
                    dve.wait_ge(ctx_stored[qc % 2], g * (16 * NQ // 2) + (16 * (qc // 2) + 1))
                    dve.tensor_tensor(ctxs[qc % 2][:], pv[:], rden[:], ALU.mult).then_inc(ctx_ready, 1)

                max_of_units(0)
                for qc in range(NQ):
                    if qc + 1 < NQ:
                        max_of_units(qc + 1)
                    normalise(qc)
                c.done(per)


def layer_norms(nc, x_dram, ctx_dram, wo_t, w_norm_row, w_router, w_shared_gate, tokens_dram,
                ident, neg_half, x1, acc, xfT, logits):
    with ExitStack() as ctx:
        m = Mem(nc, ctx)
        ct, xt = m.sb("c_ctx", [P, 2, NG, P]), m.sb("c_x", [P, 2, C])
        wo = m.sb("c_wo", [P, KC, C])
        w_norm = m.sb("c_w_norm", [P, C])
        wr = m.sb("c_w_router", [P, KC, E + 1])
        x1s, h = m.sb("c_x1s", [P, 2, C]), m.sb("c_h", [P, 2, C])
        xo, sq, xf = m.sb("c_xo", [P, 2, C]), m.sb("c_sq", [P, 2, C]), m.sb("c_xf", [P, 2, C])
        xft = m.sb("c_xft", [P, 2, KC, P])
        stats, mv = m.sb("c_stats", [P, 2, 6]), m.sb("c_mv", [P, 2, 2])
        veps, rstd = m.sb("c_veps", [P, 2]), m.sb("c_rstd", [P, 2])
        mean_sq = m.sb("c_mean_sq", [P, 2])
        held = m.sem("c_held")
        ob, tp, lg = m.ps("c_o", [P, 2, C]), m.ps("c_tp", [P, 2, KC, P]), m.ps("c_lg", [P, 2, 512])
        w_in = m.sem("c_w_in")
        in_ready = [m.sem(f"c_in_ready{b}") for b in range(2)]
        o_ready = m.sem("c_o_ready")
        xo_done = m.sem("c_xo_done")
        x1_done = m.sem("c_x1_done")
        x1_kept, h_kept = m.sem("c_x1_kept"), m.sem("c_h_kept")
        h_done = m.sem("c_h_done")
        var_ready, rstd_ready = m.sem("c_var_ready"), m.sem("c_rstd_ready")
        xf_done = m.sem("c_xf_done")
        xf_stored = [m.sem(f"c_xf_stored{b}") for b in range(2)]
        turned = m.sem("c_turned")
        turn_copied = m.sem("c_turn_copied")
        xft_kept = m.sem("c_xft_kept")
        lg_ready = m.sem("c_lg_ready")
        lg_copied = m.sem("c_lg_copied")
        chain = m.sem("c_chain")
        block = ctx.enter_context(nc.Block())
        wr_dram = w_router.rearrange("(k p) e -> p k e", p=P)

        @block.sync
        def _(sp):
            sp.dma_start(wo[:], wo_t.rearrange("(k p) n -> p k n", p=P)).then_inc(w_in, 16)
            sp.dma_start(w_norm[:], w_norm_row.to_broadcast([P, C])).then_inc(w_in, 16)
            sp.dma_start(wr[:, :, 0:E], wr_dram).then_inc(w_in, 16)
            sp.dma_start(wr[:, :, E:E + 1], w_shared_gate.rearrange("(k p) e -> p k e", p=P),
                         allow_slow_non_contiguous=True).then_inc(w_in, 16)
            with sp.Fori(0, NT // 2) as i:
                row = [sp.snap(i * (2 * P) + b * P) for b in range(2)]
                for b in range(2):
                    sp.wait_ge(o_ready, i * 2 + (b + 1))
                    sp.wait_ge(x1_done, i * 2 + (b + 1))
                    sp.dma_start(ct[:, b], ctx_dram.rearrange("(g p) t -> p g t", p=P)[:, :, ds(row[b], P)])\
                        .then_inc(in_ready[b], 16)
                    sp.dma_start(xt[:, b], x_dram[ds(row[b], P), :]).then_inc(in_ready[b], 16)

        @block.tensor
        def _(pe):
            pe.sem_inc(o_ready, 2)
            pe.sem_inc(turned, 2)
            pe.sem_inc(lg_ready, 2)
            pe.wait_ge(w_in, 64)
            with pe.Fori(0, NT // 2) as i:
                for b in range(2):
                    pe.wait_ge(in_ready[b], i * 32 + 32)
                    pe.wait_ge(xo_done, i * 2 + (b + 1))
                    for k in range(KC):
                        last = pe.matmul(ob[:, b], ct[:, b, k], wo[:, k], start=(k == 0), stop=(k == KC - 1))
                    last.then_inc(o_ready, 1)
                for b in range(2):
                    pe.wait_ge(xf_done, i * 2 + (b + 1))
                    pe.wait_ge(turn_copied, i * 2 + (b + 1))
                    for k in range(KC):
                        last = pe.transpose(tp[:, b, k], xf[:, b, k * P:(k + 1) * P], ident[:])
                    last.then_inc(turned, 1)
                for b in range(2):
                    pe.wait_ge(turn_copied, i * 2 + (b + 3))
                    pe.wait_ge(lg_copied, i * 2 + (b + 1))
                    for k in range(KC):
                        last = pe.matmul(lg[:, b, 0:E + 1], xft[:, b, k], wr[:, k],
                                         start=(k == 0), stop=(k == KC - 1))
                    last.then_inc(lg_ready, 1)

        @block.scalar
        def _(act):
            act.sem_inc(turn_copied, 2)
            act.sem_inc(lg_copied, 2)
            act.sem_inc(x1_kept, 2)
            act.sem_inc(h_kept, 2)
            with act.Fori(0, NT // 2) as i:
                row = [act.snap(i * (2 * P) + b * P) for b in range(2)]
                for b in range(2):
                    act.wait_ge(x1_done, i * 2 + (b + 3))
                    hold(act, held)
                    act.copy(x1[:, ds(i * (2 * C) + b * C, C)], x1s[:, b]).then_inc(x1_kept, 1)
                for b in range(2):
                    act.wait_ge(h_done, i * 2 + (b + 1))
                    hold(act, held)
                    act.copy(acc[:, ds(i * (2 * C) + b * C, C)], h[:, b]).then_inc(h_kept, 1)
                for b in range(2):
                    act.wait_ge(xf_done, i * 2 + (b + 1))
                    act.dma_start(tokens_dram[ds(row[b], P), :], xf[:, b]).then_inc(xf_stored[b], 16)
                for b in range(2):
                    act.wait_ge(turned, i * 2 + (b + 3))
                    act.wait_ge(lg_ready, i * 2 + (b + 1))
                    act.wait_ge(xft_kept, i * 2 + (b + 1))
                    act.copy(xft[:, b], tp[:, b]).then_inc(turn_copied, 1)
                for b in range(2):
                    act.wait_ge(lg_ready, i * 2 + (b + 3))
                    act.copy(logits[:, ds(i * (2 * (E + 1)) + b * (E + 1), E + 1)],
                             lg[:, b, 0:E + 1]).then_inc(lg_copied, 1)
            for b in range(2):
                act.wait_ge(xf_stored[b], 16 * NT // 2 + 1)

        @block.gpsimd
        def _(pool):
            pool.sem_inc(xft_kept, 2)
            with pool.Fori(0, NT // 2) as i:
                for n in range(6):
                    b = n % 2
                    pool.wait_ge(var_ready, i * 6 + (n + 1))
                    pool.tensor_tensor(rstd[:, b:b + 1], veps[:, b:b + 1], neg_half[:], ALU.pow)\
                        .then_inc(rstd_ready, 1)
                for b in range(2):
                    pool.wait_ge(turn_copied, i * 2 + (b + 3))
                    hold(pool, held)
                    pool.tensor_copy(xfT[:, :, ds(i * (2 * P) + b * P, P)], xft[:, b]).then_inc(xft_kept, 1)

        @block.vector
        def _(dve):
            dve.sem_inc(xo_done, 2)
            dve.sem_inc(x1_done, 2)
            for b in range(2):
                dve.sem_inc(xf_stored[b], 1)
            dve.wait_ge(w_in, 64)
            with dve.Fori(0, NT // 2) as i:
                c = Chain(dve, chain, i * 10)

                def variance(b, src):
                    c.link(dve.bn_stats(stats[:, b], src))
                    hold(dve, held)
                    c.link(dve.bn_aggr(mv[:, b], stats[:, b]))
                    dve.tensor_scalar(veps[:, b:b + 1], mv[:, b, 1:2], LN_EPS, None,
                                      ALU.add).then_inc(var_ready, 1)

                for b in range(2):
                    dve.wait_ge(o_ready, i * 2 + (b + 3))
                    variance(b, ob[:, b])
                for b in range(2):
                    dve.wait_ge(rstd_ready, i * 6 + (b + 1))
                    dve.tensor_scalar(xo[:, b], ob[:, b], mv[:, b, 0:1], rstd[:, b:b + 1],
                                      ALU.subtract, ALU.mult).then_inc(xo_done, 1)
                    dve.wait_ge(xo_done, i * 2 + (b + 3))
                    dve.wait_ge(in_ready[b], i * 32 + 32)
                    dve.wait_ge(x1_kept, i * 2 + (b + 1))
                    dve.tensor_tensor(x1s[:, b], xo[:, b], xt[:, b], ALU.add).then_inc(x1_done, 1)
                    dve.wait_ge(x1_done, i * 2 + (b + 3))
                    variance(b, x1s[:, b])
                for b in range(2):
                    dve.wait_ge(rstd_ready, i * 6 + (b + 3))
                    dve.wait_ge(h_kept, i * 2 + (b + 1))
                    dve.tensor_scalar(h[:, b], x1s[:, b], mv[:, b, 0:1], rstd[:, b:b + 1],
                                      ALU.subtract, ALU.mult).then_inc(h_done, 1)
                    dve.wait_ge(h_done, i * 2 + (b + 1))
                    c.link(dve.tensor_tensor_reduce(sq[:, b], h[:, b], h[:, b], 1.0 / C, 0.0, ALU.mult, ALU.add,
                                                    mean_sq[:, b:b + 1]))
                    dve.tensor_scalar(veps[:, b:b + 1], mean_sq[:, b:b + 1], RMS_EPS, None,
                                      ALU.add).then_inc(var_ready, 1)
                for b in range(2):
                    dve.wait_ge(rstd_ready, i * 6 + (b + 5))
                    dve.wait_ge(turned, i * 2 + (b + 1))
                    dve.wait_ge(xf_stored[b], i * 16 + 1)
                    dve.scalar_tensor_tensor(out=xf[:, b], in0=h[:, b], scalar=rstd[:, b:b + 1], in1=w_norm[:],
                                             op0=ALU.mult, op1=ALU.mult).then_inc(xf_done, 1)
                c.done(10)


def route(nc, before_dram, logits, best, slots, shared_gate):
    with ExitStack() as ctx:
        m = Mem(nc, ctx)
        probs = m.sb("r_probs", [P, NT, E])
        rowmax, rowsum = m.sb("r_rowmax", [P, NT]), m.sb("r_rowsum", [P, NT])
        gate_e = m.sb("r_gate_e", [P, NT])
        top, top_at = m.sb("r_top", [P, NT, 8]), m.sb("r_top_at", [P, NT, 8], U32)
        expert = m.sb("r_expert", [P, NT, K])
        lane, lane_i = m.sb("r_lane", [P, NT, E]), m.sb("r_lane_i", [P, NT, E], I32)
        spare, spare_i = m.sb("r_spare", [P, 1]), m.sb("r_spare_i", [P, 1], I32)
        chosen = [m.sb(f"r_chosen{k}", [P, NT, E]) for k in range(K)]
        mask, mask_b = m.sb("r_mask", [P, NT, E]), m.sb("r_mask_b", [P, NT, E], BF16)
        before, before_b = m.sb("r_before", [P, P]), m.sb("r_before_b", [P, P], BF16)
        ones_b = m.sb("r_ones", [P, P], BF16)
        tile_sum, prefix = m.sb("r_tile_sum", [P, NT, E]), m.sb("r_prefix", [P, NT + 1, E])
        at = m.sb("r_at", [P, NT, E])
        picked = m.sb("r_picked", [P, NT, E])
        place, fits = m.sb("r_place", [P, NT, K]), m.sb("r_fits", [P, NT, K])
        slot = m.sb("r_slot", [P, NT, K])
        within_ps, sum_ps = m.ps("r_within", [P, NT * E]), m.ps("r_sum", [P, NT * E])
        before_in, lanes_set = m.sem("r_before_in"), m.sem("r_lanes_set")
        shifted, exp_done = m.sem("r_shifted"), m.sem("r_exp_done")
        mask_ready, counted, chain = m.sem("r_mask_ready"), m.sem("r_counted"), m.sem("r_chain")
        block = ctx.enter_context(nc.Block())
        lg = logits[:].rearrange("p (t e) -> p t e", t=NT)

        @block.sync
        def _(sp):
            sp.dma_start(before[:], before_dram).then_inc(before_in, 16)

        @block.gpsimd
        def _(pool):
            pool.iota(lane_i[:], pattern=[[0, NT], [1, E]], base=0, channel_multiplier=0).then_inc(lanes_set, 1)
            pool.wait_ge(lanes_set, 1)
            pool.iota(spare_i[:], pattern=[[0, 1]], base=SLOTS, channel_multiplier=1).then_inc(lanes_set, 1)

        @block.scalar
        def _(act):
            act.wait_ge(shifted, 1)
            act.activation(probs[:], probs[:], ACT.Exp).then_inc(exp_done, 1)
            act.activation(gate_e[:], lg[:, :, E], ACT.Exp, scale=-1.0).then_inc(exp_done, 1)

        @block.tensor
        def _(pe):
            pe.wait_ge(mask_ready, 1)
            flat = mask_b[:].rearrange("p t e -> p (t e)")
            pe.matmul(within_ps[:], before_b[:], flat, start=True, stop=True)
            pe.matmul(sum_ps[:], ones_b[:], flat, start=True, stop=True).then_inc(counted, 1)

        @block.vector
        def _(dve):
            c = Chain(dve, chain)

            def over_experts(a):
                return a[:].rearrange("p (t o) -> p t o", o=1).to_broadcast([P, NT, E])

            c.link(dve.tensor_reduce(rowmax[:], lg[:, :, 0:E], AX.X, ALU.max))
            dve.tensor_tensor(probs[:], lg[:, :, 0:E], over_experts(rowmax), ALU.subtract).then_inc(shifted, 1)
            dve.wait_ge(lanes_set, 2)
            dve.wait_ge(before_in, 16)
            dve.tensor_copy(lane[:], lane_i[:])
            dve.tensor_copy(spare[:], spare_i[:])
            dve.tensor_copy(before_b[:], before[:])
            dve.memset(ones_b[:], 1.0)
            dve.wait_ge(exp_done, 2)
            c.link(dve.tensor_reduce(rowsum[:], probs[:], AX.X, ALU.add))
            c.link(dve.reciprocal(rowsum[:], rowsum[:]))
            c.link(dve.tensor_tensor(probs[:], probs[:], over_experts(rowsum), ALU.mult))
            c.link(dve.tensor_scalar(gate_e[:], gate_e[:], 1.0, None, ALU.add))
            dve.reciprocal(shared_gate[:], gate_e[:])
            for t in range(NT):
                last = dve.max(top[:, t], probs[:, t])
            c.link(last)
            for t in range(NT):
                last = dve.max_index(top_at[:, t], top[:, t], probs[:, t])
            c.link(last)
            c.link(dve.tensor_copy(expert[:], top_at[:, :, 0:K]))
            for k in range(K):
                last = dve.tensor_tensor(chosen[k][:], lane[:],
                                         expert[:, :, k:k + 1].to_broadcast([P, NT, E]), ALU.is_equal)
            c.link(last)
            c.link(dve.tensor_tensor(mask[:], chosen[0][:], chosen[1][:], ALU.add))
            c.link(dve.tensor_tensor(mask[:], mask[:], chosen[2][:], ALU.add))
            dve.tensor_tensor(mask_b[:], mask[:], chosen[3][:], ALU.add).then_inc(mask_ready, 1)
            c.link(dve.memset(prefix[:, 0], 0.0))
            dve.wait_ge(counted, 1)
            c.link(dve.tensor_copy(tile_sum[:], sum_ps[:].rearrange("p (t e) -> p t e", t=NT)))
            for t in range(NT):
                c.link(dve.tensor_tensor(prefix[:, t + 1], prefix[:, t], tile_sum[:, t], ALU.add))
            c.link(dve.tensor_tensor(at[:], within_ps[:].rearrange("p (t e) -> p t e", t=NT),
                                     prefix[:, 0:NT], ALU.add))
            for k in range(K):
                c.link(dve.tensor_tensor(picked[:], chosen[k][:], at[:], ALU.mult))
                c.link(dve.tensor_reduce(place[:, :, k], picked[:], AX.X, ALU.add))
            c.link(dve.tensor_scalar(fits[:], place[:], float(CAP), None, ALU.is_lt))
            c.link(dve.scalar_tensor_tensor(out=slot[:], in0=expert[:], scalar=float(CAP), in1=place[:],
                                            op0=ALU.mult, op1=ALU.add))
            c.link(dve.scalar_tensor_tensor(out=slot[:], in0=slot[:], scalar=spare[:, 0:1], in1=fits[:],
                                            op0=ALU.subtract, op1=ALU.mult))
            dve.tensor_scalar(slots[:], slot[:].rearrange("p t k -> p (t k)"), spare[:, 0:1], None, ALU.add)
            dve.tensor_tensor(best[:].rearrange("p (t k) -> p t k", k=K), top[:, :, 0:K], fits[:], ALU.mult)


def shared_expert(nc, sw_gate, sw_up, sw_down, ids_dram, y_dram, xfT, slots, shared_gate, acc):
    with ExitStack() as ctx:
        m = Mem(nc, ctx)
        wg, wu = m.sb("s_wg", [P, KC, FS]), m.sb("s_wu", [P, KC, FS])
        wd = m.sb("s_wd", [P, NFS, C])
        hid = m.sb("s_hid", [P, NFS, QC])
        silu = m.sb("s_silu", [P, 2, QC])
        zero_ids, zero_row = m.sb("s_zero_ids", [P, SLOTS // P + 1], I32), m.sb("s_zero_row", [P, C])
        slot4 = m.sb("s_slot4", [P, 2 * K], I32)
        token, step = m.sb("s_token", [P, 2], I32), m.sb("s_step", [P, 2], I32)
        gp, up, dp = m.ps("s_g", [P, 2, QC]), m.ps("s_u", [P, 2, QC]), m.ps("s_d", [P, 2, C])
        w_in, wd_in = m.sem("s_w_in"), m.sem("s_wd_in")
        gu_ready = m.sem("s_gu_ready")
        silu_done, hid_done = m.sem("s_silu_done"), m.sem("s_hid_done")
        down_ready = m.sem("s_down_ready")
        down_used = m.sem("s_down_used")
        zeros_set, zeros_in = m.sem("s_zeros_set"), m.sem("s_zeros_in")
        token_set, slot4_set = m.sem("s_token_set"), m.sem("s_slot4_set")
        ids_in, held = m.sem("s_ids_in"), m.sem("s_held")
        block = ctx.enter_context(nc.Block())

        @block.sync
        def _(sp):
            sp.dma_start(wg[:], sw_gate.rearrange("(k p) f -> p k f", p=P)).then_inc(w_in, 16)
            sp.dma_start(wu[:], sw_up.rearrange("(k p) f -> p k f", p=P)).then_inc(w_in, 16)
            sp.dma_start(wd[:], sw_down.rearrange("(f p) n -> p f n", p=P)).then_inc(wd_in, 16)
            sp.wait_ge(zeros_set, 2)
            sp.dma_start(ids_dram.rearrange("(p n) o -> p (n o)", p=P), zero_ids[:]).then_inc(zeros_in, 16)
            sp.dma_start(y_dram[SLOTS:SLOTS + P, :], zero_row[:]).then_inc(zeros_in, 16)
            sp.wait_ge(zeros_in, 32)

        @block.gpsimd
        def _(pool):
            pool.iota(token[:], pattern=[[P, 2]], base=0, channel_multiplier=1).then_inc(token_set, 1)
            pool.wait_ge(token_set, 1)
            pool.iota(step[:], pattern=[[0, 2]], base=2 * P, channel_multiplier=0).then_inc(token_set, 1)
            pool.wait_ge(token_set, 2)
            pool.wait_ge(zeros_in, 32)
            with pool.Fori(0, NT // 2) as i:
                pool.tensor_copy(slot4[:], slots[:, ds(i * (2 * K), 2 * K)]).then_inc(slot4_set, 1)
                pool.wait_ge(slot4_set, i + 1)
                hold(pool, held)
                for b in range(2):
                    for k in range(K):
                        n = b * K + k
                        pool.indirect_dma_start(
                            ids_dram, bass.IndirectOffsetOnAxis(ap=slot4[:, n:n + 1].bitcast(U32), axis=0),
                            token[:, b:b + 1], None).then_inc(ids_in, 16)
                        pool.wait_ge(ids_in, i * (2 * K * 16) + 16 * (n + 1))
                        hold(pool, held)
                pool.tensor_tensor(token[:], token[:], step[:], ALU.add).then_inc(token_set, 1)
                pool.wait_ge(token_set, i + 3)

        @block.tensor
        def _(pe):
            pe.wait_ge(w_in, 32)
            with pe.Fori(0, NQ) as i:
                for f in range(NFS):
                    pe.wait_ge(hid_done, i * NFS + (f + 1))
                    for w, bank in ((wg, gp), (wu, up)):
                        for k in range(KC):
                            last = pe.matmul(bank[:, f % 2], w[:, k, f * P:(f + 1) * P],
                                             xfT[:, k, ds(i * QC, QC)], start=(k == 0), stop=(k == KC - 1))
                    last.then_inc(gu_ready, 1)
                if NFS % 2:
                    pe.wait_ge(hid_done, i * NFS + (NFS + 2))
                pe.wait_ge(wd_in, 16)
                for t in range(QT):
                    pe.wait_ge(down_used, i * QT + (t + 1))
                    for f in range(NFS):
                        last = pe.matmul(dp[:, t % 2], hid[:, f, t * P:(t + 1) * P], wd[:, f],
                                         start=(f == 0), stop=(f == NFS - 1))
                    last.then_inc(down_ready, 1)

        @block.scalar
        def _(act):
            with act.Fori(0, NQ) as i:
                for f in range(NFS):
                    act.wait_ge(gu_ready, i * NFS + (f + 1))
                    act.wait_ge(hid_done, i * NFS + (f + 1))
                    act.activation(silu[:, f % 2], gp[:, f % 2], ACT.Silu).then_inc(silu_done, 1)

        @block.vector
        def _(dve):
            dve.memset(zero_ids[:], 0).then_inc(zeros_set, 1)
            dve.memset(zero_row[:], 0.0).then_inc(zeros_set, 1)
            dve.sem_inc(hid_done, 2)
            dve.sem_inc(down_used, 2)
            dve.sem_inc(down_ready, 1)
            with dve.Fori(0, NQ) as i:
                for f in range(NFS):
                    dve.wait_ge(silu_done, i * NFS + (f + 1))
                    dve.wait_ge(down_ready, i * QT + 1)
                    dve.tensor_tensor(hid[:, f], up[:, f % 2], silu[:, f % 2], ALU.mult).then_inc(hid_done, 1)
                for t in range(QT):
                    dve.wait_ge(down_ready, i * QT + (t + 2))
                    acc_t = acc[:, ds(i * (QT * C) + t * C, C)]
                    dve.scalar_tensor_tensor(out=acc_t, in0=dp[:, t % 2], scalar=shared_gate[:, ds(i * QT + t, 1)],
                                             in1=acc_t, op0=ALU.mult, op1=ALU.add).then_inc(down_used, 1)


def experts(nc, w_gate, w_up, w_down, tokens_dram, ids_dram, y_dram, ident):
    ST = CAP // P
    NF = len(FT)
    with ExitStack() as ctx:
        m = Mem(nc, ctx)
        wg, wu = ([m.sb(f"e_{n}{b}", [P, KC, F]) for b in range(2)] for n in ("wg", "wu"))
        wd = [m.sb(f"e_wd{b}", [P, NF, C]) for b in range(2)]
        ids = [m.sb(f"e_ids{b}", [P, ST], I32) for b in range(2)]
        ids_now = [m.sb(f"e_ids_now{b}", [P, ST], I32) for b in range(2)]
        xg = [m.sb(f"e_xg{b}", [P, ST, C]) for b in range(2)]
        xgT = [m.sb(f"e_xgT{b}", [P, KC, CAP]) for b in range(2)]
        silu, hid = m.sb("e_silu", [P, 2, CAP]), [m.sb(f"e_hid{b}", [P, NF, CAP]) for b in range(2)]
        y = [m.sb(f"e_y{b}", [P, ST, C]) for b in range(2)]
        tp = m.ps("e_tp", [P, 2, KC, P])
        gu = m.ps("e_gu", [P, 2, 2, CAP])
        dp = m.ps("e_d", [P, 2, C])
        w_in = [m.sem(f"e_w_in{b}") for b in range(2)]
        ids_in = [m.sem(f"e_ids_in{b}") for b in range(2)]
        ids_copied, held = m.sem("e_ids_copied"), m.sem("e_held")
        xg_in = [m.sem(f"e_xg_in{b}") for b in range(2)]
        turned = m.sem("e_turned")
        turn_copied = m.sem("e_turn_copied")
        gu_ready = m.sem("e_gu_ready")
        silu_done = m.sem("e_silu_done")
        hid_done = m.sem("e_hid_done")
        down_ready = m.sem("e_down_ready")
        y_copied = m.sem("e_y_copied")
        y_stored = [m.sem(f"e_y_stored{b}") for b in range(2)]
        block = ctx.enter_context(nc.Block())
        ids_of = ids_dram.rearrange("(t p) o -> p (t o)", p=P)

        @block.sync
        def _(sp):
            with sp.Fori(0, E // 2) as i:
                ex = [sp.snap(i * 2 + b) for b in range(2)]
                row = [sp.snap(i * (2 * C) + b * C) for b in range(2)]
                frow = [sp.snap(i * (2 * F) + b * F) for b in range(2)]
                frow_rest = [sp.snap(i * (2 * F) + (b * F + FT[2][0])) for b in range(2)]
                col = [sp.snap(i * (2 * ST) + b * ST) for b in range(2)]
                for b in range(2):
                    sp.wait_ge(down_ready, i * (2 * ST) + ST * (b + 1))
                    sp.dma_start(ids[b][:], ids_of[:, ds(col[b], ST)], allow_slow_non_contiguous=True)\
                        .then_inc(ids_in[b], 16)
                    for w, w_dram in ((wg, w_gate), (wu, w_up)):
                        sp.dma_start(w[b][:], w_dram[ds(row[b], C), :].rearrange("(k p) f -> p k f", p=P))\
                            .then_inc(w_in[b], 16)
                    sp.dma_start(wd[b][:, 0:2], w_down[ds(frow[b], 2 * P), :].rearrange("(f p) n -> p f n", p=P))\
                        .then_inc(w_in[b], 16)
                    sp.dma_start(wd[b][0:FT[2][1], 2], w_down[ds(frow_rest[b], FT[2][1]), :])\
                        .then_inc(w_in[b], 16)

        @block.gpsimd
        def _(pool):
            with pool.Fori(0, E // 2) as i:
                for b in range(2):
                    pool.wait_ge(ids_in[b], i * 16 + 16)
                    pool.wait_ge(turned, i * (2 * ST) + ST * (b + 1))
                    hold(pool, held)
                    pool.tensor_copy(ids_now[b][:], ids[b][:]).then_inc(ids_copied, 1)
                    pool.wait_ge(ids_copied, i * 2 + (b + 1))
                    hold(pool, held)
                    for t in range(ST):
                        pool.indirect_dma_start(
                            xg[b][:, t], None, tokens_dram,
                            bass.IndirectOffsetOnAxis(ap=ids_now[b][:, t:t + 1].bitcast(U32), axis=0))\
                            .then_inc(xg_in[b], 16)

        @block.tensor
        def _(pe):
            pe.sem_inc(turned, 2 * ST)
            pe.sem_inc(down_ready, 2 * ST)
            with pe.Fori(0, E // 2) as i:
                for b in range(2):
                    pe.wait_ge(xg_in[b], i * (16 * ST) + 16 * ST)
                    for t in range(ST):
                        pe.wait_ge(turn_copied, i * (2 * ST) + (b * ST + t + 1))
                        for k in range(KC):
                            last = pe.transpose(tp[:, t % 2, k], xg[b][:, t, k * P:(k + 1) * P], ident[:])
                        last.then_inc(turned, 1)
                    pe.wait_ge(turn_copied, i * (2 * ST) + (b * ST + ST + 2))
                    pe.wait_ge(w_in[b], i * 64 + 64)
                    for n, (f0, w) in enumerate(FT):
                        use = b * NF + n
                        pe.wait_ge(hid_done, i * (2 * NF) + (use + 1))
                        for s, weights in enumerate((wg, wu)):
                            for k in range(KC):
                                last = pe.matmul(gu[0:w, use % 2, s], weights[b][:, k, f0:f0 + w], xgT[b][:, k],
                                                 start=(k == 0), stop=(k == KC - 1))
                        last.then_inc(gu_ready, 1)
                    pe.wait_ge(hid_done, i * (2 * NF) + (b * NF + NF + 2))
                    for t in range(ST):
                        pe.wait_ge(y_copied, i * (2 * ST) + (b * ST + t + 1))
                        for n, (f0, w) in enumerate(FT):
                            last = pe.matmul(dp[:, t % 2], hid[b][0:w, n, t * P:(t + 1) * P], wd[b][0:w, n],
                                             start=(n == 0), stop=(n == NF - 1))
                        last.then_inc(down_ready, 1)

        @block.scalar
        def _(act):
            act.sem_inc(y_copied, 2)
            for b in range(2):
                act.sem_inc(y_stored[b], 1)
            with act.Fori(0, E // 2) as i:
                y_row = [act.snap(i * (2 * CAP) + b * CAP) for b in range(2)]
                for b in range(2):
                    for n, (f0, w) in enumerate(FT):
                        use = b * NF + n
                        act.wait_ge(gu_ready, i * (2 * NF) + (use + 1))
                        act.wait_ge(hid_done, i * (2 * NF) + (use + 1))
                        act.activation(silu[0:w, use % 2], gu[0:w, use % 2, 0], ACT.Silu).then_inc(silu_done, 1)
                    for t in range(ST):
                        act.wait_ge(down_ready, i * (2 * ST) + (2 * ST + b * ST + t + 1))
                        act.wait_ge(y_stored[b], i * 16 + 1)
                        act.copy(y[b][:, t], dp[:, t % 2]).then_inc(y_copied, 1)
                    act.wait_ge(y_copied, i * (2 * ST) + (b * ST + ST + 2))
                    act.dma_start(y_dram[ds(y_row[b], CAP), :].rearrange("(t p) c -> p t c", p=P), y[b][:])\
                        .then_inc(y_stored[b], 16)
            for b in range(2):
                act.wait_ge(y_stored[b], 16 * E // 2 + 1)

        @block.vector
        def _(dve):
            dve.sem_inc(turn_copied, 2)
            dve.sem_inc(hid_done, 2)
            with dve.Fori(0, E // 2) as i:
                for b in range(2):
                    for t in range(ST):
                        dve.wait_ge(turned, i * (2 * ST) + (2 * ST + b * ST + t + 1))
                        dve.tensor_copy(xgT[b][:, :, t * P:(t + 1) * P], tp[:, t % 2]).then_inc(turn_copied, 1)
                    for n, (f0, w) in enumerate(FT):
                        use = b * NF + n
                        dve.wait_ge(silu_done, i * (2 * NF) + (use + 1))
                        dve.tensor_tensor(hid[b][0:w, n], gu[0:w, use % 2, 1], silu[0:w, use % 2],
                                          ALU.mult).then_inc(hid_done, 1)


def combine(nc, y_dram, out_dram, x1, acc, best, slots, neg_half):
    with ExitStack() as ctx:
        m = Mem(nc, ctx)
        slot4 = [m.sb(f"f_slot4{b}", [P, K], I32) for b in range(2)]
        yk = [m.sb(f"f_y{b}", [P, K, C]) for b in range(2)]
        total = m.sb("f_total", [P, 2, C])
        o = m.sb("f_out", [P, 2, C])
        stats, mv = m.sb("f_stats", [P, 2, 6]), m.sb("f_mv", [P, 2, 2])
        veps, rstd = m.sb("f_veps", [P, 2]), m.sb("f_rstd", [P, 2])
        held = m.sem("f_held")
        slot4_set = m.sem("f_slot4_set")
        y_in = [m.sem(f"f_y_in{b}") for b in range(2)]
        y_used = m.sem("f_y_used")
        var_ready, rstd_ready = m.sem("f_var_ready"), m.sem("f_rstd_ready")
        out_ready = m.sem("f_out_ready")
        out_stored = [m.sem(f"f_out_stored{b}") for b in range(2)]
        chain = m.sem("f_chain")
        block = ctx.enter_context(nc.Block())

        @block.gpsimd
        def _(pool):
            def gather(first, b, n):
                pool.wait_ge(slot4_set, n)
                hold(pool, held)
                for k in range(K):
                    pool.indirect_dma_start(
                        yk[b][:, k], None, y_dram,
                        bass.IndirectOffsetOnAxis(ap=slot4[b][:, k:k + 1].bitcast(U32), axis=0))\
                        .then_inc(y_in[b], 16)

            with pool.Fori(0, NT // 2) as i:
                for b in range(2):
                    pool.wait_ge(y_used, i * 2 + (b + 1))
                    hold(pool, held)
                    pool.tensor_copy(slot4[b][:], slots[:, ds(i * (2 * K) + b * K, K)]).then_inc(slot4_set, 1)
                    gather(i, b, i * 2 + (b + 1))
                for b in range(2):
                    pool.wait_ge(var_ready, i * 2 + (b + 1))
                    pool.tensor_tensor(rstd[:, b:b + 1], veps[:, b:b + 1], neg_half[:], ALU.pow)\
                        .then_inc(rstd_ready, 1)

        @block.vector
        def _(dve):
            dve.sem_inc(y_used, 2)
            for b in range(2):
                dve.sem_inc(out_stored[b], 1)
            with dve.Fori(0, NT // 2) as i:
                c = Chain(dve, chain, i * (2 * K + 6))
                for b in range(2):
                    dve.wait_ge(y_in[b], i * (16 * K) + 16 * K)
                    for k in range(K):
                        so_far = acc[:, ds(i * (2 * C) + b * C, C)] if k == 0 else total[:, b]
                        c.link(dve.scalar_tensor_tensor(
                            out=total[:, b], in0=yk[b][:, k], scalar=best[:, ds(i * (2 * K) + (b * K + k), 1)],
                            in1=so_far, op0=ALU.mult, op1=ALU.add))
                    dve.sem_inc(y_used, 1)
                    c.link(dve.bn_stats(stats[:, b], total[:, b]))
                    hold(dve, held)
                    c.link(dve.bn_aggr(mv[:, b], stats[:, b]))
                    dve.tensor_scalar(veps[:, b:b + 1], mv[:, b, 1:2], LN_EPS, None,
                                      ALU.add).then_inc(var_ready, 1)
                for b in range(2):
                    dve.wait_ge(rstd_ready, i * 2 + (b + 1))
                    dve.wait_ge(out_stored[b], i * 16 + 1)
                    c.link(dve.tensor_scalar(total[:, b], total[:, b], mv[:, b, 0:1], rstd[:, b:b + 1],
                                             ALU.subtract, ALU.mult))
                    dve.tensor_tensor(o[:, b], total[:, b], x1[:, ds(i * (2 * C) + b * C, C)],
                                      ALU.add).then_inc(out_ready, 1)
                c.done(2 * K + 6)

        @block.sync
        def _(sp):
            with sp.Fori(0, NT // 2) as i:
                row = [sp.snap(i * (2 * P) + b * P) for b in range(2)]
                for b in range(2):
                    sp.wait_ge(out_ready, i * 2 + (b + 1))
                    sp.dma_start(out_dram[ds(row[b], P), :], o[:, b]).then_inc(out_stored[b], 16)
            for b in range(2):
                sp.wait_ge(out_stored[b], 16 * NT // 2 + 1)


def sandwich(nc, a, out):
    x_rows = a["x"]
    ctx_dram = nc.dram_tensor("ctx_scratch", [C, T], F32).ap()
    tokens_dram = nc.dram_tensor("tokens_scratch", [T, C], F32).ap()
    ids_dram = nc.dram_tensor("ids_scratch", [SLOTS + P, 1], I32).ap()
    y_dram = nc.dram_tensor("y_scratch", [SLOTS + P, C], F32).ap()
    with ExitStack() as ctx:
        m = Mem(nc, ctx)
        ident, neg_half = m.sb("ident", [P, P]), m.sb("neg_half", [P, 1])
        with ExitStack() as part:
            xnT = Mem(nc, part).sb("xnT", [P, KC, T])
            norm_and_transpose(nc, x_rows, a["identity"], ident, neg_half, xnT)
            attention(nc, a["wq_t"], a["wk_t"], a["wv_t"], a["rope_cos"], a["rope_sin"], a["rope_rotate"],
                      ctx_dram, ident, xnT)
        x1, acc = m.sb("x1", [P, NT * C]), m.sb("acc", [P, NT * C])
        best, slots = m.sb("best", [P, NT * K]), m.sb("slots", [P, NT * K], I32)
        shared_gate = m.sb("shared_gate", [P, NT])
        with ExitStack() as part:
            xfT = Mem(nc, part).sb("xfT", [P, KC, T])
            logits = Mem(nc, part).sb("logits", [P, NT * (E + 1)])
            layer_norms(nc, x_rows, ctx_dram, a["wo_t"], a["w_norm"], a["w_router"], a["w_shared_gate"],
                        tokens_dram, ident, neg_half, x1, acc, xfT, logits)
            route(nc, a["before"], logits, best, slots, shared_gate)
            shared_expert(nc, a["sw_gate"], a["sw_up"], a["sw_down"], ids_dram, y_dram, xfT, slots,
                          shared_gate, acc)
        experts(nc, a["w_gate"], a["w_up"], a["w_down"], tokens_dram, ids_dram, y_dram, ident)
        combine(nc, y_dram, out, x1, acc, best, slots, neg_half)


def shape_constants():
    import numpy as np

    f32 = np.float32
    inv_freq = (f32(1.0) / f32(10000.0) ** (np.arange(0, D, 2, dtype=f32) / f32(D))).astype(f32)
    freqs = np.outer(np.arange(T, dtype=f32), inv_freq).astype(f32)
    angles = np.concatenate([freqs, freqs], axis=-1).T
    rotate = np.zeros((P, P), f32)
    for j in range(HG):
        for d in range(D // 2):
            rotate[j * D + d + D // 2, j * D + d] = -1.0
            rotate[j * D + d, j * D + d + D // 2] = 1.0
    return {
        "identity": np.eye(P, dtype=f32),
        "rope_cos": np.ascontiguousarray(np.tile(np.cos(angles), (HG, 1))),
        "rope_sin": np.ascontiguousarray(np.tile(np.sin(angles), (HG, 1))),
        "rope_rotate": rotate,
        "before": np.triu(np.ones((P, P), f32), 1),
    }


def kernel(**inputs):
    import numpy as np
    import concourse.bacc as bacc
    from concourse.bass_utils import run_bass_kernel_spmd

    def plain(name):
        return np.ascontiguousarray(inputs[name])

    def turned(name):
        return np.ascontiguousarray(np.asarray(inputs[name]).T)

    arrays = {
        "x": plain("L0_attn_x").reshape(T, C),
        "wq_t": turned("L0_attn_w_q"), "wk_t": turned("L0_attn_w_k"),
        "wv_t": turned("L0_attn_w_v"), "wo_t": turned("L0_attn_w_o"),
        "w_norm": plain("L0_ffn_w_norm").reshape(1, C),
        "w_router": plain("L0_ffn_w_router"),
        "w_shared_gate": plain("L0_ffn_w_shared_gate"),
        "w_gate": plain("L0_ffn_w_gate").reshape(E * C, F),
        "w_up": plain("L0_ffn_w_up").reshape(E * C, F),
        "w_down": plain("L0_ffn_w_down").reshape(E * F, C),
        "sw_gate": plain("L0_ffn_sw_gate"), "sw_up": plain("L0_ffn_sw_up"), "sw_down": plain("L0_ffn_sw_down"),
        **shape_constants(),
    }
    nc = bacc.Bacc("TRN2", target_bir_lowering=False, num_devices=1)
    handles = {n: nc.dram_tensor(f"in_{n}", v.shape, mybir.dt.from_np(v.dtype), kind="ExternalInput").ap()
               for n, v in arrays.items()}
    out = nc.dram_tensor("out", (T, C), F32, kind="ExternalOutput").ap()
    sandwich(nc, handles, out)
    r = run_bass_kernel_spmd(nc, [{f"in_{n}": v for n, v in arrays.items()}], core_ids=[0])
    return r.results[0]["out"].reshape(1, T, C)
```

```python
from contextlib import ExitStack

import concourse.bass as bass
from concourse import mybir

P = 128
F32 = mybir.dt.float32
F32R = mybir.dt.float32r
BF16 = mybir.dt.bfloat16
I32 = mybir.dt.int32
U32 = mybir.dt.uint32
ALU = mybir.AluOpType
ACT = mybir.ActivationFunctionType
AX = mybir.AxisListType
ds = bass.ds

T, C = 2048, 512
NT, KC = T // P, C // P
H, D = 16, 32
HG = P // D
NG = H // HG
QC = 512
NQ = T // QC
QT = QC // P
HALF = 64
BIG = -1.0e30
LN_EPS, RMS_EPS = 1e-5, 1e-6
E, K, F, CAP = 32, 4, 352, 256
FS = 1408
NFS = FS // P
FT = [(0, 128), (128, 128), (256, 96)]
SLOTS = E * CAP
ST = CAP // P
PRODUCTS = ((0, 0), (0, 1), (1, 0))


class Chain:

    def __init__(self, eng, sem, base=0):
        self.eng, self.sem, self.base, self.n = eng, sem, base, 0

    def link(self, ins):
        ins.then_inc(self.sem, 1)
        self.n += 1
        self.eng.wait_ge(self.sem, self.base + self.n)

    def done(self, per):
        assert self.n == per, (self.n, per)


def hold(eng, held):
    eng.sem_inc(held, 1)


class Mem:

    def __init__(self, nc, ctx):
        self.nc, self.ctx = nc, ctx

    def sb(self, name, shape, dt=F32):
        return self.ctx.enter_context(self.nc.sbuf_tensor(name, shape, dt))

    def ps(self, name, shape, dt=F32):
        return self.ctx.enter_context(self.nc.psum_tensor(name, shape, dt))

    def sem(self, name):
        return self.ctx.enter_context(self.nc.semaphore(name))


def norm_and_transpose(nc, x_dram, identity_dram, ident, neg_half, xnT):
    with ExitStack() as ctx:
        m = Mem(nc, ctx)
        xt = m.sb("a_x", [P, 2, C])
        xn = m.sb("a_xn", [P, 2, C])
        stats = m.sb("a_stats", [P, 2, 6])
        mv = m.sb("a_mean_var", [P, 2, 2])
        veps = m.sb("a_var_eps", [P, 2])
        rstd = m.sb("a_rstd", [P, 2])
        held = m.sem("a_held")
        tp = m.ps("a_tp", [P, 2, KC, P])
        ident_ready, consts_ready = m.sem("a_ident_ready"), m.sem("a_consts_ready")
        x_ready = [m.sem(f"a_x_ready{b}") for b in range(2)]
        xn_done = m.sem("a_xn_done")
        var_ready, rstd_ready = m.sem("a_var_ready"), m.sem("a_rstd_ready")
        tp_ready = m.sem("a_tp_ready")
        tp_copied = m.sem("a_tp_copied")
        chain = m.sem("a_dve_chain")
        block = ctx.enter_context(nc.Block())

        @block.sync
        def _(sp):
            sp.dma_start(ident[:], identity_dram).then_inc(ident_ready, 16)
            with sp.Fori(0, NT // 2) as i:
                row = [sp.snap(i * (2 * P) + b * P) for b in range(2)]
                for b in range(2):
                    sp.wait_ge(xn_done, i * 2 + (b + 1))
                    sp.dma_start(xt[:, b], x_dram[ds(row[b], P), :]).then_inc(x_ready[b], 16)

        @block.vector
        def _(dve):
            dve.sem_inc(xn_done, 2)
            dve.memset(neg_half[:], -0.5).then_inc(consts_ready, 1)
            with dve.Fori(0, NT // 2) as i:
                c = Chain(dve, chain, i * 4)
                for b in range(2):
                    dve.wait_ge(x_ready[b], i * 16 + 16)
                    c.link(dve.bn_stats(stats[:, b], xt[:, b]))
                    hold(dve, held)
                    c.link(dve.bn_aggr(mv[:, b], stats[:, b]))
                    dve.tensor_scalar(veps[:, b:b + 1], mv[:, b, 1:2], LN_EPS, None,
                                      ALU.add).then_inc(var_ready, 1)
                for b in range(2):
                    dve.wait_ge(rstd_ready, i * 2 + (b + 1))
                    dve.wait_ge(tp_ready, i * 2 + (b + 1))
                    dve.tensor_scalar(xn[:, b], xt[:, b], mv[:, b, 0:1], rstd[:, b:b + 1],
                                      ALU.subtract, ALU.mult).then_inc(xn_done, 1)
                c.done(4)

        @block.gpsimd
        def _(pool):
            pool.wait_ge(consts_ready, 1)
            with pool.Fori(0, NT // 2) as i:
                for b in range(2):
                    pool.wait_ge(var_ready, i * 2 + (b + 1))
                    pool.tensor_tensor(rstd[:, b:b + 1], veps[:, b:b + 1], neg_half[:],
                                       ALU.pow).then_inc(rstd_ready, 1)

        @block.tensor
        def _(pe):
            pe.sem_inc(tp_ready, 2)
            pe.wait_ge(ident_ready, 16)
            with pe.Fori(0, NT // 2) as i:
                for b in range(2):
                    pe.wait_ge(xn_done, i * 2 + (b + 3))
                    pe.wait_ge(tp_copied, i * 2 + (b + 1))
                    for k in range(KC):
                        last = pe.transpose(tp[:, b, k], xn[:, b, k * P:(k + 1) * P], ident[:])
                    last.then_inc(tp_ready, 1)

        @block.scalar
        def _(act):
            act.sem_inc(tp_copied, 2)
            with act.Fori(0, NT // 2) as i:
                for b in range(2):
                    act.wait_ge(tp_ready, i * 2 + (b + 3))
                    act.copy(xnT[:, :, ds(i * (2 * P) + b * P, P)], tp[:, b]).then_inc(tp_copied, 1)


def interleave(pieces, steps, units, ahead, last_added, parts):
    MATMUL, FULL_PRECISION, VECTOR = 0.215 / QC, 0.86 / QC, 0.61 / QC
    TURN, ROWS = 0.3, 5.0
    order, free = [], [0.0, 0.0]
    pe = dve = 0.0
    use = 0
    maxima = [("unit", qc, n) for qc in range(1, NQ) for n in range(ahead if qc == 1 else 0, len(units[qc]))]
    turns, rows_ready = [], {}

    def unit():
        nonlocal pe, dve, use
        kind, qc, n = maxima.pop(0)
        order.append((kind, qc, n))
        w = units[qc][n][3]
        pe = max(pe, free[use % 2]) + MATMUL * w + 0.08
        dve = max(dve, pe + 0.1) + VECTOR * w
        free[use % 2] = dve + 0.1
        use += 1
        if not maxima or maxima[0][1] != qc:
            order.append(("negmax", qc))
            dve += 0.8
            turns.append((dve + 0.2, qc))

    def turn():
        nonlocal pe, dve, use
        start, qc = turns.pop(0)
        order.append(("turn", qc))
        pe = max(pe, start, free[use % 2]) + TURN
        dve = max(dve, pe) + 0.8
        free[use % 2] = dve
        rows_ready[qc] = dve + ROWS
        use += 1

    def turn_or_unit(by):
        if turns and turns[0][0] <= by:
            turn()
        elif maxima and free[use % 2] <= by:
            unit()
        else:
            return False
        return True

    for piece in pieces:
        what, qc, *at = piece
        if what == "scores" and at == [0, 0] and qc:
            while qc not in rows_ready:
                if not turn_or_unit(pe):
                    pe += 0.05
            while pe < rows_ready[qc] and maxima:
                if not turn_or_unit(pe):
                    pe += 0.05
        while turn_or_unit(pe + 0):
            pass
        order.append(piece)
        if what == "normalise":
            dve = max(dve, pe) + 2.4
        else:
            w = QC - steps[qc][at[0]][1]
            pe += MATMUL * w + 0.03 if what == "scores" else FULL_PRECISION * w / parts[qc][at[0]] + 0.12
            if what == "values" and qc == NQ - 1 and at[0] in last_added[1:] and at[1] == 0:
                dve += 2 * VECTOR * w
    assert not maxima and not turns
    return order


def attention(nc, wq_t, wk_t, wv_t, cos_dram, sin_dram, rotate_dram, ctx_dram, ident, xnT):
    scale = float(D) ** -0.5
    steps = [[(kt, max(0, kt - QT * qc) * P) for kt in range(QT * (qc + 1))] for qc in range(NQ)]
    n_steps = sum(map(len, steps))
    first_step = [sum(map(len, steps[:qc])) for qc in range(NQ)]
    units = [[(qt, kc, j, min(QC, (qt + 1) * P - kc * QC))
              for qt in range(QT * qc, QT * (qc + 1)) for kc in range(qc + 1) for j in range(HG)]
             for qc in range(NQ)]
    n_mx = sum(map(len, units)) + NQ
    n_rope = 2 * NQ
    rope_units = [(s, 2 * half + n) for half in range(2) for s in range(2) for n in range(2)]
    added_steps = [[] for _ in range(NQ - 2)]
    added_steps.append([i for i in range(len(steps[-2])) if i % 2])
    added_steps.append([i for i in range(len(steps[-1])) if i % 3])
    both = (slice(0, 2), slice(2, HG))
    add_heads = [(slice(0, HG), None)] * (NQ - 1) + [both]
    n_adds = [[len(added_steps[qc]) - 1 if added_steps[qc] and add_heads[qc][by] else 0 for qc in range(NQ)]
              for by in range(2)]
    n_sums = sum(1 for added in added_steps if added)
    V_AHEAD = 2 * (NT - QT - len(units[0]) // 2)
    parts = [[2 if 0 < i < len(steps[qc]) - 2 else 1 for i in range(len(steps[qc]))] for qc in range(NQ)]
    pieces = []

    def products(qc, i):
        kinds = ("values",) if i in added_steps[qc] else ("values", "sums")
        return [(kind, qc, i, part) for kind in kinds for part in range(parts[qc][i])]

    for qc in range(NQ):
        for i in range(len(steps[qc])):
            pieces += [("scores", qc, i, j) for j in range(HG)]
            if i == 1 and qc:
                pieces.insert(-2, ("normalise", qc - 1))
            if i or qc:
                pieces += products(*((qc, i - 1) if i else (qc - 1, len(steps[qc - 1]) - 1)))
    pieces += products(NQ - 1, len(steps[-1]) - 1)
    pieces.append(("normalise", NQ - 1))
    order = interleave(pieces, steps, units, V_AHEAD, added_steps[-1], parts)
    HALF_IN = 2 * 3 * HG * 16
    M_ROW = 3 * D

    with ExitStack() as ctx:
        m = Mem(nc, ctx)
        cos, sin = m.sb("rope_cos", [P, T]), m.sb("rope_sin", [P, T])
        rotate = m.sb("rope_rotate", [P, P])
        wq, wk = m.sb("wq_g", [P, KC, P]), m.sb("wk_g", [P, KC, P])
        wv = m.sb("wv_g", [P, KC, P])
        work = m.sb("work", [P, 6, QC])
        raw, by_cos, by_sin, sums = work[:, 0:2], work[:, 2:4], work[:, 4:6], work[:, 0:HG]
        hilo = [m.sb(f"hilo_{s}", [P, 2, T], F32R) for s in "qk"]
        stack = [[m.sb(f"stack_{s}{j}", [P, T], F32R) for j in range(HG)] for s in "qk"]
        v = m.sb("v_g", [P, NT, P])
        probs = [m.sb(f"probs{b}", [P, HG, QC]) for b in range(2)]
        den_turned, rden_one, rden = m.sb("den_turned", [P, QC]), m.sb("rden_one", [P, QC // D]), m.sb("rden", [P, QC])
        ctxs = [m.sb(f"ctx{b}", [P, QC]) for b in range(2)]
        tops = m.sb("tops", [P, NT, HG, NQ])
        negmax = m.sb("negmax", [P, QT, HG])
        negmax_hi = m.sb("negmax_hi", [P, QT, HG], F32R)
        spread = m.sb("negmax_spread", [P, QT, P])
        max_rows = m.sb("max_rows", [P, QC], F32R)
        ones = m.sb("ones_d", [P, D])
        first_half = m.sb("first_half", [P, P], BF16)
        second_half = m.sb("second_half", [P, P], BF16)
        first_big = m.sb("first_big", [P, P], BF16)
        second_big = m.sb("second_big", [P, P], BF16)
        out_banks = [m.ps("pv", [P, QC]), m.ps("den", [P, QC])]
        pv, den = out_banks
        mx = m.ps("mx", [P, 2, QC])
        st = m.ps("st", [P, HG, QC])

        consts_in, w_in, masks_set = m.sem("b_consts_in"), m.sem("b_w_in"), m.sem("b_masks_set")
        zeros_set, held = m.sem("b_zeros_set"), m.sem("b_held")
        qk_projected, v_projected = m.sem("b_qk_projected"), m.sem("b_v_projected")
        raw_copied, v_copied = m.sem("b_raw_copied"), m.sem("b_v_copied")
        rotated, cos_done, split_done = m.sem("b_rotated"), m.sem("b_cos_done"), m.sem("b_split_done")
        added = m.sem("b_added")
        stack_in = [m.sem("b_first_half_in"), m.sem("b_second_half_in")]
        mx_ready, negmax_split = m.sem("b_mx_ready"), m.sem("b_negmax_split")
        mx_free = m.sem("b_mx_free")
        max_rows_set, max_rows_in = m.sem("b_max_rows_set"), m.sem("b_max_rows_in")
        sums_begun, den_done = m.sem("b_sums_begun"), m.sem("b_den_done")
        summed = [m.sem("b_summed_pool"), m.sem("b_summed_dve")]
        st_ready, exp_done, pv_done = m.sem("b_st_ready"), m.sem("b_exp_done"), m.sem("b_pv_done")
        ctx_ready = m.sem("b_ctx_ready")
        ctx_stored = [m.sem(f"b_ctx_stored{b}") for b in range(2)]
        chain = m.sem("b_dve_chain")
        block = ctx.enter_context(nc.Block())

        def adds(g, by, qc, n):
            return g * sum(n_adds[by]) + (sum(n_adds[by][:qc]) + n)

        def sums_of(qc):
            return sum(1 for added in added_steps[:qc] if added)

        def add_to_sums(eng, g, qc, n, by):
            i = added_steps[qc][n + 1]
            q0, s = steps[qc][i][1], first_step[qc] + i
            eng.wait_ge(exp_done, g * (2 * n_steps) + (2 * s + 2))
            if n == 0:
                eng.wait_ge(sums_begun, g * n_sums + (sums_of(qc) + 1))
            else:
                eng.wait_ge(summed[by], adds(g, by, qc, n))
            heads = add_heads[qc][by]
            own = sums[:, heads, q0:QC]
            eng.tensor_tensor(own, own, probs[s % 2][:, heads, q0:QC], ALU.add).then_inc(summed[by], 1)

        @block.sync
        def _(sp):
            sp.dma_start(cos[:], cos_dram).then_inc(consts_in, 16)
            sp.dma_start(sin[:], sin_dram).then_inc(consts_in, 16)
            sp.dma_start(rotate[:], rotate_dram).then_inc(consts_in, 16)

            def load_weights(at):
                for w, w_dram in ((wq, wq_t), (wk, wk_t), (wv, wv_t)):
                    sp.dma_start(w[:], w_dram.rearrange("(k p) n -> p k n", p=P)[:, :, at]).then_inc(w_in, 16)

            load_weights(slice(0, P))
            with sp.Fori(0, NG) as g:
                channel, steps_before = sp.snap(g * P), sp.snap(g * n_steps)
                next_channel = sp.snap((g + 1) % NG * P)
                for half in range(2):
                    for s in range(2):
                        sp.wait_ge(split_done, g * n_rope + 2 * (2 * half + s + 1))
                        if s == 0 and half == 0:
                            hold(sp, held)
                            sp.wait_ge(pv_done, steps_before + 1)
                        cols = slice(half * T // 2, (half + 1) * T // 2)
                        for r, part in enumerate(((0, 0, 1), (0, 1, 0))[s]):
                            for j in range(HG):
                                sp.dma_start(stack[s][j][r * D:(r + 1) * D, cols].bitcast(F32),
                                             hilo[s][j * D:(j + 1) * D, part, cols].bitcast(F32))\
                                    .then_inc(stack_in[half], 16)

                def max_rows_of(qc):
                    sp.wait_ge(max_rows_set, g * NQ + (qc + 1))
                    for j in range(HG):
                        sp.dma_start(stack[0][j][M_ROW:M_ROW + 2, qc * QC:(qc + 1) * QC].bitcast(F32),
                                     max_rows[j * D:j * D + 2, :].bitcast(F32)).then_inc(max_rows_in, 16)

                max_rows_of(0)
                for qc in range(NQ):
                    if qc + 1 < NQ:
                        max_rows_of(qc + 1)
                    if qc == 0:
                        sp.wait_ge(v_projected, g * NQ + (NQ + 1))
                        hold(sp, held)
                        load_weights(ds(next_channel, P))
                    sp.wait_ge(ctx_ready, g * NQ + (qc + 2))
                    sp.dma_start(ctx_dram[ds(channel, P), qc * QC:(qc + 1) * QC],
                                 ctxs[qc % 2][:]).then_inc(ctx_stored[qc % 2], 16)
            sp.wait_ge(w_in, 48 * (NG + 1))
            for b in range(2):
                sp.wait_ge(ctx_stored[b], 16 * NG * NQ // 2 + 1)

        @block.gpsimd
        def _(pool):
            setup = Chain(pool, masks_set)
            for t in (first_half, second_half, first_big, second_big):
                setup.link(pool.memset(t[:], 0.0))
            setup.link(pool.memset(ones[:], 1.0))
            setup.link(pool.memset(first_half[0:1, 0:HALF], 1.0))
            setup.link(pool.memset(second_half[0:1, HALF:P], 1.0))
            setup.link(pool.memset(first_big[0:1, 0:HALF], BIG))
            setup.link(pool.memset(second_big[0:1, HALF:P], BIG))
            for j in range(HG):
                setup.link(pool.memset(stack[1][j][M_ROW:P, :].bitcast(F32), 1.0))
            pool.wait_ge(consts_in, 48)
            with pool.Fori(0, NG) as g:
                for u in range(n_rope):
                    b, tc = u % 2, rope_units[u][1]
                    pool.wait_ge(raw_copied, g * n_rope + (u + 1))
                    if u >= 2:
                        pool.wait_ge(added, g * n_rope + (u - 1))
                    pool.tensor_tensor(by_cos[:, b], raw[:, b], cos[:, tc * QC:(tc + 1) * QC],
                                       ALU.mult).then_inc(cos_done, 1)
                for qc in range(NQ):
                    for n in range(n_adds[0][qc]):
                        add_to_sums(pool, g, qc, n, 0)

        @block.tensor
        def _(pe):
            pe.wait_ge(consts_in, 48)
            pe.wait_ge(masks_set, 9 + HG)

            with pe.Fori(0, NG) as g:
                def project(u):
                    s, tc = rope_units[u]
                    if u >= 2:
                        pe.wait_ge(raw_copied, g * n_rope + (u - 1))
                    for k in range(KC):
                        last = pe.matmul(mx[:, u % 2], (wq, wk)[s][:, k], xnT[:, k, tc * QC:(tc + 1) * QC],
                                         start=(k == 0), stop=(k == KC - 1))
                    last.then_inc(qk_projected, 1)

                def rotate_pairs(u):
                    pe.wait_ge(raw_copied, g * n_rope + (u + 1))
                    if u >= 2:
                        pe.wait_ge(split_done, g * n_rope + (u - 1))
                    pe.matmul(st[:, u % 2], rotate[:], raw[:, u % 2], start=True, stop=True)\
                        .then_inc(rotated, 1)

                def project_v(tile):
                    n, t = divmod(tile, QT)
                    if n >= 2 and t == 0:
                        pe.wait_ge(v_copied, g * NQ + (n - 1))
                    for k in range(KC):
                        last = pe.matmul(out_banks[n % 2][:, t * P:(t + 1) * P], xnT[:, k, tile * P:(tile + 1) * P],
                                         wv[:, k], start=(k == 0), stop=(k == KC - 1))
                    if t == QT - 1:
                        last.then_inc(v_projected, 1)

                def max_unit(qc, n, use):
                    qt, kc, j, w = units[qc][n]
                    pe.wait_ge(mx_free, g * n_mx + (use + 1))
                    diagonal = (qt + 1) * P <= (kc + 1) * QC
                    last = pe.matmul(mx[:, use % 2, 0:w], stack[0][j][0:M_ROW, qt * P:(qt + 1) * P],
                                     stack[1][j][0:M_ROW, kc * QC:kc * QC + w], start=True, stop=not diagonal)
                    if diagonal:
                        last = pe.matmul(mx[:, use % 2, w - P:w], first_half[:], second_big[:],
                                         start=False, stop=True)
                    last.then_inc(mx_ready, 1)

                def turn_max(qc, use):
                    pe.wait_ge(mx_free, g * n_mx + (use + 1))
                    pe.wait_ge(negmax_split, g * NQ + (qc + 1))
                    for t in range(QT):
                        last = pe.transpose(mx[:, use % 2, t * P:(t + 1) * P], spread[:, t], ident[:])
                    last.then_inc(mx_ready, 1)

                def scores(qc, i, j):
                    kt, q0 = steps[qc][i]
                    s = first_step[qc] + i
                    diagonal = kt >= QT * qc
                    if i == 0 and j == 0:
                        pe.wait_ge(max_rows_in, g * (64 * NQ) + (64 * (qc + 1) + 1))
                    if s and j % 2 == 0:
                        pe.wait_ge(exp_done, g * (2 * n_steps) + (2 * s + j // 2 - 1))
                    last = pe.matmul(st[:, j, q0:QC], stack[1][j][0:M_ROW + 2, kt * P:(kt + 1) * P],
                                     stack[0][j][0:M_ROW + 2, qc * QC + q0:(qc + 1) * QC],
                                     start=True, stop=not diagonal)
                    if diagonal:
                        last = pe.matmul(st[:, j, q0:q0 + P], second_half[:], first_big[:],
                                         start=False, stop=True)
                    if j % 2:
                        last.then_inc(st_ready, 1)

                def part_of(qc, i, part):
                    q0, n = steps[qc][i][1], parts[qc][i]
                    return slice(q0 + part * (QC - q0) // n, q0 + (part + 1) * (QC - q0) // n)

                def weigh_values(qc, i, part):
                    kt, cols = steps[qc][i][0], part_of(qc, i, part)
                    s = first_step[qc] + i
                    pe.wait_ge(exp_done, g * (2 * n_steps) + (2 * s + 2))
                    if i == 0 and part == 0:
                        pe.wait_ge(ctx_ready, g * NQ + (qc + 1))
                    for j in range(HG):
                        last = pe.matmul(pv[j * D:(j + 1) * D, cols], v[:, kt, j * D:(j + 1) * D],
                                         probs[s % 2][:, j, cols], start=(i == 0), stop=(i == len(steps[qc]) - 1))
                    if i in added_steps[qc] and part == parts[qc][i] - 1:
                        last.then_inc(pv_done, 1)

                def sum_probs(qc, i, part):
                    cols = part_of(qc, i, part)
                    s = first_step[qc] + i
                    for j in range(HG):
                        last = pe.matmul(den[j * D:(j + 1) * D, cols], ones[:], probs[s % 2][:, j, cols],
                                         start=(i == 0),
                                         stop=(i == len(steps[qc]) - 1 and not added_steps[qc]))
                    if part == parts[qc][i] - 1:
                        last.then_inc(pv_done, 1)

                def sum_the_sums(qc):
                    for by in range(2):
                        if n_adds[by][qc]:
                            pe.wait_ge(summed[by], adds(g, by, qc, n_adds[by][qc]))
                    q0 = steps[qc][added_steps[qc][0]][1]
                    for j in range(HG):
                        last = pe.matmul(den[j * D:(j + 1) * D, q0:QC], ones[:], sums[:, j, q0:QC],
                                         start=False, stop=True)
                    last.then_inc(den_done, 1)

                pe.wait_ge(w_in, g * 48 + 48)
                pe.wait_ge(mx_free, g * n_mx + 2)
                project(0)
                for u in range(1, n_rope):
                    project(u)
                    rotate_pairs(u - 1)
                rotate_pairs(n_rope - 1)
                pe.wait_ge(ctx_ready, g * NQ + 1)
                v_tile = 0
                while v_tile < QT:
                    project_v(v_tile)
                    v_tile += 1
                pe.wait_ge(stack_in[0], g * HALF_IN + (HALF_IN + 1))
                use = 0
                for n in range(len(units[0])):
                    max_unit(0, n, use)
                    use += 1
                    if n % 2:
                        project_v(v_tile)
                        v_tile += 1
                turn_max(0, use)
                use += 1
                ahead = 0
                while v_tile < NT:
                    project_v(v_tile)
                    v_tile += 1
                    for _ in range(2):
                        max_unit(1, ahead, use)
                        ahead, use = ahead + 1, use + 1
                pe.wait_ge(v_copied, g * NQ + NQ)
                assert ahead == V_AHEAD
                for what, qc, *at in order:
                    if what == "scores":
                        scores(qc, *at)
                    elif what == "values":
                        weigh_values(qc, *at)
                    elif what == "sums":
                        sum_probs(qc, *at)
                    elif what == "normalise":
                        if added_steps[qc]:
                            sum_the_sums(qc)
                    elif what == "turn":
                        turn_max(qc, use)
                        use += 1
                    elif what == "unit":
                        if (qc, *at) == (2, 0):
                            pe.wait_ge(stack_in[1], g * HALF_IN + (HALF_IN + 1))
                        max_unit(qc, *at, use)
                        use += 1
                assert use == n_mx

        @block.scalar
        def _(act):
            with act.Fori(0, NG) as g:
                for u in range(n_rope):
                    act.wait_ge(qk_projected, g * n_rope + (u + 1))
                    if u >= 2:
                        act.wait_ge(rotated, g * n_rope + (u - 1))
                        act.wait_ge(cos_done, g * n_rope + (u - 1))
                    act.copy(raw[:, u % 2], mx[:, u % 2]).then_inc(raw_copied, 1)
                for n in range(NQ):
                    act.wait_ge(v_projected, g * NQ + (n + 2))
                    act.copy(v[:, n * QT:(n + 1) * QT, :],
                             out_banks[n % 2][:].rearrange("p (t c) -> p t c", t=QT)).then_inc(v_copied, 1)
                for qc in range(NQ):
                    for i, (kt, q0) in enumerate(steps[qc]):
                        s = first_step[qc] + i
                        for pair in range(2):
                            heads = slice(2 * pair, 2 * pair + 2)
                            act.wait_ge(st_ready, g * (2 * n_steps) + (2 * s + pair + 1))
                            if s >= 2:
                                act.wait_ge(pv_done, g * n_steps + s)
                                in_chunk = max(n for n in range(NQ) if first_step[n] <= s - 2)
                                was = s - 2 - first_step[in_chunk]
                                if was in added_steps[in_chunk][1:]:
                                    for by in range(2):
                                        if n_adds[by][in_chunk]:
                                            act.wait_ge(summed[by],
                                                        adds(g, by, in_chunk, added_steps[in_chunk].index(was)))
                            act.activation(probs[s % 2][:, heads, q0:QC], st[:, heads, q0:QC], ACT.Exp,
                                           scale=scale).then_inc(exp_done, 1)
                        if i in added_steps[qc][:1]:
                            if sums_of(qc) == 0:
                                act.wait_ge(split_done, g * n_rope + n_rope)
                            else:
                                act.wait_ge(den_done, g * n_sums + sums_of(qc))
                            act.wait_ge(exp_done, g * (2 * n_steps) + (2 * s + 2))
                            act.copy(sums[:, :, q0:QC], probs[s % 2][:, :, q0:QC]).then_inc(sums_begun, 1)

        @block.vector
        def _(dve):
            dve.memset(tops[:], -3.0e38).then_inc(zeros_set, 1)
            dve.memset(spread[:], 0.0).then_inc(zeros_set, 1)
            dve.wait_ge(zeros_set, 2)
            dve.wait_ge(consts_in, 48)
            dve.sem_inc(mx_free, 2)
            for started in (v_projected, pv_done, ctx_ready, max_rows_in, *stack_in, *ctx_stored):
                dve.sem_inc(started, 1)
            per = 2 * n_rope + 5 * NQ
            with dve.Fori(0, NG) as g:
                c = Chain(dve, chain, g * per)
                for u in range(n_rope):
                    b, (s, tc) = u % 2, rope_units[u]
                    cols = slice(tc * QC, (tc + 1) * QC)
                    dve.wait_ge(rotated, g * n_rope + (u + 1))
                    c.link(dve.tensor_tensor(by_sin[:, b], st[:, b], sin[:, cols], ALU.mult))
                    dve.wait_ge(cos_done, g * n_rope + (u + 1))
                    dve.tensor_tensor(by_sin[:, b], by_sin[:, b], by_cos[:, b], ALU.add).then_inc(added, 1)
                    dve.wait_ge(added, g * n_rope + (u + 1))
                    dve.wait_ge(stack_in[tc // 2], g * HALF_IN + 1)
                    c.link(dve.tensor_copy(hilo[s][:, 0, cols], by_sin[:, b]))
                    dve.tensor_tensor(hilo[s][:, 1, cols], by_sin[:, b], hilo[s][:, 0, cols].bitcast(F32),
                                      ALU.subtract).then_inc(split_done, 1)

                state = {"use": 0}

                def max_of_unit(qc, n):
                    qt, kc, j, w = units[qc][n]
                    dve.wait_ge(mx_ready, g * n_mx + (state["use"] + 1))
                    dve.tensor_reduce(tops[:, qt, j, kc:kc + 1], mx[:, state["use"] % 2, 0:w], AX.X,
                                      ALU.max).then_inc(mx_free, 1)
                    state["use"] += 1

                def negate_and_split(qc):
                    dve.wait_ge(mx_free, g * n_mx + (state["use"] + 2))
                    lo_hi = spread[:].rearrange("p t (j r) -> p t j r", r=D)
                    c.link(dve.tensor_reduce(negmax[:], tops[:, QT * qc:QT * (qc + 1)], AX.X, ALU.max,
                                             negate=True))
                    c.link(dve.tensor_copy(negmax_hi[:], negmax[:]))
                    dve.tensor_copy(lo_hi[:, :, :, 0], negmax_hi[:].bitcast(F32))
                    dve.tensor_tensor(lo_hi[:, :, :, 1], negmax[:], negmax_hi[:].bitcast(F32),
                                      ALU.subtract).then_inc(negmax_split, 1)

                def max_to_rows(qc):
                    dve.wait_ge(mx_ready, g * n_mx + (state["use"] + 1))
                    dve.wait_ge(max_rows_in, g * (64 * NQ) + (64 * qc + 1))
                    dve.tensor_copy(max_rows[:], mx[:, state["use"] % 2]).then_inc(mx_free, 1)
                    dve.wait_ge(mx_free, g * n_mx + (state["use"] + 3))
                    dve.sem_inc(max_rows_set, 1)
                    state["use"] += 1

                def normalise(qc):
                    if added_steps[qc]:
                        dve.wait_ge(den_done, g * n_sums + (sums_of(qc) + 1))
                    else:
                        dve.wait_ge(pv_done, g * n_steps + (first_step[qc] + len(steps[qc]) + 1))
                    c.link(dve.transpose(den_turned[:], den[:]))
                    c.link(dve.reciprocal(rden_one[:], den_turned[:].rearrange("p (b c) -> p b c", c=D)[:, :, 0]))
                    c.link(dve.transpose(rden[:], rden_one[:].rearrange("p (b o) -> p b o", o=1)
                                         .to_broadcast([P, QC // D, D])))
                    dve.wait_ge(ctx_stored[qc % 2], g * (16 * NQ // 2) + (16 * (qc // 2) + 1))
                    dve.tensor_tensor(ctxs[qc % 2][:], pv[:], rden[:], ALU.mult).then_inc(ctx_ready, 1)

                for n in range(len(units[0])):
                    max_of_unit(0, n)
                negate_and_split(0)
                max_to_rows(0)
                for n in range(V_AHEAD):
                    max_of_unit(1, n)
                for what, qc, *at in order:
                    if what == "unit":
                        max_of_unit(qc, *at)
                    elif what == "negmax":
                        negate_and_split(qc)
                    elif what == "turn":
                        max_to_rows(qc)
                    elif what == "values" and at[1] == 0 and n_adds[1][qc] and at[0] in added_steps[qc][1:]:
                        add_to_sums(dve, g, qc, added_steps[qc].index(at[0]) - 1, 1)
                    elif what == "normalise":
                        normalise(qc)
                c.done(per)


def staggered(n, *steps):
    for at in range(n + len(steps) - 1):
        for lag, step in enumerate(steps):
            if 0 <= at - lag < n:
                step(at - lag)


def layer_norms(nc, x_dram, ctx_dram, wo_t, w_norm_row, w_router, w_shared_gate, tokens_dram,
                ident, neg_half, x1, acc, xfT, logits):
    NB = 4
    TURNS = NT // NB
    with ExitStack() as ctx:
        m = Mem(nc, ctx)
        ct, xt = m.sb("c_ctx", [P, NB, NG, P]), m.sb("c_x", [P, NB, C])
        wo = m.sb("c_wo", [P, KC, C])
        w_norm = m.sb("c_w_norm", [P, C])
        wr = m.sb("c_w_router", [P, KC, E + 1])
        x1s, h = m.sb("c_x1s", [P, NB, C]), m.sb("c_h", [P, NB, C])
        o_centred, sq, xf = m.sb("c_o_centred", [P, NB, C]), m.sb("c_sq", [P, 2, C]), m.sb("c_xf", [P, NB, C])
        xft = m.sb("c_xft", [P, NB, KC, P])
        stats, mv = m.sb("c_stats", [P, NB, 6]), m.sb("c_mv", [P, NB, 2])
        negmean = m.sb("c_negmean", [P, NB])
        veps, rstd = m.sb("c_veps", [P, NB]), m.sb("c_rstd", [P, NB])
        mean_sq = m.sb("c_mean_sq", [P, NB])
        held = m.sem("c_held")
        ob, tp, lg = m.ps("c_o", [P, NB, C]), m.ps("c_tp", [P, 2, KC, P]), m.ps("c_lg", [P, 2, 512])
        w_in = m.sem("c_w_in")
        in_ready = [m.sem(f"c_in_ready{b}") for b in range(NB)]
        o_ready = m.sem("c_o_ready")
        negmean_done = m.sem("c_negmean_done")
        o_centred_done = m.sem("c_o_centred_done")
        x1_done = m.sem("c_x1_done")
        x1_kept, h_kept = m.sem("c_x1_kept"), m.sem("c_h_kept")
        h_done, sq_done = m.sem("c_h_done"), m.sem("c_sq_done")
        stats_done, mv_done = m.sem("c_stats_done"), m.sem("c_mv_done")
        var_ready, rstd_ready = m.sem("c_var_ready"), m.sem("c_rstd_ready")
        xf_done = m.sem("c_xf_done")
        xf_stored = [m.sem(f"c_xf_stored{b}") for b in range(NB)]
        turned = m.sem("c_turned")
        turn_copied = m.sem("c_turn_copied")
        xft_kept = m.sem("c_xft_kept")
        lg_ready = m.sem("c_lg_ready")
        lg_copied = m.sem("c_lg_copied")
        block = ctx.enter_context(nc.Block())
        wr_dram = w_router.rearrange("(k p) e -> p k e", p=P)

        @block.sync
        def _(sp):
            sp.dma_start(wo[:], wo_t.rearrange("(k p) n -> p k n", p=P)).then_inc(w_in, 16)
            with sp.Fori(0, TURNS) as i:
                row = [sp.snap(i * (NB * P) + b * P) for b in range(NB)]
                for b in range(NB):
                    sp.wait_ge(o_ready, i * NB + (b + 1))
                    sp.wait_ge(x1_done, i * NB + (b + 1))
                    sp.dma_start(ct[:, b], ctx_dram.rearrange("(g p) t -> p g t", p=P)[:, :, ds(row[b], P)])\
                        .then_inc(in_ready[b], 16)
                    sp.dma_start(xt[:, b], x_dram[ds(row[b], P), :]).then_inc(in_ready[b], 16)

        @block.tensor
        def _(pe):
            pe.sem_inc(o_ready, NB)
            pe.sem_inc(turned, NB)
            pe.sem_inc(lg_ready, NB)
            pe.wait_ge(w_in, 64)

            def project(i):
                for b in range(NB):
                    pe.wait_ge(in_ready[b], i * 32 + 32)
                    pe.wait_ge(o_centred_done, i * NB + (b + 1))
                    for k in range(KC):
                        last = pe.matmul(ob[:, b], ct[:, b, k], wo[:, k], start=(k == 0), stop=(k == KC - 1))
                    last.then_inc(o_ready, 1)

            def turn_and_route(i):
                for b in range(NB):
                    pe.wait_ge(xf_done, i * NB + (b + 1))
                    pe.wait_ge(turn_copied, i * NB + (b + 1))
                    for k in range(KC):
                        last = pe.transpose(tp[:, b % 2, k], xf[:, b, k * P:(k + 1) * P], ident[:])
                    last.then_inc(turned, 1)
                for b in range(NB):
                    pe.wait_ge(turn_copied, i * NB + (b + 3))
                    pe.wait_ge(lg_copied, i * NB + (b + 1))
                    for k in range(KC):
                        last = pe.matmul(lg[:, b % 2, 0:E + 1], xft[:, b, k], wr[:, k],
                                         start=(k == 0), stop=(k == KC - 1))
                    last.then_inc(lg_ready, 1)

            project(0)
            with pe.Fori(0, TURNS - 1) as i:
                project(i + 1)
                turn_and_route(i)
            turn_and_route(TURNS - 1)

        @block.scalar
        def _(act):
            act.dma_start(w_norm[:], w_norm_row.to_broadcast([P, C])).then_inc(w_in, 16)
            act.dma_start(wr[:, :, 0:E], wr_dram).then_inc(w_in, 16)
            act.dma_start(wr[:, :, E:E + 1], w_shared_gate.rearrange("(k p) e -> p k e", p=P),
                          allow_slow_non_contiguous=True).then_inc(w_in, 16)
            act.sem_inc(turn_copied, 2)
            act.sem_inc(lg_copied, 2)
            act.sem_inc(x1_kept, NB)
            act.sem_inc(h_kept, NB)
            act.sem_inc(o_centred_done, NB)

            def centre(i):
                for b in range(NB):
                    act.wait_ge(negmean_done, i * NB + (b + 1))
                    act.wait_ge(x1_done, i * NB + (b + 1))
                    act.activation(o_centred[:, b], ob[:, b], ACT.Identity, bias=negmean[:, b:b + 1])\
                        .then_inc(o_centred_done, 1)

            def keep(i, row, last=False):
                for b in range(NB):
                    act.wait_ge(x1_done, i * NB + (b + 1 + NB))
                    hold(act, held)
                    act.copy(x1[:, ds(i * (NB * C) + b * C, C)], x1s[:, b]).then_inc(x1_kept, 1)
                for b in range(NB):
                    act.wait_ge(h_done, i * NB + (b + 1))
                    hold(act, held)
                    act.copy(acc[:, ds(i * (NB * C) + b * C, C)], h[:, b]).then_inc(h_kept, 1)
                for b in range(NB):
                    act.wait_ge(xf_done, i * NB + (b + 1))
                    act.dma_start(tokens_dram[ds(row[b], P), :], xf[:, b]).then_inc(xf_stored[b], 16)
                for b in range(NB):
                    act.wait_ge(turned, i * NB + (b + 1 + NB))
                    act.wait_ge(lg_ready, i * NB + (b + 1))
                    act.wait_ge(xft_kept, i * NB + (b + 1))
                    act.copy(xft[:, b], tp[:, b % 2])
                    act.copy(xfT[:, 0, :, ds(i * (NB * P) + b * P, P)], tp[:, b % 2]).then_inc(turn_copied, 1)
                if not last:
                    centre(i + 1)
                for b in range(NB):
                    act.wait_ge(lg_ready, i * NB + (b + 1 + NB))
                    act.copy(logits[:, ds(i * (NB * (E + 1)) + b * (E + 1), E + 1)],
                             lg[:, b % 2, 0:E + 1]).then_inc(lg_copied, 1)

            centre(0)
            with act.Fori(0, TURNS - 1) as i:
                keep(i, [act.snap(i * (NB * P) + b * P) for b in range(NB)])
            keep(TURNS - 1, [(NT - NB + b) * P for b in range(NB)], last=True)
            for b in range(NB):
                act.wait_ge(xf_stored[b], 16 * TURNS + 1)

        @block.gpsimd
        def _(pool):
            pool.sem_inc(xft_kept, NB)

            def deviation(i, phase, b):
                n = phase * NB + b
                pool.wait_ge(var_ready, i * (3 * NB) + (n + 1))
                pool.tensor_tensor(rstd[:, b:b + 1], veps[:, b:b + 1], neg_half[:], ALU.pow)\
                    .then_inc(rstd_ready, 1)

            def keep_lo(i, b):
                at = ds(i * (NB * P) + b * P, P)
                pool.wait_ge(turn_copied, i * NB + (b + 3))
                hold(pool, held)
                pool.tensor_tensor(xfT[:, 1, :, at], xft[:, b], xfT[:, 0, :, at], ALU.subtract).then_inc(xft_kept, 1)

            for phase in range(3):
                for b in range(NB):
                    deviation(0, phase, b)
            with pool.Fori(0, TURNS - 1) as i:
                for b in range(NB):
                    deviation(i + 1, 0, b)
                for b in range(NB):
                    deviation(i + 1, 1, b)
                    keep_lo(i, b)
                for b in range(NB):
                    deviation(i + 1, 2, b)
            for b in range(NB):
                keep_lo(TURNS - 1, b)

        @block.vector
        def _(dve):
            dve.sem_inc(x1_done, NB)
            for b in range(NB):
                dve.sem_inc(xf_stored[b], 1)
            dve.wait_ge(w_in, 64)
            with dve.Fori(0, TURNS) as i:
                def stats_of(ready, src):
                    def step(b):
                        dve.wait_ge(ready, i * NB + (b + 1 + NB))
                        dve.bn_stats(stats[:, b], src[:, b]).then_inc(stats_done, 1)
                    return step

                def mean_var(phase):
                    def step(b):
                        dve.wait_ge(stats_done, i * (2 * NB) + (phase * NB + b + 1))
                        hold(dve, held)
                        dve.bn_aggr(mv[:, b], stats[:, b]).then_inc(mv_done, 1)
                    return step

                def var_eps(phase):
                    def step(b):
                        dve.wait_ge(mv_done, i * (2 * NB) + (phase * NB + b + 1))
                        dve.tensor_scalar(veps[:, b:b + 1], mv[:, b, 1:2], LN_EPS, None,
                                          ALU.add).then_inc(var_ready, 1)
                        if phase == 0:
                            dve.tensor_scalar(negmean[:, b:b + 1], mv[:, b, 0:1], -1.0, None,
                                              ALU.mult).then_inc(negmean_done, 1)
                    return step

                def residual(b):
                    dve.wait_ge(rstd_ready, i * (3 * NB) + (b + 1))
                    dve.wait_ge(o_centred_done, i * NB + (b + 1 + NB))
                    dve.wait_ge(in_ready[b], i * 32 + 32)
                    dve.wait_ge(x1_kept, i * NB + (b + 1))
                    dve.scalar_tensor_tensor(out=x1s[:, b], in0=o_centred[:, b], scalar=rstd[:, b:b + 1],
                                             in1=xt[:, b], op0=ALU.mult, op1=ALU.add).then_inc(x1_done, 1)

                def normal(b):
                    dve.wait_ge(rstd_ready, i * (3 * NB) + (b + 1 + NB))
                    dve.wait_ge(h_kept, i * NB + (b + 1))
                    dve.tensor_scalar(h[:, b], x1s[:, b], mv[:, b, 0:1], rstd[:, b:b + 1],
                                      ALU.subtract, ALU.mult).then_inc(h_done, 1)

                def square_sum(b):
                    dve.wait_ge(h_done, i * NB + (b + 1))
                    dve.tensor_tensor_reduce(sq[:, b % 2], h[:, b], h[:, b], 1.0 / C, 0.0, ALU.mult, ALU.add,
                                             mean_sq[:, b:b + 1]).then_inc(sq_done, 1)

                def rms_eps(b):
                    dve.wait_ge(sq_done, i * NB + (b + 1))
                    dve.tensor_scalar(veps[:, b:b + 1], mean_sq[:, b:b + 1], RMS_EPS, None,
                                      ALU.add).then_inc(var_ready, 1)

                staggered(NB, stats_of(o_ready, ob), mean_var(0), var_eps(0))
                staggered(NB, residual, stats_of(x1_done, x1s), mean_var(1), var_eps(1))
                staggered(NB, normal, square_sum, rms_eps)
                for b in range(NB):
                    dve.wait_ge(rstd_ready, i * (3 * NB) + (b + 1 + 2 * NB))
                    dve.wait_ge(turned, i * NB + (b + 1))
                    dve.wait_ge(xf_stored[b], i * 16 + 1)
                    dve.scalar_tensor_tensor(out=xf[:, b], in0=h[:, b], scalar=rstd[:, b:b + 1], in1=w_norm[:],
                                             op0=ALU.mult, op1=ALU.mult).then_inc(xf_done, 1)


def route(nc, before_dram, logits, best, slots, shared_gate):
    with ExitStack() as ctx:
        m = Mem(nc, ctx)
        probs = m.sb("r_probs", [P, NT, E])
        rowmax, rowsum = m.sb("r_rowmax", [P, NT]), m.sb("r_rowsum", [P, NT])
        gate_e = m.sb("r_gate_e", [P, NT])
        top, top_at = m.sb("r_top", [P, NT, 8]), m.sb("r_top_at", [P, NT, 8], U32)
        expert = m.sb("r_expert", [P, NT, K])
        lane, lane_i = m.sb("r_lane", [P, NT, E]), m.sb("r_lane_i", [P, NT, E], I32)
        spare, spare_i = m.sb("r_spare", [P, 1]), m.sb("r_spare_i", [P, 1], I32)
        chosen = [m.sb(f"r_chosen{k}", [P, NT, E]) for k in range(K)]
        mask, mask_b = m.sb("r_mask", [P, NT, E]), m.sb("r_mask_b", [P, NT, E], BF16)
        before, before_b = m.sb("r_before", [P, P]), m.sb("r_before_b", [P, P], BF16)
        ones_b = m.sb("r_ones", [P, P], BF16)
        tile_sum, prefix = m.sb("r_tile_sum", [P, NT, E]), m.sb("r_prefix", [P, NT + 1, E])
        at = m.sb("r_at", [P, NT, E])
        picked = m.sb("r_picked", [P, NT, E])
        place, fits = m.sb("r_place", [P, NT, K]), m.sb("r_fits", [P, NT, K])
        slot, tile_of = m.sb("r_slot", [P, NT, K]), m.sb("r_tile_of", [P, NT, K])
        within_ps, sum_ps = m.ps("r_within", [P, NT * E]), m.ps("r_sum", [P, NT * E])
        before_in, lanes_set = m.sem("r_before_in"), m.sem("r_lanes_set")
        shifted, exp_done = m.sem("r_shifted"), m.sem("r_exp_done")
        mask_ready, counted, chain = m.sem("r_mask_ready"), m.sem("r_counted"), m.sem("r_chain")
        block = ctx.enter_context(nc.Block())
        lg = logits[:].rearrange("p (t e) -> p t e", t=NT)

        @block.sync
        def _(sp):
            sp.dma_start(before[:], before_dram).then_inc(before_in, 16)

        @block.gpsimd
        def _(pool):
            pool.iota(lane_i[:], pattern=[[0, NT], [1, E]], base=0, channel_multiplier=0).then_inc(lanes_set, 1)
            pool.wait_ge(lanes_set, 1)
            pool.iota(spare_i[:], pattern=[[0, 1]], base=SLOTS, channel_multiplier=1).then_inc(lanes_set, 1)

        @block.scalar
        def _(act):
            act.wait_ge(shifted, 1)
            act.activation(probs[:], probs[:], ACT.Exp).then_inc(exp_done, 1)
            act.activation(gate_e[:], lg[:, :, E], ACT.Exp, scale=-1.0).then_inc(exp_done, 1)

        @block.tensor
        def _(pe):
            pe.wait_ge(mask_ready, 1)
            flat = mask_b[:].rearrange("p t e -> p (t e)")
            pe.matmul(within_ps[:], before_b[:], flat, start=True, stop=True)
            pe.matmul(sum_ps[:], ones_b[:], flat, start=True, stop=True).then_inc(counted, 1)

        @block.vector
        def _(dve):
            c = Chain(dve, chain)

            def over_experts(a):
                return a[:].rearrange("p (t o) -> p t o", o=1).to_broadcast([P, NT, E])

            c.link(dve.tensor_reduce(rowmax[:], lg[:, :, 0:E], AX.X, ALU.max))
            dve.tensor_tensor(probs[:], lg[:, :, 0:E], over_experts(rowmax), ALU.subtract).then_inc(shifted, 1)
            dve.wait_ge(lanes_set, 2)
            dve.wait_ge(before_in, 16)
            dve.tensor_copy(lane[:], lane_i[:])
            dve.tensor_copy(spare[:], spare_i[:])
            dve.tensor_copy(before_b[:], before[:])
            dve.memset(ones_b[:], 1.0)
            dve.wait_ge(exp_done, 2)
            c.link(dve.tensor_reduce(rowsum[:], probs[:], AX.X, ALU.add))
            c.link(dve.reciprocal(rowsum[:], rowsum[:]))
            c.link(dve.tensor_tensor(probs[:], probs[:], over_experts(rowsum), ALU.mult))
            c.link(dve.tensor_scalar(gate_e[:], gate_e[:], 1.0, None, ALU.add))
            dve.reciprocal(shared_gate[:], gate_e[:])
            for t in range(NT):
                last = dve.max(top[:, t], probs[:, t])
            c.link(last)
            for t in range(NT):
                last = dve.max_index(top_at[:, t], top[:, t], probs[:, t])
            c.link(last)
            c.link(dve.tensor_copy(expert[:], top_at[:, :, 0:K]))
            for k in range(K):
                last = dve.tensor_tensor(chosen[k][:], lane[:],
                                         expert[:, :, k:k + 1].to_broadcast([P, NT, E]), ALU.is_equal)
            c.link(last)
            c.link(dve.tensor_tensor(mask[:], chosen[0][:], chosen[1][:], ALU.add))
            c.link(dve.tensor_tensor(mask[:], mask[:], chosen[2][:], ALU.add))
            dve.tensor_tensor(mask_b[:], mask[:], chosen[3][:], ALU.add).then_inc(mask_ready, 1)
            c.link(dve.memset(prefix[:, 0], 0.0))
            dve.wait_ge(counted, 1)
            c.link(dve.tensor_copy(tile_sum[:], sum_ps[:].rearrange("p (t e) -> p t e", t=NT)))
            for t in range(NT):
                c.link(dve.tensor_tensor(prefix[:, t + 1], prefix[:, t], tile_sum[:, t], ALU.add))
            c.link(dve.tensor_tensor(at[:], within_ps[:].rearrange("p (t e) -> p t e", t=NT),
                                     prefix[:, 0:NT], ALU.add))
            for k in range(K):
                c.link(dve.tensor_tensor(picked[:], chosen[k][:], at[:], ALU.mult))
                c.link(dve.tensor_reduce(place[:, :, k], picked[:], AX.X, ALU.add))
            c.link(dve.tensor_scalar(fits[:], place[:], float(CAP), None, ALU.is_lt))
            c.link(dve.tensor_scalar(tile_of[:], place[:], float(P), float(1 - P * E * ST), ALU.is_ge, ALU.mult))
            c.link(dve.scalar_tensor_tensor(out=slot[:], in0=place[:], scalar=float(E * ST), in1=tile_of[:],
                                            op0=ALU.mult, op1=ALU.add))
            c.link(dve.scalar_tensor_tensor(out=slot[:], in0=expert[:], scalar=float(ST), in1=slot[:],
                                            op0=ALU.mult, op1=ALU.add))
            c.link(dve.scalar_tensor_tensor(out=slot[:], in0=slot[:], scalar=spare[:, 0:1], in1=fits[:],
                                            op0=ALU.subtract, op1=ALU.mult))
            dve.tensor_scalar(slots[:], slot[:].rearrange("p t k -> p (t k)"), spare[:, 0:1], None, ALU.add)
            dve.tensor_tensor(best[:].rearrange("p (t k) -> p t k", k=K), top[:, :, 0:K], fits[:], ALU.mult)


def shared_expert(nc, sw_gate, sw_up, sw_down, ids_dram, y_dram, xfT, slots, shared_gate, acc):
    with ExitStack() as ctx:
        m = Mem(nc, ctx)
        wg_raw, wu_raw = ([m.sb(f"s_{n}_raw{b}", [P, KC, P]) for b in range(2)] for n in ("wg", "wu"))
        wd_raw = [m.sb(f"s_wd_raw{b}", [P, C]) for b in range(2)]
        wg, wu = ([m.sb(f"s_{n}{b}", [P, 2, KC, P], F32R) for b in range(2)] for n in ("wg", "wu"))
        wd = [m.sb(f"s_wd{b}", [P, 2, C], F32R) for b in range(2)]
        silu, hid_full = m.sb("s_silu", [P, 2, QC]), m.sb("s_hid_full", [P, 2, QC])
        hid = m.sb("s_hid", [P, 2, 2, QC], F32R)
        zero_ids, zero_row = m.sb("s_zero_ids", [P, SLOTS // P + 1], I32), m.sb("s_zero_row", [P, C])
        slot4 = m.sb("s_slot4", [P, 2 * K], I32)
        token, step = m.sb("s_token", [P, 2], I32), m.sb("s_step", [P, 2], I32)
        gp, up, dp = m.ps("s_g", [P, 2, QC]), m.ps("s_u", [P, 2, QC]), m.ps("s_d", [P, QT, C])
        w_in = [m.sem(f"s_w_in{b}") for b in range(2)]
        w_hi, w_split = m.sem("s_w_hi"), m.sem("s_w_split")
        gu_ready, silu_done = m.sem("s_gu_ready"), m.sem("s_silu_done")
        hid_done = m.sem("s_hid_done")
        hid_hi, hid_split = m.sem("s_hid_hi"), m.sem("s_hid_split")
        down_ready = m.sem("s_down_ready")
        down_used = m.sem("s_down_used")
        zeros_set, zeros_in = m.sem("s_zeros_set"), m.sem("s_zeros_in")
        token_set, slot4_set = m.sem("s_token_set"), m.sem("s_slot4_set")
        ids_in, held = m.sem("s_ids_in"), m.sem("s_held")
        block = ctx.enter_context(nc.Block())
        LAST = NFS - 1
        assert NFS % 2 == 1

        @block.sync
        def _(sp):
            def load(b, col):
                for raw, w_dram in ((wg_raw, sw_gate), (wu_raw, sw_up)):
                    sp.dma_start(raw[b][:], w_dram.rearrange("(k p) f -> p k f", p=P)[:, :, ds(col, P)])\
                        .then_inc(w_in[b], 16)
                sp.dma_start(wd_raw[b][:], sw_down[ds(col, P), :]).then_inc(w_in[b], 16)

            for b in range(2):
                load(b, b * P)
            sp.wait_ge(zeros_set, 2)
            sp.dma_start(ids_dram.rearrange("(p n) o -> p (n o)", p=P), zero_ids[:]).then_inc(zeros_in, 16)
            sp.dma_start(y_dram[SLOTS:SLOTS + P, :], zero_row[:]).then_inc(zeros_in, 16)
            with sp.Fori(0, NFS // 2 - 1) as i:
                col = [sp.snap(i * (2 * P) + (b + 2) * P) for b in range(2)]
                for b in range(2):
                    sp.wait_ge(w_split, i * 6 + 3 * (b + 1))
                    load(b, col[b])
            sp.wait_ge(w_split, 3 * LAST - 3)
            load(0, LAST * P)
            sp.wait_ge(zeros_in, 32)

        @block.gpsimd
        def _(pool):
            pool.iota(token[:], pattern=[[P, 2]], base=0, channel_multiplier=1).then_inc(token_set, 1)
            pool.wait_ge(token_set, 1)
            pool.iota(step[:], pattern=[[0, 2]], base=2 * P, channel_multiplier=0).then_inc(token_set, 1)
            pool.wait_ge(token_set, 2)
            pool.wait_ge(zeros_in, 32)
            with pool.Fori(0, NT // 2) as i:
                pool.tensor_copy(slot4[:], slots[:, ds(i * (2 * K), 2 * K)]).then_inc(slot4_set, 1)
                pool.wait_ge(slot4_set, i + 1)
                hold(pool, held)
                for b in range(2):
                    for k in range(K):
                        n = b * K + k
                        pool.indirect_dma_start(
                            ids_dram, bass.IndirectOffsetOnAxis(ap=slot4[:, n:n + 1].bitcast(U32), axis=0),
                            token[:, b:b + 1], None).then_inc(ids_in, 16)
                        pool.wait_ge(ids_in, i * (2 * K * 16) + 16 * (n + 1))
                        hold(pool, held)
                pool.tensor_tensor(token[:], token[:], step[:], ALU.add).then_inc(token_set, 1)
                pool.wait_ge(token_set, i + 3)

        @block.tensor
        def _(pe):
            def gate_and_up(f, b, c):
                if c == 0:
                    pe.wait_ge(w_split, f * 3 + 3)
                pe.wait_ge(hid_done, f * NQ + (c + 1))
                for w, bank in ((wg, gp), (wu, up)):
                    for k in range(KC):
                        for part, (of_w, of_x) in enumerate(PRODUCTS):
                            last = pe.matmul(bank[:, c % 2], w[b][:, of_w, k], xfT[:, of_x, k, c * QC:(c + 1) * QC],
                                             start=(k == 0 and part == 0), stop=(k == KC - 1 and part == 2))
                last.then_inc(gu_ready, 1)

            def down(f, b, c):
                pe.wait_ge(hid_split, f * NQ + (c + 1))
                for t in range(QT):
                    pe.wait_ge(down_used, f * (NQ * QT) + (c * QT + t + 1))
                    for part, (of_w, of_h) in enumerate(PRODUCTS):
                        last = pe.matmul(dp[:, t], hid[:, c % 2, of_h, t * P:(t + 1) * P], wd[b][:, of_w],
                                         start=(part == 0), stop=(part == 2))
                    last.then_inc(down_ready, 1)

            def tile(f, b, last=False):
                for c in range(NQ):
                    if c < NQ - 1:
                        gate_and_up(f, b, c + 1)
                    elif not last:
                        gate_and_up(f + 1, 1 - b, 0)
                    down(f, b, c)

            gate_and_up(0, 0, 0)
            with pe.Fori(0, NFS // 2) as i:
                for b in range(2):
                    tile(i * 2 + b, b)
            tile(LAST, 0, last=True)

        @block.scalar
        def _(act):
            def split_weights(b, i):
                act.wait_ge(w_in[b], i * 48 + 48)
                for hi, raw in ((wg[b][:, 0], wg_raw[b][:]), (wu[b][:, 0], wu_raw[b][:]), (wd[b][:, 0], wd_raw[b][:])):
                    act.copy(hi, raw).then_inc(w_hi, 1)

            def hidden(f, c):
                act.wait_ge(gu_ready, f * NQ + (c + 1))
                act.activation(silu[:, c % 2], gp[:, c % 2], ACT.Silu).then_inc(silu_done, 1)
                act.wait_ge(hid_done, f * NQ + (c + 3))
                act.copy(hid[:, c % 2, 0], hid_full[:, c % 2]).then_inc(hid_hi, 1)

            split_weights(0, 0)
            with act.Fori(0, NFS // 2) as i:
                for b in range(2):
                    for c in range(NQ):
                        hidden(i * 2 + b, c)
                        if c == 1:
                            split_weights(1 - b, i + b)
            for c in range(NQ):
                hidden(LAST, c)

        @block.vector
        def _(dve):
            dve.memset(zero_ids[:], 0).then_inc(zeros_set, 1)
            dve.memset(zero_row[:], 0.0).then_inc(zeros_set, 1)
            dve.sem_inc(hid_done, 2)
            dve.sem_inc(down_used, QT)

            def split_weights(b, f):
                for n, (w, raw) in enumerate(((wg[b], wg_raw[b]), (wu[b], wu_raw[b]), (wd[b], wd_raw[b]))):
                    dve.wait_ge(w_hi, f * 3 + (n + 1))
                    dve.tensor_tensor(w[:, 1], raw[:], w[:, 0], ALU.subtract).then_inc(w_split, 1)

            def hidden_full(f, c):
                dve.wait_ge(silu_done, f * NQ + (c + 1))
                dve.tensor_tensor(hid_full[:, c % 2], up[:, c % 2], silu[:, c % 2], ALU.mult).then_inc(hid_done, 1)

            def hidden_lo(f, c):
                dve.wait_ge(hid_hi, f * NQ + (c + 1))
                dve.tensor_tensor(hid[:, c % 2, 1], hid_full[:, c % 2], hid[:, c % 2, 0],
                                  ALU.subtract).then_inc(hid_split, 1)

            def accumulate(f, c, tiles):
                for t in tiles:
                    n = c * QT + t
                    dve.wait_ge(down_ready, f * (NQ * QT) + (n + 1))
                    acc_t = acc[:, n * C:(n + 1) * C]
                    dve.scalar_tensor_tensor(out=acc_t, in0=dp[:, t], scalar=shared_gate[:, n:n + 1], in1=acc_t,
                                             op0=ALU.mult, op1=ALU.add).then_inc(down_used, 1)

            def tile(f, b, last=False):
                for c in range(NQ):
                    following = (f, c + 1) if c < NQ - 1 else None if last else (f + 1, 0)
                    if following:
                        hidden_full(*following)
                    accumulate(f, c, range(0, QT // 2))
                    if following:
                        hidden_lo(*following)
                    accumulate(f, c, range(QT // 2, QT))
                    if c == 1 and not last:
                        split_weights(1 - b, f + 1)

            split_weights(0, 0)
            hidden_full(0, 0)
            hidden_lo(0, 0)
            with dve.Fori(0, NFS // 2) as i:
                for b in range(2):
                    tile(i * 2 + b, b)
            tile(LAST, 0, last=True)


def experts(nc, w_gate, w_up, w_down, tokens_dram, ids_dram, y_dram, ident):
    NF = len(FT)
    KH = KC // 2
    with ExitStack() as ctx:
        m = Mem(nc, ctx)
        wg_raw, wu_raw = ([m.sb(f"e_{n}_raw{b}", [P, KC, F]) for b in range(2)] for n in ("wg", "wu"))
        wd_raw = [m.sb(f"e_wd_raw{b}", [P, NF, C]) for b in range(2)]
        wg, wu = ([m.sb(f"e_{n}{b}", [P, 2, KC, F], F32R) for b in range(2)] for n in ("wg", "wu"))
        wd = [m.sb(f"e_wd{b}", [P, 2, NF, C], F32R) for b in range(2)]
        ids = m.sb("e_ids", [P, E * ST], I32)
        ids_now = [m.sb(f"e_ids_now{b}", [P, ST], I32) for b in range(2)]
        xg = [m.sb(f"e_xg{b}", [P, ST, C]) for b in range(2)]
        xgT = m.sb("e_xgT", [P, 2, KC, CAP], F32R)
        silu, hid_full = m.sb("e_silu", [P, NF, CAP]), m.sb("e_hid_full", [P, NF, CAP])
        hid = m.sb("e_hid", [P, 2, NF, CAP], F32R)
        y = [m.sb(f"e_y{b}", [P, ST, C]) for b in range(2)]
        tp = m.ps("e_tp", [P, ST, KC, P])
        gu = m.ps("e_gu", [P, NF, 2, CAP])
        dp = m.ps("e_d", [P, ST, C])
        ids_in, ids_copied, held = m.sem("e_ids_in"), m.sem("e_ids_copied"), m.sem("e_held")
        gate_in = [m.sem(f"e_gate_in{b}") for b in range(2)]
        up_in = [m.sem(f"e_up_in{b}") for b in range(2)]
        down_in = [m.sem(f"e_down_in{b}") for b in range(2)]
        w_hi = m.sem("e_w_hi")
        gate_split, up_split, down_split = m.sem("e_gate_split"), m.sem("e_up_split"), m.sem("e_down_split")
        xg_in = [m.sem(f"e_xg_in{b}") for b in range(2)]
        turned, xg_hi, xg_split = m.sem("e_turned"), m.sem("e_xg_hi"), m.sem("e_xg_split")
        gu_ready, silu_done = m.sem("e_gu_ready"), m.sem("e_silu_done")
        hid_done = m.sem("e_hid_done")
        hid_hi, hid_split = m.sem("e_hid_hi"), m.sem("e_hid_split")
        down_ready = m.sem("e_down_ready")
        y_copied = m.sem("e_y_copied")
        y_stored = [m.sem(f"e_y_stored{b}") for b in range(2)]
        block = ctx.enter_context(nc.Block())
        N_HI = 2 + 2 + NF

        def gate_up_parts(b, raw, split):
            return [(raw[b][:, h * KH:(h + 1) * KH], split[b][:, 0, h * KH:(h + 1) * KH],
                     split[b][:, 1, h * KH:(h + 1) * KH]) for h in range(2)]

        def down_parts(b):
            return [(wd_raw[b][0:w, n], wd[b][0:w, 0, n], wd[b][0:w, 1, n]) for n, (f0, w) in enumerate(FT)]

        @block.sync
        def _(sp):
            sp.dma_start(ids[:], ids_dram[0:SLOTS, :].rearrange("(p n) o -> p (n o)", p=P)).then_inc(ids_in, 16)

            def load_gate_up(b, row):
                for raw, w_dram, loaded in ((wg_raw, w_gate, gate_in), (wu_raw, w_up, up_in)):
                    sp.dma_start(raw[b][:], w_dram[ds(row, C), :].rearrange("(k p) f -> p k f", p=P))\
                        .then_inc(loaded[b], 16)

            def load_down(b, frow, frow_rest):
                sp.dma_start(wd_raw[b][:, 0:2], w_down[ds(frow, 2 * P), :].rearrange("(f p) n -> p f n", p=P))\
                    .then_inc(down_in[b], 16)
                sp.dma_start(wd_raw[b][0:FT[2][1], 2], w_down[ds(frow_rest, FT[2][1]), :])\
                    .then_inc(down_in[b], 16)

            for b in range(2):
                load_gate_up(b, b * C)
                load_down(b, b * F, b * F + FT[2][0])
            with sp.Fori(0, E // 2 - 1) as i:
                row = [sp.snap(i * (2 * C) + (b + 2) * C) for b in range(2)]
                frow = [sp.snap(i * (2 * F) + (b + 2) * F) for b in range(2)]
                frow_rest = [sp.snap(i * (2 * F) + ((b + 2) * F + FT[2][0])) for b in range(2)]
                for b in range(2):
                    sp.wait_ge(gate_split, i * 4 + 2 * (b + 1))
                    sp.wait_ge(up_split, i * 4 + 2 * (b + 1))
                    load_gate_up(b, row[b])
                    sp.wait_ge(down_split, i * (2 * NF) + NF * (b + 1))
                    load_down(b, frow[b], frow_rest[b])

        @block.gpsimd
        def _(pool):
            def gather(b, col, e):
                pool.tensor_copy(ids_now[b][:], ids[:, ds(col, ST)]).then_inc(ids_copied, 1)
                pool.wait_ge(ids_copied, e + 1)
                hold(pool, held)
                for t in range(ST):
                    pool.indirect_dma_start(
                        xg[b][:, t], None, tokens_dram,
                        bass.IndirectOffsetOnAxis(ap=ids_now[b][:, t:t + 1].bitcast(U32), axis=0))\
                        .then_inc(xg_in[b], 16)

            def split_up_down(b, e):
                for n, (raw, hi, lo) in enumerate(gate_up_parts(b, wu_raw, wu)):
                    pool.wait_ge(w_hi, e * N_HI + (3 + n))
                    hold(pool, held)
                    pool.tensor_tensor(lo, raw, hi, ALU.subtract).then_inc(up_split, 1)
                for n, (raw, hi, lo) in enumerate(down_parts(b)):
                    pool.wait_ge(w_hi, e * N_HI + (5 + n))
                    hold(pool, held)
                    pool.tensor_tensor(lo, raw, hi, ALU.subtract).then_inc(down_split, 1)

            pool.wait_ge(ids_in, 16)
            gather(0, 0, 0)
            gather(1, ST, 1)
            split_up_down(0, 0)
            with pool.Fori(0, E // 2 - 1) as i:
                for b in range(2):
                    pool.wait_ge(turned, i * (2 * ST) + ST * (b + 1))
                    hold(pool, held)
                    gather(b, i * (2 * ST) + ST * (b + 2), i * 2 + (b + 2))
                    split_up_down(1 - b, i * 2 + (b + 1))
            split_up_down(1, E - 1)

        @block.tensor
        def _(pe):
            def turn(b, e, i):
                pe.wait_ge(xg_in[b], i * (16 * ST) + 16 * ST)
                for t in range(ST):
                    for k in range(KC):
                        last = pe.transpose(tp[:, t, k], xg[b][:, t, k * P:(k + 1) * P], ident[:])
                    last.then_inc(turned, 1)

            def gate_and_up(b, e):
                pe.wait_ge(xg_split, e * ST + ST)
                pe.wait_ge(gate_split, e * 2 + 2)
                pe.wait_ge(up_split, e * 2 + 2)
                for n, (f0, w) in enumerate(FT):
                    pe.wait_ge(hid_done, e * NF + (n + 1))
                    for s, weights in enumerate((wg, wu)):
                        for k in range(KC):
                            for part, (of_w, of_x) in enumerate(PRODUCTS):
                                last = pe.matmul(gu[0:w, n, s], weights[b][:, of_w, k, f0:f0 + w], xgT[:, of_x, k],
                                                 start=(k == 0 and part == 0), stop=(k == KC - 1 and part == 2))
                    last.then_inc(gu_ready, 1)

            def down(b, e):
                pe.wait_ge(y_copied, e * ST + ST)
                pe.wait_ge(down_split, e * NF + NF)
                for n, (f0, w) in enumerate(FT):
                    pe.wait_ge(hid_split, e * NF + (n + 1))
                    for t in range(ST):
                        for part, (of_w, of_h) in enumerate(PRODUCTS):
                            last = pe.matmul(dp[:, t], hid[0:w, of_h, n, t * P:(t + 1) * P], wd[b][0:w, of_w, n],
                                             start=(n == 0 and part == 0), stop=(n == NF - 1 and part == 2))
                        if n == NF - 1:
                            last.then_inc(down_ready, 1)

            turn(0, 0, 0)
            with pe.Fori(0, E // 2 - 1) as i:
                for b in range(2):
                    gate_and_up(b, i * 2 + b)
                    turn(1 - b, i * 2 + (b + 1), i + b)
                    down(b, i * 2 + b)
            gate_and_up(0, E - 2)
            turn(1, E - 1, E // 2 - 1)
            down(0, E - 2)
            gate_and_up(1, E - 1)
            down(1, E - 1)

        @block.scalar
        def _(act):
            act.sem_inc(y_copied, ST)
            for b in range(2):
                act.sem_inc(y_stored[b], 1)

            def split_hi(parts, loaded, count):
                act.wait_ge(loaded, count)
                for raw, hi, _ in parts:
                    act.copy(hi, raw).then_inc(w_hi, 1)

            def split_gate(b, i):
                split_hi(gate_up_parts(b, wg_raw, wg), gate_in[b], i * 16 + 16)

            def split_up(b, i):
                split_hi(gate_up_parts(b, wu_raw, wu), up_in[b], i * 16 + 16)

            def split_down(b, i):
                split_hi(down_parts(b), down_in[b], i * 32 + 32)

            def tokens_hi(e):
                for t in range(ST):
                    act.wait_ge(turned, e * ST + (t + 1))
                    act.copy(xgT[:, 0, :, t * P:(t + 1) * P], tp[:, t]).then_inc(xg_hi, 1)

            def hidden(e, n):
                w = FT[n][1]
                act.wait_ge(gu_ready, e * NF + (n + 1))
                act.activation(silu[0:w, n], gu[0:w, n, 0], ACT.Silu).then_inc(silu_done, 1)
                act.wait_ge(hid_done, e * NF + (n + 1 + NF))
                act.copy(hid[0:w, 0, n], hid_full[0:w, n]).then_inc(hid_hi, 1)

            def results(b, e, i, y_row):
                for t in range(ST):
                    act.wait_ge(down_ready, e * ST + (t + 1))
                    act.wait_ge(y_stored[b], i * 16 + 1)
                    act.copy(y[b][:, t], dp[:, t]).then_inc(y_copied, 1)
                act.wait_ge(y_copied, e * ST + 2 * ST)
                act.dma_start(y_dram[0:SLOTS, :].rearrange("(p n) c -> p n c", p=P)[:, ds(y_row, ST)], y[b][:])\
                    .then_inc(y_stored[b], 16)

            def expert(b, i, y_row, last=False):
                e = i * 2 + b
                if not last:
                    split_gate(1 - b, i + b)
                hidden(e, 0)
                if not last:
                    split_up(1 - b, i + b)
                hidden(e, 1)
                if not last:
                    split_down(1 - b, i + b)
                hidden(e, 2)
                if not last:
                    tokens_hi(e + 1)
                results(b, e, i, y_row)

            split_gate(0, 0)
            tokens_hi(0)
            split_up(0, 0)
            split_down(0, 0)
            with act.Fori(0, E // 2 - 1) as i:
                y_row = [act.snap(i * (2 * ST) + b * ST) for b in range(2)]
                for b in range(2):
                    expert(b, i, y_row[b])
            expert(0, E // 2 - 1, (E - 2) * ST)
            expert(1, E // 2 - 1, (E - 1) * ST, last=True)
            for b in range(2):
                act.wait_ge(y_stored[b], 16 * E // 2 + 1)

        @block.vector
        def _(dve):
            dve.sem_inc(hid_done, NF)

            def split_gate(b, e):
                for n, (raw, hi, lo) in enumerate(gate_up_parts(b, wg_raw, wg)):
                    dve.wait_ge(w_hi, e * N_HI + (n + 1))
                    dve.tensor_tensor(lo, raw, hi, ALU.subtract).then_inc(gate_split, 1)

            def tokens_lo(e):
                for t in range(ST):
                    dve.wait_ge(xg_hi, e * ST + (t + 1))
                    dve.tensor_tensor(xgT[:, 1, :, t * P:(t + 1) * P], tp[:, t], xgT[:, 0, :, t * P:(t + 1) * P],
                                      ALU.subtract).then_inc(xg_split, 1)

            def hidden(e):
                for n, (f0, w) in enumerate(FT):
                    dve.wait_ge(silu_done, e * NF + (n + 1))
                    dve.tensor_tensor(hid_full[0:w, n], gu[0:w, n, 1], silu[0:w, n], ALU.mult).then_inc(hid_done, 1)
                    dve.wait_ge(hid_hi, e * NF + (n + 1))
                    dve.tensor_tensor(hid[0:w, 1, n], hid_full[0:w, n], hid[0:w, 0, n],
                                      ALU.subtract).then_inc(hid_split, 1)

            split_gate(0, 0)
            tokens_lo(0)
            with dve.Fori(0, E // 2 - 1) as i:
                for b in range(2):
                    split_gate(1 - b, i * 2 + (b + 1))
                    hidden(i * 2 + b)
                    tokens_lo(i * 2 + (b + 1))
            split_gate(1, E - 1)
            hidden(E - 2)
            tokens_lo(E - 1)
            hidden(E - 1)


def combine(nc, y_dram, out_dram, x1, acc, best, slots, neg_half):
    NB, PAIRS = 4, NT // 2
    with ExitStack() as ctx:
        m = Mem(nc, ctx)
        slot4 = [m.sb(f"f_slot4{h}", [P, 2 * K], I32) for h in range(2)]
        yk = [m.sb(f"f_y{b}", [P, K, C]) for b in range(NB)]
        total, centred = m.sb("f_total", [P, NB, C]), m.sb("f_centred", [P, NB, C])
        o = m.sb("f_out", [P, NB, C])
        stats, mv = m.sb("f_stats", [P, NB, 6]), m.sb("f_mv", [P, NB, 2])
        negmean = m.sb("f_negmean", [P, NB])
        veps, rstd = m.sb("f_veps", [P, NB]), m.sb("f_rstd", [P, NB])
        held = m.sem("f_held")
        slot4_set = m.sem("f_slot4_set")
        y_in = [m.sem(f"f_y_in{b}") for b in range(NB)]
        y_used = m.sem("f_y_used")
        mean_ready, var_ready, rstd_ready = m.sem("f_mean_ready"), m.sem("f_var_ready"), m.sem("f_rstd_ready")
        centred_done, out_ready = m.sem("f_centred_done"), m.sem("f_out_ready")
        out_stored = [m.sem(f"f_out_stored{b}") for b in range(NB)]
        chain = m.sem("f_chain")
        block = ctx.enter_context(nc.Block())

        @block.gpsimd
        def _(pool):
            def gather(pair, h):
                pool.wait_ge(y_used, pair)
                hold(pool, held)
                pool.tensor_copy(slot4[h][:], slots[:, ds(pair * (2 * K), 2 * K)]).then_inc(slot4_set, 1)
                pool.wait_ge(slot4_set, pair + 1)
                hold(pool, held)
                for b in range(2):
                    for k in range(K):
                        n = b * K + k
                        pool.indirect_dma_start(
                            yk[2 * h + b][:, k], None, y_dram,
                            bass.IndirectOffsetOnAxis(ap=slot4[h][:, n:n + 1].bitcast(U32), axis=0))\
                            .then_inc(y_in[2 * h + b], 16)

            def deviation(pair, h):
                pool.wait_ge(var_ready, pair * 2 + 2)
                hold(pool, held)
                for b in range(2 * h, 2 * h + 2):
                    last = pool.tensor_tensor(rstd[:, b:b + 1], veps[:, b:b + 1], neg_half[:], ALU.pow)
                last.then_inc(rstd_ready, 1)

            pool.tensor_copy(slot4[0][:], slots[:, 0:2 * K]).then_inc(slot4_set, 1)
            pool.wait_ge(slot4_set, 1)
            for b in range(2):
                for k in range(K):
                    n = b * K + k
                    pool.indirect_dma_start(
                        yk[b][:, k], None, y_dram,
                        bass.IndirectOffsetOnAxis(ap=slot4[0][:, n:n + 1].bitcast(U32), axis=0))\
                        .then_inc(y_in[b], 16)
            with pool.Fori(0, NT // NB - 1) as i:
                for h in range(2):
                    gather(i * 2 + (h + 1), 1 - h)
                    deviation(i * 2 + h, h)
            gather(PAIRS - 1, 1)
            deviation(PAIRS - 2, 0)
            deviation(PAIRS - 1, 1)

        @block.vector
        def _(dve):
            dve.sem_inc(y_used, 1)
            for b in range(NB):
                dve.sem_inc(out_stored[b], 1)
            PER_PAIR = 2 * K + 4

            def sums(pair, h, i):
                at = pair * PER_PAIR
                for k in range(K):
                    for b in range(2):
                        bb = 2 * h + b
                        if k == 0:
                            dve.wait_ge(y_in[bb], i * (16 * K) + 16 * K)
                            so_far = acc[:, ds(pair * (2 * C) + b * C, C)]
                        else:
                            dve.wait_ge(chain, at + (2 * (k - 1) + b + 1))
                            so_far = total[:, bb]
                        dve.scalar_tensor_tensor(
                            out=total[:, bb], in0=yk[bb][:, k], scalar=best[:, ds(pair * (2 * K) + (b * K + k), 1)],
                            in1=so_far, op0=ALU.mult, op1=ALU.add).then_inc(chain, 1)
                dve.sem_inc(y_used, 1)
                for b in range(2):
                    bb = 2 * h + b
                    dve.wait_ge(chain, at + (2 * (K - 1) + b + 1))
                    dve.bn_stats(stats[:, bb], total[:, bb]).then_inc(chain, 1)
                for b in range(2):
                    bb = 2 * h + b
                    dve.wait_ge(chain, at + (2 * K + b + 1))
                    hold(dve, held)
                    dve.bn_aggr(mv[:, bb], stats[:, bb]).then_inc(chain, 1)
                for b in range(2):
                    bb = 2 * h + b
                    dve.wait_ge(chain, at + (2 * K + 2 + b + 1))
                    dve.tensor_scalar(veps[:, bb:bb + 1], mv[:, bb, 1:2], LN_EPS, None,
                                      ALU.add).then_inc(var_ready, 1)
                    dve.tensor_scalar(negmean[:, bb:bb + 1], mv[:, bb, 0:1], -1.0, None,
                                      ALU.mult).then_inc(mean_ready, 1)

            def finish(pair, h, i):
                dve.wait_ge(rstd_ready, pair + 1)
                for b in range(2):
                    bb = 2 * h + b
                    dve.wait_ge(centred_done, pair * 2 + (b + 1))
                    dve.wait_ge(out_stored[bb], i * 16 + 1)
                    dve.scalar_tensor_tensor(out=o[:, bb], in0=centred[:, bb], scalar=rstd[:, bb:bb + 1],
                                             in1=x1[:, ds(pair * (2 * C) + b * C, C)], op0=ALU.mult,
                                             op1=ALU.add).then_inc(out_ready, 1)

            sums(0, 0, 0)
            with dve.Fori(0, NT // NB - 1) as i:
                for h in range(2):
                    sums(i * 2 + (h + 1), 1 - h, i + h)
                    finish(i * 2 + h, h, i)
            sums(PAIRS - 1, 1, NT // NB - 1)
            finish(PAIRS - 2, 0, NT // NB - 1)
            finish(PAIRS - 1, 1, NT // NB - 1)

        @block.scalar
        def _(act):
            act.sem_inc(out_ready, NB)
            with act.Fori(0, NT // NB) as i:
                for b in range(NB):
                    act.wait_ge(mean_ready, i * NB + (b + 1))
                    act.wait_ge(out_ready, i * NB + (b + 1))
                    act.activation(centred[:, b], total[:, b], ACT.Identity, bias=negmean[:, b:b + 1])\
                        .then_inc(centred_done, 1)

        @block.sync
        def _(sp):
            with sp.Fori(0, NT // NB) as i:
                row = [sp.snap(i * (NB * P) + b * P) for b in range(NB)]
                for b in range(NB):
                    sp.wait_ge(out_ready, i * NB + (b + 1 + NB))
                    sp.dma_start(out_dram[ds(row[b], P), :], o[:, b]).then_inc(out_stored[b], 16)
            for b in range(NB):
                sp.wait_ge(out_stored[b], 16 * NT // NB + 1)


def sandwich(nc, a, out):
    x_rows = a["x"]
    ctx_dram = nc.dram_tensor("ctx_scratch", [C, T], F32).ap()
    tokens_dram = nc.dram_tensor("tokens_scratch", [T, C], F32).ap()
    ids_dram = nc.dram_tensor("ids_scratch", [SLOTS + P, 1], I32).ap()
    y_dram = nc.dram_tensor("y_scratch", [SLOTS + P, C], F32).ap()
    with ExitStack() as ctx:
        m = Mem(nc, ctx)
        ident, neg_half = m.sb("ident", [P, P]), m.sb("neg_half", [P, 1])
        with ExitStack() as part:
            xnT = Mem(nc, part).sb("xnT", [P, KC, T])
            norm_and_transpose(nc, x_rows, a["identity"], ident, neg_half, xnT)
            attention(nc, a["wq_t"], a["wk_t"], a["wv_t"], a["rope_cos"], a["rope_sin"], a["rope_rotate"],
                      ctx_dram, ident, xnT)
        x1, acc = m.sb("x1", [P, NT * C]), m.sb("acc", [P, NT * C])
        best, slots = m.sb("best", [P, NT * K]), m.sb("slots", [P, NT * K], I32)
        shared_gate = m.sb("shared_gate", [P, NT])
        with ExitStack() as part:
            xfT = Mem(nc, part).sb("xfT", [P, 2, KC, T], F32R)
            logits = Mem(nc, part).sb("logits", [P, NT * (E + 1)])
            layer_norms(nc, x_rows, ctx_dram, a["wo_t"], a["w_norm"], a["w_router"], a["w_shared_gate"],
                        tokens_dram, ident, neg_half, x1, acc, xfT, logits)
            route(nc, a["before"], logits, best, slots, shared_gate)
            shared_expert(nc, a["sw_gate"], a["sw_up"], a["sw_down"], ids_dram, y_dram, xfT, slots,
                          shared_gate, acc)
        experts(nc, a["w_gate"], a["w_up"], a["w_down"], tokens_dram, ids_dram, y_dram, ident)
        combine(nc, y_dram, out, x1, acc, best, slots, neg_half)


def shape_constants():
    import numpy as np

    f32 = np.float32
    inv_freq = (f32(1.0) / f32(10000.0) ** (np.arange(0, D, 2, dtype=f32) / f32(D))).astype(f32)
    freqs = np.outer(np.arange(T, dtype=f32), inv_freq).astype(f32)
    angles = np.concatenate([freqs, freqs], axis=-1).T
    rotate = np.zeros((P, P), f32)
    for j in range(HG):
        for d in range(D // 2):
            rotate[j * D + d + D // 2, j * D + d] = -1.0
            rotate[j * D + d, j * D + d + D // 2] = 1.0
    return {
        "identity": np.eye(P, dtype=f32),
        "rope_cos": np.ascontiguousarray(np.tile(np.cos(angles), (HG, 1))),
        "rope_sin": np.ascontiguousarray(np.tile(np.sin(angles), (HG, 1))),
        "rope_rotate": rotate,
        "before": np.triu(np.ones((P, P), f32), 1),
    }


def kernel(**inputs):
    import numpy as np
    import concourse.bacc as bacc
    from concourse.bass_utils import run_bass_kernel_spmd

    def plain(name):
        return np.ascontiguousarray(inputs[name])

    def turned(name):
        return np.ascontiguousarray(np.asarray(inputs[name]).T)

    arrays = {
        "x": plain("L0_attn_x").reshape(T, C),
        "wq_t": turned("L0_attn_w_q"), "wk_t": turned("L0_attn_w_k"),
        "wv_t": turned("L0_attn_w_v"), "wo_t": turned("L0_attn_w_o"),
        "w_norm": plain("L0_ffn_w_norm").reshape(1, C),
        "w_router": plain("L0_ffn_w_router"),
        "w_shared_gate": plain("L0_ffn_w_shared_gate"),
        "w_gate": plain("L0_ffn_w_gate").reshape(E * C, F),
        "w_up": plain("L0_ffn_w_up").reshape(E * C, F),
        "w_down": plain("L0_ffn_w_down").reshape(E * F, C),
        "sw_gate": plain("L0_ffn_sw_gate"), "sw_up": plain("L0_ffn_sw_up"), "sw_down": plain("L0_ffn_sw_down"),
        **shape_constants(),
    }
    nc = bacc.Bacc("TRN2", target_bir_lowering=False, num_devices=1)
    handles = {n: nc.dram_tensor(f"in_{n}", v.shape, mybir.dt.from_np(v.dtype), kind="ExternalInput").ap()
               for n, v in arrays.items()}
    out = nc.dram_tensor("out", (T, C), F32, kind="ExternalOutput").ap()
    sandwich(nc, handles, out)
    r = run_bass_kernel_spmd(nc, [{f"in_{n}": v for n, v in arrays.items()}], core_ids=[0])
    return r.results[0]["out"].reshape(1, T, C)
```

```python
from contextlib import ExitStack

import concourse.bass as bass
from concourse import mybir

P = 128
F32 = mybir.dt.float32
F32R = mybir.dt.float32r
BF16 = mybir.dt.bfloat16
I32 = mybir.dt.int32
U32 = mybir.dt.uint32
ALU = mybir.AluOpType
ACT = mybir.ActivationFunctionType
AX = mybir.AxisListType
ds = bass.ds

T, C = 2048, 512
NT, KC = T // P, C // P
H, D = 16, 32
HG = P // D
NG = H // HG
QC = 512
NQ = T // QC
QT = QC // P
HALF = 64
BIG = -1.0e30
LN_EPS, RMS_EPS = 1e-5, 1e-6
E, K, F, CAP = 32, 4, 352, 256
FS = 1408
NFS = FS // P
FT = [(0, 128), (128, 128), (256, 96)]
SLOTS = E * CAP
ST = CAP // P
PRODUCTS = ((0, 0), (0, 1), (1, 0))


class Chain:

    def __init__(self, eng, sem, base=0):
        self.eng, self.sem, self.base, self.n = eng, sem, base, 0

    def link(self, ins):
        ins.then_inc(self.sem, 1)
        self.n += 1
        self.eng.wait_ge(self.sem, self.base + self.n)

    def done(self, per):
        assert self.n == per, (self.n, per)


def hold(eng, held):
    eng.sem_inc(held, 1)


class Mem:

    def __init__(self, nc, ctx):
        self.nc, self.ctx = nc, ctx

    def sb(self, name, shape, dt=F32):
        return self.ctx.enter_context(self.nc.sbuf_tensor(name, shape, dt))

    def ps(self, name, shape, dt=F32):
        return self.ctx.enter_context(self.nc.psum_tensor(name, shape, dt))

    def sem(self, name):
        return self.ctx.enter_context(self.nc.semaphore(name))


def staggered(n, *steps):
    for at in range(n + len(steps) - 1):
        for lag, step in enumerate(steps):
            if 0 <= at - lag < n:
                step(at - lag)


def norm_and_transpose(nc, x_dram, identity_dram, tables, ident, neg_half, xnT):
    NB = 4
    with ExitStack() as ctx:
        m = Mem(nc, ctx)
        xt, xn = m.sb("a_x", [P, NB, C]), m.sb("a_xn", [P, NB, C])
        stats, mv = m.sb("a_stats", [P, NB, 6]), m.sb("a_mean_var", [P, NB, 2])
        veps, rstd = m.sb("a_var_eps", [P, NB]), m.sb("a_rstd", [P, NB])
        held = m.sem("a_held")
        tp = m.ps("a_tp", [P, NB, KC, P])
        ident_ready, consts_ready, tables_in = m.sem("a_ident_ready"), m.sem("a_consts_ready"), m.sem("a_tables_in")
        x_ready = [m.sem(f"a_x_ready{b}") for b in range(NB)]
        xn_done = m.sem("a_xn_done")
        stats_done, mv_done = m.sem("a_stats_done"), m.sem("a_mv_done")
        var_ready, rstd_ready = m.sem("a_var_ready"), m.sem("a_rstd_ready")
        tp_ready = m.sem("a_tp_ready")
        tp_copied = m.sem("a_tp_copied")
        block = ctx.enter_context(nc.Block())

        @block.sync
        def _(sp):
            with sp.Fori(0, NT // NB) as i:
                row = [sp.snap(i * (NB * P) + b * P) for b in range(NB)]
                for b in range(NB):
                    sp.wait_ge(xn_done, i * NB + (b + 1))
                    sp.dma_start(xt[:, b], x_dram[ds(row[b], P), :]).then_inc(x_ready[b], 16)
            for place, table in tables:
                sp.dma_start(place, table).then_inc(tables_in, 16)
            sp.wait_ge(tables_in, 16 * len(tables))

        @block.vector
        def _(dve):
            dve.sem_inc(xn_done, NB)
            dve.memset(neg_half[:], -0.5).then_inc(consts_ready, 1)
            with dve.Fori(0, NT // NB) as i:
                def stats_of(b):
                    dve.wait_ge(x_ready[b], i * 16 + 16)
                    dve.bn_stats(stats[:, b], xt[:, b]).then_inc(stats_done, 1)

                def mean_var(b):
                    dve.wait_ge(stats_done, i * NB + (b + 1))
                    hold(dve, held)
                    dve.bn_aggr(mv[:, b], stats[:, b]).then_inc(mv_done, 1)

                def var_eps(b):
                    dve.wait_ge(mv_done, i * NB + (b + 1))
                    dve.tensor_scalar(veps[:, b:b + 1], mv[:, b, 1:2], LN_EPS, None,
                                      ALU.add).then_inc(var_ready, 1)

                def normal(b):
                    dve.wait_ge(rstd_ready, i * NB + (b + 1))
                    dve.wait_ge(tp_ready, i * NB + (b + 1))
                    dve.tensor_scalar(xn[:, b], xt[:, b], mv[:, b, 0:1], rstd[:, b:b + 1],
                                      ALU.subtract, ALU.mult).then_inc(xn_done, 1)

                staggered(NB, stats_of, mean_var, var_eps, normal)

        @block.gpsimd
        def _(pool):
            pool.wait_ge(consts_ready, 1)
            with pool.Fori(0, NT // NB) as i:
                for b in range(NB):
                    pool.wait_ge(var_ready, i * NB + (b + 1))
                    pool.tensor_tensor(rstd[:, b:b + 1], veps[:, b:b + 1], neg_half[:],
                                       ALU.pow).then_inc(rstd_ready, 1)

        @block.tensor
        def _(pe):
            pe.sem_inc(tp_ready, NB)
            pe.wait_ge(ident_ready, 16)
            with pe.Fori(0, NT // NB) as i:
                for b in range(NB):
                    pe.wait_ge(xn_done, i * NB + (b + 1 + NB))
                    pe.wait_ge(tp_copied, i * NB + (b + 1))
                    for k in range(KC):
                        last = pe.transpose(tp[:, b, k], xn[:, b, k * P:(k + 1) * P], ident[:])
                    last.then_inc(tp_ready, 1)

        @block.scalar
        def _(act):
            act.dma_start(ident[:], identity_dram).then_inc(ident_ready, 16)
            act.sem_inc(tp_copied, NB)
            with act.Fori(0, NT // NB) as i:
                for b in range(NB):
                    act.wait_ge(tp_ready, i * NB + (b + 1 + NB))
                    act.copy(xnT[:, :, ds(i * (NB * P) + b * P, P)], tp[:, b]).then_inc(tp_copied, 1)


def interleave(pieces, steps, units, ahead, last_added, parts):
    MATMUL, FULL_PRECISION, VECTOR = 0.215 / QC, 0.86 / QC, 0.61 / QC
    TURN, ROWS = 0.3, 5.0
    order, free = [], [0.0, 0.0]
    pe = dve = 0.0
    use = 0
    maxima = [("unit", qc, n) for qc in range(1, NQ) for n in range(ahead if qc == 1 else 0, len(units[qc]))]
    turns, rows_ready = [], {}

    def unit():
        nonlocal pe, dve, use
        kind, qc, n = maxima.pop(0)
        order.append((kind, qc, n))
        w = units[qc][n][3]
        pe = max(pe, free[use % 2]) + MATMUL * w + 0.08
        dve = max(dve, pe + 0.1) + VECTOR * w
        free[use % 2] = dve + 0.1
        use += 1
        if not maxima or maxima[0][1] != qc:
            order.append(("negmax", qc))
            dve += 0.8
            turns.append((dve + 0.2, qc))

    def turn():
        nonlocal pe, dve, use
        start, qc = turns.pop(0)
        order.append(("turn", qc))
        pe = max(pe, start, free[use % 2]) + TURN
        dve = max(dve, pe) + 0.8
        free[use % 2] = dve
        rows_ready[qc] = dve + ROWS
        use += 1

    def turn_or_unit(by):
        if turns and turns[0][0] <= by:
            turn()
        elif maxima and free[use % 2] <= by:
            unit()
        else:
            return False
        return True

    for piece in pieces:
        what, qc, *at = piece
        if what == "scores" and at == [0, 0] and qc:
            while qc not in rows_ready:
                if not turn_or_unit(pe):
                    pe += 0.05
            while pe < rows_ready[qc] and maxima:
                if not turn_or_unit(pe):
                    pe += 0.05
        while turn_or_unit(pe):
            pass
        order.append(piece)
        if what == "normalise":
            dve = max(dve, pe) + 2.2
        else:
            w = QC - steps[qc][at[0]][1]
            pe += MATMUL * w + 0.03 if what == "scores" else FULL_PRECISION * w / parts[qc][at[0]] + 0.12
            if what == "values" and qc == NQ - 1 and at[0] in last_added[1:] and at[1] == 0:
                dve += 2 * VECTOR * w
    assert not maxima and not turns
    return order


def head_columns(w_dram, at):
    return w_dram.rearrange("(k p) n -> p k n", p=P)[:, :, at]


def attention(nc, wq_t, wk_t, wv_t, ctx_dram, ident, xnT, cos, sin, rotate, wq, wk, wv):
    scale = float(D) ** -0.5
    steps = [[(kt, max(0, kt - QT * qc) * P) for kt in range(QT * (qc + 1))] for qc in range(NQ)]
    n_steps = sum(map(len, steps))
    first_step = [sum(map(len, steps[:qc])) for qc in range(NQ)]
    units = [[(qt, kc, j, min(QC, (qt + 1) * P - kc * QC))
              for qt in range(QT * qc, QT * (qc + 1)) for kc in range(qc + 1) for j in range(HG)]
             for qc in range(NQ)]
    n_mx = sum(map(len, units)) + NQ
    n_rope = 2 * NQ
    rope_units = [(s, 2 * half + n) for half in range(2) for s in range(2) for n in range(2)]
    added_steps = [[] for _ in range(NQ - 2)]
    added_steps.append([i for i in range(len(steps[-2])) if i % 2])
    added_steps.append([i for i in range(len(steps[-1])) if i % 3])
    both = (slice(0, 2), slice(2, HG))
    add_heads = [(slice(0, HG), None)] * (NQ - 1) + [both]
    n_adds = [[len(added_steps[qc]) - 1 if added_steps[qc] and add_heads[qc][by] else 0 for qc in range(NQ)]
              for by in range(2)]
    n_sums = sum(1 for added in added_steps if added)
    V_AHEAD = 2 * (NT - QT - len(units[0]) // 2)
    parts = [[2 if 0 < i < len(steps[qc]) - 2 else 1 for i in range(len(steps[qc]))] for qc in range(NQ)]
    pieces = []

    def products(qc, i):
        kinds = ("values",) if i in added_steps[qc] else ("values", "sums")
        return [(kind, qc, i, part) for kind in kinds for part in range(parts[qc][i])]

    for qc in range(NQ):
        for i in range(len(steps[qc])):
            pieces += [("scores", qc, i, j) for j in range(HG)]
            if i == 1 and qc:
                pieces.insert(-HG, ("normalise", qc - 1))
            if i or qc:
                pieces += products(*((qc, i - 1) if i else (qc - 1, len(steps[qc - 1]) - 1)))
    pieces += products(NQ - 1, len(steps[-1]) - 1)
    pieces.append(("normalise", NQ - 1))
    order = interleave(pieces, steps, units, V_AHEAD, added_steps[-1], parts)
    HALF_IN = 2 * 3 * HG * 16
    M_ROW = 3 * D

    with ExitStack() as ctx:
        m = Mem(nc, ctx)
        work = m.sb("work", [P, 6, QC])
        raw, by_cos, by_sin, sums = work[:, 0:2], work[:, 2:4], work[:, 4:6], work[:, 0:HG]
        hilo = [m.sb(f"hilo_{s}", [P, 2, T], F32R) for s in "qk"]
        stack = [[m.sb(f"stack_{s}{j}", [P, T], F32R) for j in range(HG)] for s in "qk"]
        v = m.sb("v_g", [P, NT, P])
        probs = [m.sb(f"probs{b}", [P, HG, QC]) for b in range(2)]
        den_turned, rden_one, rden = m.sb("den_turned", [P, QC]), m.sb("rden_one", [P, QC // D]), m.sb("rden", [P, QC])
        ctxs = [m.sb(f"ctx{b}", [P, QC]) for b in range(2)]
        tops = m.sb("tops", [P, NT, HG, NQ])
        negmax = m.sb("negmax", [P, QT, HG])
        negmax_hi = m.sb("negmax_hi", [P, QT, HG], F32R)
        spread = m.sb("negmax_spread", [P, QT, P])
        max_rows = m.sb("max_rows", [P, QC], F32R)
        ones = m.sb("ones_d", [P, D])
        first_half = m.sb("first_half", [P, P], BF16)
        second_half = m.sb("second_half", [P, P], BF16)
        first_big = m.sb("first_big", [P, P], BF16)
        second_big = m.sb("second_big", [P, P], BF16)
        out_banks = [m.ps("pv", [P, QC]), m.ps("den", [P, QC])]
        pv, den = out_banks
        mx = m.ps("mx", [P, 2, QC])
        st = m.ps("st", [P, HG, QC])

        w_in, masks_set = m.sem("b_w_in"), m.sem("b_masks_set")
        zeros_set, held = m.sem("b_zeros_set"), m.sem("b_held")
        qk_projected, v_projected = m.sem("b_qk_projected"), m.sem("b_v_projected")
        raw_copied, v_copied = m.sem("b_raw_copied"), m.sem("b_v_copied")
        rotated, cos_done, split_done = m.sem("b_rotated"), m.sem("b_cos_done"), m.sem("b_split_done")
        added = m.sem("b_added")
        stack_in = [m.sem("b_first_half_in"), m.sem("b_second_half_in")]
        mx_ready, negmax_split = m.sem("b_mx_ready"), m.sem("b_negmax_split")
        mx_free = m.sem("b_mx_free")
        max_rows_set, max_rows_in = m.sem("b_max_rows_set"), m.sem("b_max_rows_in")
        sums_begun, den_done = m.sem("b_sums_begun"), m.sem("b_den_done")
        summed = [m.sem("b_summed_pool"), m.sem("b_summed_dve")]
        st_ready, exp_done, pv_done = m.sem("b_st_ready"), m.sem("b_exp_done"), m.sem("b_pv_done")
        ctx_ready = m.sem("b_ctx_ready")
        ctx_stored = [m.sem(f"b_ctx_stored{b}") for b in range(2)]
        chain = m.sem("b_dve_chain")
        block = ctx.enter_context(nc.Block())

        def adds(g, by, qc, n):
            return g * sum(n_adds[by]) + (sum(n_adds[by][:qc]) + n)

        def sums_of(qc):
            return sum(1 for added in added_steps[:qc] if added)

        def add_to_sums(eng, g, qc, n, by):
            i = added_steps[qc][n + 1]
            q0, s = steps[qc][i][1], first_step[qc] + i
            eng.wait_ge(exp_done, g * (2 * n_steps) + (2 * s + 2))
            if n == 0:
                eng.wait_ge(sums_begun, g * n_sums + (sums_of(qc) + 1))
            else:
                eng.wait_ge(summed[by], adds(g, by, qc, n))
            heads = add_heads[qc][by]
            own = sums[:, heads, q0:QC]
            eng.tensor_tensor(own, own, probs[s % 2][:, heads, q0:QC], ALU.add).then_inc(summed[by], 1)

        @block.sync
        def _(sp):
            with sp.Fori(0, NG) as g:
                channel, steps_before = sp.snap(g * P), sp.snap(g * n_steps)
                next_channel = sp.snap((g + 1) % NG * P)
                for half in range(2):
                    for s in range(2):
                        sp.wait_ge(split_done, g * n_rope + 2 * (2 * half + s + 1))
                        if s == 0 and half == 0:
                            hold(sp, held)
                            sp.wait_ge(pv_done, steps_before + 1)
                        cols = slice(half * T // 2, (half + 1) * T // 2)
                        for r, part in enumerate(((0, 0, 1), (0, 1, 0))[s]):
                            for j in range(HG):
                                sp.dma_start(stack[s][j][r * D:(r + 1) * D, cols].bitcast(F32),
                                             hilo[s][j * D:(j + 1) * D, part, cols].bitcast(F32))\
                                    .then_inc(stack_in[half], 16)

                def max_rows_of(qc):
                    sp.wait_ge(max_rows_set, g * NQ + (qc + 1))
                    for j in range(HG):
                        sp.dma_start(stack[0][j][M_ROW:M_ROW + 2, qc * QC:(qc + 1) * QC].bitcast(F32),
                                     max_rows[j * D:j * D + 2, :].bitcast(F32)).then_inc(max_rows_in, 16)

                max_rows_of(0)
                for qc in range(NQ):
                    if qc + 1 < NQ:
                        max_rows_of(qc + 1)
                    if qc == 0:
                        sp.wait_ge(v_projected, g * NQ + (NQ + 1))
                        hold(sp, held)
                        for w, w_dram in ((wq, wq_t), (wk, wk_t), (wv, wv_t)):
                            sp.dma_start(w[:], head_columns(w_dram, ds(next_channel, P))).then_inc(w_in, 16)
                    sp.wait_ge(ctx_ready, g * NQ + (qc + 2))
                    sp.dma_start(ctx_dram[ds(channel, P), qc * QC:(qc + 1) * QC],
                                 ctxs[qc % 2][:]).then_inc(ctx_stored[qc % 2], 16)
            sp.wait_ge(w_in, 48 * NG + 1)
            for b in range(2):
                sp.wait_ge(ctx_stored[b], 16 * NG * NQ // 2 + 1)

        @block.gpsimd
        def _(pool):
            setup = Chain(pool, masks_set)
            for t in (first_half, second_half, first_big, second_big):
                setup.link(pool.memset(t[:], 0.0))
            setup.link(pool.memset(ones[:], 1.0))
            setup.link(pool.memset(first_half[0:1, 0:HALF], 1.0))
            setup.link(pool.memset(second_half[0:1, HALF:P], 1.0))
            setup.link(pool.memset(first_big[0:1, 0:HALF], BIG))
            setup.link(pool.memset(second_big[0:1, HALF:P], BIG))
            for j in range(HG):
                setup.link(pool.memset(stack[1][j][M_ROW:P, :].bitcast(F32), 1.0))
            with pool.Fori(0, NG) as g:
                for u in range(n_rope):
                    b, tc = u % 2, rope_units[u][1]
                    pool.wait_ge(raw_copied, g * n_rope + (u + 1))
                    if u >= 2:
                        pool.wait_ge(added, g * n_rope + (u - 1))
                    pool.tensor_tensor(by_cos[:, b], raw[:, b], cos[:, tc * QC:(tc + 1) * QC],
                                       ALU.mult).then_inc(cos_done, 1)
                for qc in range(NQ):
                    for n in range(n_adds[0][qc]):
                        add_to_sums(pool, g, qc, n, 0)

        @block.tensor
        def _(pe):
            with pe.Fori(0, NG) as g:
                def project(u):
                    s, tc = rope_units[u]
                    if u >= 2:
                        pe.wait_ge(raw_copied, g * n_rope + (u - 1))
                    for k in range(KC):
                        last = pe.matmul(mx[:, u % 2], (wq, wk)[s][:, k], xnT[:, k, tc * QC:(tc + 1) * QC],
                                         start=(k == 0), stop=(k == KC - 1))
                    last.then_inc(qk_projected, 1)

                def rotate_pairs(u):
                    pe.wait_ge(raw_copied, g * n_rope + (u + 1))
                    if u >= 2:
                        pe.wait_ge(split_done, g * n_rope + (u - 1))
                    pe.matmul(st[:, u % 2], rotate[:], raw[:, u % 2], start=True, stop=True)\
                        .then_inc(rotated, 1)

                def project_v(tile):
                    n, t = divmod(tile, QT)
                    if n >= 2 and t == 0:
                        pe.wait_ge(v_copied, g * NQ + (n - 1))
                    for k in range(KC):
                        last = pe.matmul(out_banks[n % 2][:, t * P:(t + 1) * P], xnT[:, k, tile * P:(tile + 1) * P],
                                         wv[:, k], start=(k == 0), stop=(k == KC - 1))
                    if t == QT - 1:
                        last.then_inc(v_projected, 1)

                def max_unit(qc, n, use):
                    qt, kc, j, w = units[qc][n]
                    pe.wait_ge(mx_free, g * n_mx + (use + 1))
                    diagonal = (qt + 1) * P <= (kc + 1) * QC
                    last = pe.matmul(mx[:, use % 2, 0:w], stack[0][j][0:M_ROW, qt * P:(qt + 1) * P],
                                     stack[1][j][0:M_ROW, kc * QC:kc * QC + w], start=True, stop=not diagonal)
                    if diagonal:
                        last = pe.matmul(mx[:, use % 2, w - P:w], first_half[:], second_big[:],
                                         start=False, stop=True)
                    last.then_inc(mx_ready, 1)

                def turn_max(qc, use):
                    pe.wait_ge(mx_free, g * n_mx + (use + 1))
                    pe.wait_ge(negmax_split, g * NQ + (qc + 1))
                    for t in range(QT):
                        last = pe.transpose(mx[:, use % 2, t * P:(t + 1) * P], spread[:, t], ident[:])
                    last.then_inc(mx_ready, 1)

                def scores(qc, i, j):
                    kt, q0 = steps[qc][i]
                    s = first_step[qc] + i
                    diagonal = kt >= QT * qc
                    if i == 0 and j == 0:
                        pe.wait_ge(max_rows_in, g * (64 * NQ) + (64 * (qc + 1) + 1))
                    if s and j % 2 == 0:
                        pe.wait_ge(exp_done, g * (2 * n_steps) + (2 * s + j // 2 - 1))
                    last = pe.matmul(st[:, j, q0:QC], stack[1][j][0:M_ROW + 2, kt * P:(kt + 1) * P],
                                     stack[0][j][0:M_ROW + 2, qc * QC + q0:(qc + 1) * QC],
                                     start=True, stop=not diagonal)
                    if diagonal:
                        last = pe.matmul(st[:, j, q0:q0 + P], second_half[:], first_big[:],
                                         start=False, stop=True)
                    if j % 2:
                        last.then_inc(st_ready, 1)

                def part_of(qc, i, part):
                    q0, n = steps[qc][i][1], parts[qc][i]
                    return slice(q0 + part * (QC - q0) // n, q0 + (part + 1) * (QC - q0) // n)

                def weigh_values(qc, i, part):
                    kt, cols = steps[qc][i][0], part_of(qc, i, part)
                    s = first_step[qc] + i
                    pe.wait_ge(exp_done, g * (2 * n_steps) + (2 * s + 2))
                    if i == 0 and part == 0:
                        pe.wait_ge(ctx_ready, g * NQ + (qc + 1))
                    for j in range(HG):
                        last = pe.matmul(pv[j * D:(j + 1) * D, cols], v[:, kt, j * D:(j + 1) * D],
                                         probs[s % 2][:, j, cols], start=(i == 0), stop=(i == len(steps[qc]) - 1))
                    if i in added_steps[qc] and part == parts[qc][i] - 1:
                        last.then_inc(pv_done, 1)

                def sum_probs(qc, i, part):
                    cols = part_of(qc, i, part)
                    s = first_step[qc] + i
                    for j in range(HG):
                        last = pe.matmul(den[j * D:(j + 1) * D, cols], ones[:], probs[s % 2][:, j, cols],
                                         start=(i == 0),
                                         stop=(i == len(steps[qc]) - 1 and not added_steps[qc]))
                    if part == parts[qc][i] - 1:
                        last.then_inc(pv_done, 1)

                def sum_the_sums(qc):
                    for by in range(2):
                        if n_adds[by][qc]:
                            pe.wait_ge(summed[by], adds(g, by, qc, n_adds[by][qc]))
                    q0 = steps[qc][added_steps[qc][0]][1]
                    for j in range(HG):
                        last = pe.matmul(den[j * D:(j + 1) * D, q0:QC], ones[:], sums[:, j, q0:QC],
                                         start=False, stop=True)
                    last.then_inc(den_done, 1)

                pe.wait_ge(w_in, g * 48 + 1)
                pe.wait_ge(mx_free, g * n_mx + 2)
                project(0)
                for u in range(1, n_rope):
                    project(u)
                    rotate_pairs(u - 1)
                rotate_pairs(n_rope - 1)
                pe.wait_ge(ctx_ready, g * NQ + 1)
                v_tile = 0
                while v_tile < QT:
                    project_v(v_tile)
                    v_tile += 1
                pe.wait_ge(stack_in[0], g * HALF_IN + (HALF_IN + 1))
                pe.wait_ge(masks_set, 9 + HG)
                use = 0
                for n in range(len(units[0])):
                    max_unit(0, n, use)
                    use += 1
                    if n % 2:
                        project_v(v_tile)
                        v_tile += 1
                turn_max(0, use)
                use += 1
                ahead = 0
                while v_tile < NT:
                    project_v(v_tile)
                    v_tile += 1
                    for _ in range(2):
                        max_unit(1, ahead, use)
                        ahead, use = ahead + 1, use + 1
                pe.wait_ge(v_copied, g * NQ + NQ)
                assert ahead == V_AHEAD
                for what, qc, *at in order:
                    if what == "scores":
                        scores(qc, *at)
                    elif what == "values":
                        weigh_values(qc, *at)
                    elif what == "sums":
                        sum_probs(qc, *at)
                    elif what == "normalise":
                        if added_steps[qc]:
                            sum_the_sums(qc)
                    elif what == "turn":
                        turn_max(qc, use)
                        use += 1
                    elif what == "unit":
                        if (qc, *at) == (2, 0):
                            pe.wait_ge(stack_in[1], g * HALF_IN + (HALF_IN + 1))
                        max_unit(qc, *at, use)
                        use += 1
                assert use == n_mx

        @block.scalar
        def _(act):
            with act.Fori(0, NG) as g:
                for u in range(n_rope):
                    act.wait_ge(qk_projected, g * n_rope + (u + 1))
                    if u >= 2:
                        act.wait_ge(rotated, g * n_rope + (u - 1))
                        act.wait_ge(cos_done, g * n_rope + (u - 1))
                    act.copy(raw[:, u % 2], mx[:, u % 2]).then_inc(raw_copied, 1)
                for n in range(NQ):
                    act.wait_ge(v_projected, g * NQ + (n + 2))
                    act.copy(v[:, n * QT:(n + 1) * QT, :],
                             out_banks[n % 2][:].rearrange("p (t c) -> p t c", t=QT)).then_inc(v_copied, 1)
                for qc in range(NQ):
                    for i, (kt, q0) in enumerate(steps[qc]):
                        s = first_step[qc] + i
                        for pair in range(2):
                            heads = slice(2 * pair, 2 * pair + 2)
                            act.wait_ge(st_ready, g * (2 * n_steps) + (2 * s + pair + 1))
                            if s >= 2:
                                act.wait_ge(pv_done, g * n_steps + s)
                                in_chunk = max(n for n in range(NQ) if first_step[n] <= s - 2)
                                was = s - 2 - first_step[in_chunk]
                                if was in added_steps[in_chunk][1:]:
                                    for by in range(2):
                                        if n_adds[by][in_chunk]:
                                            act.wait_ge(summed[by],
                                                        adds(g, by, in_chunk, added_steps[in_chunk].index(was)))
                            act.activation(probs[s % 2][:, heads, q0:QC], st[:, heads, q0:QC], ACT.Exp,
                                           scale=scale).then_inc(exp_done, 1)
                        if i in added_steps[qc][:1]:
                            if sums_of(qc) == 0:
                                act.wait_ge(split_done, g * n_rope + n_rope)
                            else:
                                act.wait_ge(den_done, g * n_sums + sums_of(qc))
                            act.wait_ge(exp_done, g * (2 * n_steps) + (2 * s + 2))
                            act.copy(sums[:, :, q0:QC], probs[s % 2][:, :, q0:QC]).then_inc(sums_begun, 1)

        @block.vector
        def _(dve):
            dve.memset(tops[:], -3.0e38).then_inc(zeros_set, 1)
            dve.memset(spread[:], 0.0).then_inc(zeros_set, 1)
            dve.wait_ge(zeros_set, 2)
            dve.sem_inc(mx_free, 2)
            for started in (w_in, v_projected, pv_done, ctx_ready, max_rows_in, *stack_in, *ctx_stored):
                dve.sem_inc(started, 1)
            per = 2 * n_rope + 5 * NQ
            with dve.Fori(0, NG) as g:
                c = Chain(dve, chain, g * per)
                for u in range(n_rope):
                    b, (s, tc) = u % 2, rope_units[u]
                    cols = slice(tc * QC, (tc + 1) * QC)
                    dve.wait_ge(rotated, g * n_rope + (u + 1))
                    c.link(dve.tensor_tensor(by_sin[:, b], st[:, b], sin[:, cols], ALU.mult))
                    dve.wait_ge(cos_done, g * n_rope + (u + 1))
                    dve.tensor_tensor(by_sin[:, b], by_sin[:, b], by_cos[:, b], ALU.add).then_inc(added, 1)
                    dve.wait_ge(added, g * n_rope + (u + 1))
                    dve.wait_ge(stack_in[tc // 2], g * HALF_IN + 1)
                    c.link(dve.tensor_copy(hilo[s][:, 0, cols], by_sin[:, b]))
                    dve.tensor_tensor(hilo[s][:, 1, cols], by_sin[:, b], hilo[s][:, 0, cols].bitcast(F32),
                                      ALU.subtract).then_inc(split_done, 1)

                state = {"use": 0}

                def max_of_unit(qc, n):
                    qt, kc, j, w = units[qc][n]
                    dve.wait_ge(mx_ready, g * n_mx + (state["use"] + 1))
                    dve.tensor_reduce(tops[:, qt, j, kc:kc + 1], mx[:, state["use"] % 2, 0:w], AX.X,
                                      ALU.max).then_inc(mx_free, 1)
                    state["use"] += 1

                def negate_and_split(qc):
                    dve.wait_ge(mx_free, g * n_mx + (state["use"] + 2))
                    lo_hi = spread[:].rearrange("p t (j r) -> p t j r", r=D)
                    c.link(dve.tensor_reduce(negmax[:], tops[:, QT * qc:QT * (qc + 1)], AX.X, ALU.max,
                                             negate=True))
                    c.link(dve.tensor_copy(negmax_hi[:], negmax[:]))
                    dve.tensor_copy(lo_hi[:, :, :, 0], negmax_hi[:].bitcast(F32))
                    dve.tensor_tensor(lo_hi[:, :, :, 1], negmax[:], negmax_hi[:].bitcast(F32),
                                      ALU.subtract).then_inc(negmax_split, 1)

                def max_to_rows(qc):
                    dve.wait_ge(mx_ready, g * n_mx + (state["use"] + 1))
                    dve.wait_ge(max_rows_in, g * (64 * NQ) + (64 * qc + 1))
                    dve.tensor_copy(max_rows[:], mx[:, state["use"] % 2]).then_inc(mx_free, 1)
                    dve.wait_ge(mx_free, g * n_mx + (state["use"] + 3))
                    dve.sem_inc(max_rows_set, 1)
                    state["use"] += 1

                def normalise(qc):
                    if added_steps[qc]:
                        dve.wait_ge(den_done, g * n_sums + (sums_of(qc) + 1))
                    else:
                        dve.wait_ge(pv_done, g * n_steps + (first_step[qc] + len(steps[qc]) + 1))
                    c.link(dve.transpose(den_turned[:], den[:]))
                    c.link(dve.reciprocal(rden_one[:], den_turned[:].rearrange("p (b c) -> p b c", c=D)[:, :, 0]))
                    c.link(dve.transpose(rden[:], rden_one[:].rearrange("p (b o) -> p b o", o=1)
                                         .to_broadcast([P, QC // D, D])))
                    dve.wait_ge(ctx_stored[qc % 2], g * (16 * NQ // 2) + (16 * (qc // 2) + 1))
                    dve.tensor_tensor(ctxs[qc % 2][:], pv[:], rden[:], ALU.mult).then_inc(ctx_ready, 1)

                for n in range(len(units[0])):
                    max_of_unit(0, n)
                negate_and_split(0)
                max_to_rows(0)
                for n in range(V_AHEAD):
                    max_of_unit(1, n)
                for what, qc, *at in order:
                    if what == "unit":
                        max_of_unit(qc, *at)
                    elif what == "negmax":
                        negate_and_split(qc)
                    elif what == "turn":
                        max_to_rows(qc)
                    elif what == "values" and at[1] == 0 and n_adds[1][qc] and at[0] in added_steps[qc][1:]:
                        add_to_sums(dve, g, qc, added_steps[qc].index(at[0]) - 1, 1)
                    elif what == "normalise":
                        normalise(qc)
                c.done(per)


def layer_norms(nc, x_dram, ctx_dram, wo_t, w_norm_row, w_router, w_shared_gate, tokens_dram,
                ident, neg_half, x1, acc, xfT, logits):
    NB = 4
    TURNS = NT // NB
    with ExitStack() as ctx:
        m = Mem(nc, ctx)
        ct, xt = m.sb("c_ctx", [P, NB, NG, P]), m.sb("c_x", [P, NB, C])
        wo = m.sb("c_wo", [P, KC, C])
        w_norm = m.sb("c_w_norm", [P, C])
        wr = m.sb("c_w_router", [P, KC, E + 1])
        sq = m.sb("c_sq", [P, 2, C])
        x1s = xf = m.sb("c_x1s_xf", [P, NB, C])
        o_centred = h = m.sb("c_o_centred_h", [P, NB, C])
        xft = m.sb("c_xft", [P, NB, KC, P])
        stats, mv = m.sb("c_stats", [P, NB, 6]), m.sb("c_mv", [P, NB, 2])
        negmean = m.sb("c_negmean", [P, NB])
        veps, rstd = m.sb("c_veps", [P, NB]), m.sb("c_rstd", [P, NB])
        mean_sq = m.sb("c_mean_sq", [P, NB])
        held = m.sem("c_held")
        ob, tp, lg = m.ps("c_o", [P, NB, C]), m.ps("c_tp", [P, 2, KC, P]), m.ps("c_lg", [P, 2, 512])
        wo_in, w_in = m.sem("c_wo_in"), m.sem("c_w_in")
        ctx_in, x_in = ([m.sem(f"c_{n}_in{b}") for b in range(NB)] for n in ("ctx", "x"))
        o_ready = m.sem("c_o_ready")
        negmean_done = m.sem("c_negmean_done")
        o_centred_done = m.sem("c_o_centred_done")
        x1_done = m.sem("c_x1_done")
        x1_kept = m.sem("c_x1_kept")
        h_kept = m.sem("c_h_kept")
        h_done, sq_done = m.sem("c_h_done"), m.sem("c_sq_done")
        stats_done, mv_done = m.sem("c_stats_done"), m.sem("c_mv_done")
        var_ready, rstd_ready = m.sem("c_var_ready"), m.sem("c_rstd_ready")
        xf_done = m.sem("c_xf_done")
        xf_stored = [m.sem(f"c_xf_stored{b}") for b in range(NB)]
        turned = m.sem("c_turned")
        turn_copied = m.sem("c_turn_copied")
        xft_kept = m.sem("c_xft_kept")
        lg_ready = m.sem("c_lg_ready")
        lg_copied = m.sem("c_lg_copied")
        block = ctx.enter_context(nc.Block())
        wr_dram = w_router.rearrange("(k p) e -> p k e", p=P)

        @block.sync
        def _(sp):
            with sp.Fori(0, TURNS) as i:
                row = [sp.snap(i * (NB * P) + b * P) for b in range(NB)]
                for b in range(NB):
                    sp.wait_ge(o_ready, i * NB + (b + 1))
                    sp.dma_start(ct[:, b], ctx_dram.rearrange("(g p) t -> p g t", p=P)[:, :, ds(row[b], P)])\
                        .then_inc(ctx_in[b], 16)
                for b in range(NB):
                    sp.wait_ge(x1_done, i * NB + (b + 1))
                    sp.dma_start(xt[:, b], x_dram[ds(row[b], P), :]).then_inc(x_in[b], 16)

        @block.tensor
        def _(pe):
            pe.sem_inc(o_ready, NB)
            pe.sem_inc(turned, NB)
            pe.sem_inc(lg_ready, NB)
            pe.wait_ge(wo_in, 16)

            def project(i):
                for b in range(NB):
                    pe.wait_ge(ctx_in[b], i * 16 + 16)
                    pe.wait_ge(o_centred_done, i * NB + (b + 1))
                    for k in range(KC):
                        last = pe.matmul(ob[:, b], ct[:, b, k], wo[:, k], start=(k == 0), stop=(k == KC - 1))
                    last.then_inc(o_ready, 1)

            def turn_and_route(i):
                pe.wait_ge(w_in, 48)
                for b in range(NB):
                    pe.wait_ge(xf_done, i * NB + (b + 1))
                    pe.wait_ge(turn_copied, i * NB + (b + 1))
                    for k in range(KC):
                        last = pe.transpose(tp[:, b % 2, k], xf[:, b, k * P:(k + 1) * P], ident[:])
                    last.then_inc(turned, 1)
                for b in range(NB):
                    pe.wait_ge(turn_copied, i * NB + (b + 3))
                    pe.wait_ge(lg_copied, i * NB + (b + 1))
                    for k in range(KC):
                        last = pe.matmul(lg[:, b % 2, 0:E + 1], xft[:, b, k], wr[:, k],
                                         start=(k == 0), stop=(k == KC - 1))
                    last.then_inc(lg_ready, 1)

            project(0)
            with pe.Fori(0, TURNS - 1) as i:
                project(i + 1)
                turn_and_route(i)
            turn_and_route(TURNS - 1)

        @block.scalar
        def _(act):
            act.dma_start(wo[:], wo_t.rearrange("(k p) n -> p k n", p=P)).then_inc(wo_in, 16)
            act.dma_start(w_norm[:], w_norm_row.to_broadcast([P, C])).then_inc(w_in, 16)
            act.dma_start(wr[:, :, 0:E], wr_dram).then_inc(w_in, 16)
            act.dma_start(wr[:, :, E:E + 1], w_shared_gate.rearrange("(k p) e -> p k e", p=P),
                          allow_slow_non_contiguous=True).then_inc(w_in, 16)
            act.sem_inc(turn_copied, 2)
            act.sem_inc(lg_copied, 2)
            act.sem_inc(o_centred_done, NB)
            act.sem_inc(h_kept, NB)

            def centre(i):
                for b in range(NB):
                    act.wait_ge(negmean_done, i * NB + (b + 1))
                    act.wait_ge(x1_done, i * NB + (b + 1))
                    act.wait_ge(h_kept, i * NB + (b + 1))
                    act.activation(o_centred[:, b], ob[:, b], ACT.Identity, bias=negmean[:, b:b + 1])\
                        .then_inc(o_centred_done, 1)

            def keep(i, row, last=False):
                for b in range(NB):
                    act.wait_ge(x1_done, i * NB + (b + 1 + NB))
                    hold(act, held)
                    act.copy(x1[:, ds(i * (NB * C) + b * C, C)], x1s[:, b]).then_inc(x1_kept, 1)
                for b in range(NB):
                    act.wait_ge(h_done, i * NB + (b + 1))
                    hold(act, held)
                    act.copy(acc[:, ds(i * (NB * C) + b * C, C)], h[:, b]).then_inc(h_kept, 1)
                for b in range(NB):
                    act.wait_ge(xf_done, i * NB + (b + 1))
                    act.dma_start(tokens_dram[ds(row[b], P), :], xf[:, b]).then_inc(xf_stored[b], 16)
                if not last:
                    centre(i + 1)
                for b in range(NB):
                    act.wait_ge(turned, i * NB + (b + 1 + NB))
                    act.wait_ge(lg_ready, i * NB + (b + 1))
                    act.wait_ge(xft_kept, i * NB + (b + 1))
                    act.copy(xft[:, b], tp[:, b % 2])
                    act.copy(xfT[:, 0, :, ds(i * (NB * P) + b * P, P)], tp[:, b % 2]).then_inc(turn_copied, 1)
                for b in range(NB):
                    act.wait_ge(lg_ready, i * NB + (b + 1 + NB))
                    act.copy(logits[:, ds(i * (NB * (E + 1)) + b * (E + 1), E + 1)],
                             lg[:, b % 2, 0:E + 1]).then_inc(lg_copied, 1)

            centre(0)
            with act.Fori(0, TURNS - 1) as i:
                keep(i, [act.snap(i * (NB * P) + b * P) for b in range(NB)])
            keep(TURNS - 1, [(NT - NB + b) * P for b in range(NB)], last=True)
            for b in range(NB):
                act.wait_ge(xf_stored[b], 16 * TURNS + 1)

        @block.gpsimd
        def _(pool):
            pool.sem_inc(xft_kept, NB)

            def deviation(i, phase, b):
                n = phase * NB + b
                pool.wait_ge(var_ready, i * (3 * NB) + (n + 1))
                pool.tensor_tensor(rstd[:, b:b + 1], veps[:, b:b + 1], neg_half[:], ALU.pow)\
                    .then_inc(rstd_ready, 1)

            def keep_lo(i, b):
                at = ds(i * (NB * P) + b * P, P)
                pool.wait_ge(turn_copied, i * NB + (b + 3))
                hold(pool, held)
                pool.tensor_tensor(xfT[:, 1, :, at], xft[:, b], xfT[:, 0, :, at], ALU.subtract).then_inc(xft_kept, 1)

            for phase in range(3):
                for b in range(NB):
                    deviation(0, phase, b)
            with pool.Fori(0, TURNS - 1) as i:
                for b in range(NB):
                    deviation(i + 1, 0, b)
                for b in range(NB):
                    deviation(i + 1, 1, b)
                    keep_lo(i, b)
                for b in range(NB):
                    deviation(i + 1, 2, b)
            for b in range(NB):
                keep_lo(TURNS - 1, b)

        @block.vector
        def _(dve):
            dve.sem_inc(x1_done, NB)
            for b in range(NB):
                dve.sem_inc(xf_stored[b], 1)
            dve.wait_ge(w_in, 48)
            with dve.Fori(0, TURNS) as i:
                def stats_of(ready, src):
                    def step(b):
                        dve.wait_ge(ready, i * NB + (b + 1 + NB))
                        dve.bn_stats(stats[:, b], src[:, b]).then_inc(stats_done, 1)
                    return step

                def mean_var(phase):
                    def step(b):
                        dve.wait_ge(stats_done, i * (2 * NB) + (phase * NB + b + 1))
                        hold(dve, held)
                        dve.bn_aggr(mv[:, b], stats[:, b]).then_inc(mv_done, 1)
                    return step

                def var_eps(phase):
                    def step(b):
                        dve.wait_ge(mv_done, i * (2 * NB) + (phase * NB + b + 1))
                        dve.tensor_scalar(veps[:, b:b + 1], mv[:, b, 1:2], LN_EPS, None,
                                          ALU.add).then_inc(var_ready, 1)
                        if phase == 0:
                            dve.tensor_scalar(negmean[:, b:b + 1], mv[:, b, 0:1], -1.0, None,
                                              ALU.mult).then_inc(negmean_done, 1)
                    return step

                def residual(b):
                    dve.wait_ge(rstd_ready, i * (3 * NB) + (b + 1))
                    dve.wait_ge(o_centred_done, i * NB + (b + 1 + NB))
                    dve.wait_ge(x_in[b], i * 16 + 16)
                    dve.wait_ge(turned, i * NB + (b + 1))
                    dve.wait_ge(xf_stored[b], i * 16 + 1)
                    dve.scalar_tensor_tensor(out=x1s[:, b], in0=o_centred[:, b], scalar=rstd[:, b:b + 1],
                                             in1=xt[:, b], op0=ALU.mult, op1=ALU.add).then_inc(x1_done, 1)

                def normal(b):
                    dve.wait_ge(rstd_ready, i * (3 * NB) + (b + 1 + NB))
                    dve.tensor_scalar(h[:, b], x1s[:, b], mv[:, b, 0:1], rstd[:, b:b + 1],
                                      ALU.subtract, ALU.mult).then_inc(h_done, 1)

                def square_sum(b):
                    dve.wait_ge(h_done, i * NB + (b + 1))
                    dve.tensor_tensor_reduce(sq[:, b % 2], h[:, b], h[:, b], 1.0 / C, 0.0, ALU.mult, ALU.add,
                                             mean_sq[:, b:b + 1]).then_inc(sq_done, 1)

                def rms_eps(b):
                    dve.wait_ge(sq_done, i * NB + (b + 1))
                    dve.tensor_scalar(veps[:, b:b + 1], mean_sq[:, b:b + 1], RMS_EPS, None,
                                      ALU.add).then_inc(var_ready, 1)

                staggered(NB, stats_of(o_ready, ob), mean_var(0), var_eps(0))
                staggered(NB, residual, stats_of(x1_done, x1s), mean_var(1), var_eps(1))
                staggered(NB, normal, square_sum, rms_eps)
                for b in range(NB):
                    dve.wait_ge(rstd_ready, i * (3 * NB) + (b + 1 + 2 * NB))
                    dve.wait_ge(x1_kept, i * NB + (b + 1))
                    dve.scalar_tensor_tensor(out=xf[:, b], in0=h[:, b], scalar=rstd[:, b:b + 1], in1=w_norm[:],
                                             op0=ALU.mult, op1=ALU.mult).then_inc(xf_done, 1)


def gate_and_up_products(pe, xfT, chunk, weights, banks):
    for w, bank in zip(weights, banks):
        for k in range(KC):
            for part, (of_w, of_x) in enumerate(PRODUCTS):
                last = pe.matmul(bank, w[:, of_w, k], xfT[:, of_x, k, chunk * QC:(chunk + 1) * QC],
                                 start=(k == 0 and part == 0), stop=(k == KC - 1 and part == 2))
    return last


def route(nc, before_dram, logits, best, slots, shared_gate, loads, splits, xfT, first_split, first_banks):
    with ExitStack() as ctx:
        m = Mem(nc, ctx)
        probs = m.sb("r_probs", [P, NT, E])
        rowmax, rowsum = m.sb("r_rowmax", [P, NT]), m.sb("r_rowsum", [P, NT])
        gate_e = m.sb("r_gate_e", [P, NT])
        top, top_at = m.sb("r_top", [P, NT, 8]), m.sb("r_top_at", [P, NT, 8], U32)
        expert = m.sb("r_expert", [P, NT, K])
        lane, lane_i = m.sb("r_lane", [P, NT, E]), m.sb("r_lane_i", [P, NT, E], I32)
        spare, spare_i = m.sb("r_spare", [P, 1]), m.sb("r_spare_i", [P, 1], I32)
        chosen = [m.sb(f"r_chosen{k}", [P, NT, E]) for k in range(K)]
        mask, mask_b = m.sb("r_mask", [P, NT, E]), m.sb("r_mask_b", [P, NT, E], BF16)
        before, before_b = m.sb("r_before", [P, P]), m.sb("r_before_b", [P, P], BF16)
        ones_b = m.sb("r_ones", [P, P], BF16)
        tile_sum, prefix = m.sb("r_tile_sum", [P, NT, E]), m.sb("r_prefix", [P, NT + 1, E])
        at = m.sb("r_at", [P, NT, E])
        picked = m.sb("r_picked", [P, NT, E])
        place, fits = m.sb("r_place", [P, NT, K]), m.sb("r_fits", [P, NT, K])
        slot, tile_of = m.sb("r_slot", [P, NT, K]), m.sb("r_tile_of", [P, NT, K])
        within_ps, sum_ps = m.ps("r_within", [P, NT * E]), m.ps("r_sum", [P, NT * E])
        before_in, lanes_set = m.sem("r_before_in"), m.sem("r_lanes_set")
        shifted, exp_done = m.sem("r_shifted"), m.sem("r_exp_done")
        mask_ready, counted, chain = m.sem("r_mask_ready"), m.sem("r_counted"), m.sem("r_chain")
        loaded, weights_hi, weights_split = m.sem("r_loaded"), m.sem("r_weights_hi"), m.sem("r_weights_split")
        block = ctx.enter_context(nc.Block())
        lg = logits[:].rearrange("p (t e) -> p t e", t=NT)

        @block.sync
        def _(sp):
            sp.dma_start(before[:], before_dram).then_inc(before_in, 16)
            for place, array in loads:
                sp.dma_start(place, array).then_inc(loaded, 16)

        @block.gpsimd
        def _(pool):
            pool.iota(lane_i[:], pattern=[[0, NT], [1, E]], base=0, channel_multiplier=0).then_inc(lanes_set, 1)
            pool.wait_ge(lanes_set, 1)
            pool.iota(spare_i[:], pattern=[[0, 1]], base=SLOTS, channel_multiplier=1).then_inc(lanes_set, 1)
            for n, (raw, hi, lo) in enumerate(splits):
                pool.wait_ge(weights_hi, n + 1)
                pool.tensor_tensor(lo, raw, hi, ALU.subtract).then_inc(weights_split, 1)

        @block.scalar
        def _(act):
            act.wait_ge(shifted, 1)
            act.activation(probs[:], probs[:], ACT.Exp).then_inc(exp_done, 1)
            act.activation(gate_e[:], lg[:, :, E], ACT.Exp, scale=-1.0).then_inc(exp_done, 1)
            act.wait_ge(loaded, 16 * len(loads))
            for raw, hi, lo in splits:
                act.copy(hi, raw).then_inc(weights_hi, 1)

        @block.tensor
        def _(pe):
            pe.wait_ge(mask_ready, 1)
            flat = mask_b[:].rearrange("p t e -> p (t e)")
            pe.matmul(within_ps[:], before_b[:], flat, start=True, stop=True)
            pe.matmul(sum_ps[:], ones_b[:], flat, start=True, stop=True).then_inc(counted, 1)
            pe.wait_ge(weights_split, len(splits))
            gate_and_up_products(pe, xfT, 0, first_split, first_banks)

        @block.vector
        def _(dve):
            c = Chain(dve, chain)

            def over_experts(a):
                return a[:].rearrange("p (t o) -> p t o", o=1).to_broadcast([P, NT, E])

            c.link(dve.tensor_reduce(rowmax[:], lg[:, :, 0:E], AX.X, ALU.max))
            dve.tensor_tensor(probs[:], lg[:, :, 0:E], over_experts(rowmax), ALU.subtract).then_inc(shifted, 1)
            dve.wait_ge(lanes_set, 2)
            dve.wait_ge(before_in, 16)
            dve.tensor_copy(lane[:], lane_i[:])
            dve.tensor_copy(spare[:], spare_i[:])
            dve.tensor_copy(before_b[:], before[:])
            dve.memset(ones_b[:], 1.0)
            dve.wait_ge(exp_done, 2)
            c.link(dve.tensor_reduce(rowsum[:], probs[:], AX.X, ALU.add))
            c.link(dve.reciprocal(rowsum[:], rowsum[:]))
            c.link(dve.tensor_tensor(probs[:], probs[:], over_experts(rowsum), ALU.mult))
            c.link(dve.tensor_scalar(gate_e[:], gate_e[:], 1.0, None, ALU.add))
            dve.reciprocal(shared_gate[:], gate_e[:])
            for t in range(NT):
                last = dve.max(top[:, t], probs[:, t])
            c.link(last)
            for t in range(NT):
                last = dve.max_index(top_at[:, t], top[:, t], probs[:, t])
            c.link(last)
            c.link(dve.tensor_copy(expert[:], top_at[:, :, 0:K]))
            for k in range(K):
                last = dve.tensor_tensor(chosen[k][:], lane[:],
                                         expert[:, :, k:k + 1].to_broadcast([P, NT, E]), ALU.is_equal)
            c.link(last)
            c.link(dve.tensor_tensor(mask[:], chosen[0][:], chosen[1][:], ALU.add))
            c.link(dve.tensor_tensor(mask[:], mask[:], chosen[2][:], ALU.add))
            dve.tensor_tensor(mask_b[:], mask[:], chosen[3][:], ALU.add).then_inc(mask_ready, 1)
            c.link(dve.memset(prefix[:, 0], 0.0))
            dve.wait_ge(counted, 1)
            c.link(dve.tensor_copy(tile_sum[:], sum_ps[:].rearrange("p (t e) -> p t e", t=NT)))
            for t in range(NT):
                c.link(dve.tensor_tensor(prefix[:, t + 1], prefix[:, t], tile_sum[:, t], ALU.add))
            c.link(dve.tensor_tensor(at[:], within_ps[:].rearrange("p (t e) -> p t e", t=NT),
                                     prefix[:, 0:NT], ALU.add))
            for k in range(K):
                c.link(dve.tensor_tensor(picked[:], chosen[k][:], at[:], ALU.mult))
                c.link(dve.tensor_reduce(place[:, :, k], picked[:], AX.X, ALU.add))
            c.link(dve.tensor_scalar(fits[:], place[:], float(CAP), None, ALU.is_lt))
            c.link(dve.tensor_scalar(tile_of[:], place[:], float(P), float(1 - P * E * ST), ALU.is_ge, ALU.mult))
            c.link(dve.scalar_tensor_tensor(out=slot[:], in0=place[:], scalar=float(E * ST), in1=tile_of[:],
                                            op0=ALU.mult, op1=ALU.add))
            c.link(dve.scalar_tensor_tensor(out=slot[:], in0=expert[:], scalar=float(ST), in1=slot[:],
                                            op0=ALU.mult, op1=ALU.add))
            c.link(dve.scalar_tensor_tensor(out=slot[:], in0=slot[:], scalar=spare[:, 0:1], in1=fits[:],
                                            op0=ALU.subtract, op1=ALU.mult))
            dve.tensor_scalar(slots[:], slot[:].rearrange("p t k -> p (t k)"), spare[:, 0:1], None, ALU.add)
            dve.tensor_tensor(best[:].rearrange("p (t k) -> p t k", k=K), top[:, :, 0:K], fits[:], ALU.mult)


def shared_tile(sw_gate, sw_up, sw_down, col):
    return (sw_gate.rearrange("(k p) f -> p k f", p=P)[:, :, ds(col, P)],
            sw_up.rearrange("(k p) f -> p k f", p=P)[:, :, ds(col, P)], sw_down[ds(col, P), :])


def shared_expert(nc, sw_gate, sw_up, sw_down, raw, first_split, gp, up, ids_dram, y_dram, xfT, slots,
                  shared_gate, acc, tables, tokens_dram, ids, ids_first, xg_first):
    with ExitStack() as ctx:
        m = Mem(nc, ctx)
        split = [first_split, [m.sb("s_wg1", [P, 2, KC, P], F32R), m.sb("s_wu1", [P, 2, KC, P], F32R),
                               m.sb("s_wd1", [P, 2, C], F32R)]]
        wd = [of_tile[2] for of_tile in split]
        silu, hid_full = m.sb("s_silu", [P, 2, QC]), m.sb("s_hid_full", [P, 2, QC])
        hid = m.sb("s_hid", [P, 2, 2, QC], F32R)
        zero_ids, zero_row = m.sb("s_zero_ids", [P, SLOTS // P + 1], I32), m.sb("s_zero_row", [P, C])
        slot4 = m.sb("s_slot4", [P, 2 * K], I32)
        token, step = m.sb("s_token", [P, 2], I32), m.sb("s_step", [P, 2], I32)
        dp = m.ps("s_d", [P, QT, C])
        w_in = [m.sem(f"s_w_in{b}") for b in range(2)]
        w_hi, w_split = m.sem("s_w_hi"), m.sem("s_w_split")
        gu_ready, silu_done = m.sem("s_gu_ready"), m.sem("s_silu_done")
        hid_done = m.sem("s_hid_done")
        hid_hi, hid_split = m.sem("s_hid_hi"), m.sem("s_hid_split")
        down_ready = m.sem("s_down_ready")
        down_used = m.sem("s_down_used")
        zeros_set, zeros_in = m.sem("s_zeros_set"), m.sem("s_zeros_in")
        token_set, slot4_set = m.sem("s_token_set"), m.sem("s_slot4_set")
        ids_in, held = m.sem("s_ids_in"), m.sem("s_held")
        tables_in, all_scattered = m.sem("s_tables_in"), m.sem("s_all_scattered")
        ids_loaded, ids_copied, xg_in = m.sem("s_ids_loaded"), m.sem("s_ids_copied"), m.sem("s_xg_in")
        block = ctx.enter_context(nc.Block())
        LAST = NFS - 1
        assert NFS % 2 == 1

        @block.sync
        def _(sp):
            def load(b, col):
                for place, array in zip(raw[b], shared_tile(sw_gate, sw_up, sw_down, col)):
                    sp.dma_start(place[:], array).then_inc(w_in[b], 16)

            sp.wait_ge(zeros_set, 2)
            sp.dma_start(ids_dram.rearrange("(p n) o -> p (n o)", p=P), zero_ids[:]).then_inc(zeros_in, 16)
            sp.dma_start(y_dram[SLOTS:SLOTS + P, :], zero_row[:]).then_inc(zeros_in, 16)
            with sp.Fori(0, NFS // 2 - 1) as i:
                col = [sp.snap(i * (2 * P) + (b + 2) * P) for b in range(2)]
                for b in range(2):
                    sp.wait_ge(w_split, i * 6 + 3 * (b + 1))
                    load(b, col[b])
            sp.wait_ge(w_split, 3 * LAST - 3)
            load(0, LAST * P)
            for place, table in tables:
                sp.dma_start(place, table).then_inc(tables_in, 16)
            sp.wait_ge(all_scattered, 1)
            sp.dma_start(ids[:], ids_dram[0:SLOTS, :].rearrange("(p n) o -> p (n o)", p=P)).then_inc(ids_loaded, 16)
            sp.wait_ge(ids_loaded, 16)
            sp.wait_ge(zeros_in, 32)
            sp.wait_ge(tables_in, 16 * len(tables))

        @block.gpsimd
        def _(pool):
            pool.iota(token[:], pattern=[[P, 2]], base=0, channel_multiplier=1).then_inc(token_set, 1)
            pool.wait_ge(token_set, 1)
            pool.iota(step[:], pattern=[[0, 2]], base=2 * P, channel_multiplier=0).then_inc(token_set, 1)
            pool.wait_ge(token_set, 2)
            pool.wait_ge(zeros_in, 32)
            with pool.Fori(0, NT // 2) as i:
                pool.tensor_copy(slot4[:], slots[:, ds(i * (2 * K), 2 * K)]).then_inc(slot4_set, 1)
                pool.wait_ge(slot4_set, i + 1)
                hold(pool, held)
                for b in range(2):
                    for k in range(K):
                        n = b * K + k
                        pool.indirect_dma_start(
                            ids_dram, bass.IndirectOffsetOnAxis(ap=slot4[:, n:n + 1].bitcast(U32), axis=0),
                            token[:, b:b + 1], None).then_inc(ids_in, 16)
                        pool.wait_ge(ids_in, i * (2 * K * 16) + 16 * (n + 1))
                        hold(pool, held)
                pool.tensor_tensor(token[:], token[:], step[:], ALU.add).then_inc(token_set, 1)
                pool.wait_ge(token_set, i + 3)
            pool.wait_ge(ids_in, NT * K * 16)
            pool.sem_inc(all_scattered, 1)
            pool.wait_ge(ids_loaded, 16)
            pool.tensor_copy(ids_first[:], ids[:, 0:ST]).then_inc(ids_copied, 1)
            pool.wait_ge(ids_copied, 1)
            for t in range(ST):
                pool.indirect_dma_start(
                    xg_first[:, t], None, tokens_dram,
                    bass.IndirectOffsetOnAxis(ap=ids_first[:, t:t + 1].bitcast(U32), axis=0)).then_inc(xg_in, 16)
            pool.wait_ge(xg_in, 16 * ST)

        @block.tensor
        def _(pe):
            def gate_and_up(f, b, c):
                if c == 0:
                    pe.wait_ge(w_split, f * 3 + 3)
                pe.wait_ge(hid_done, f * NQ + (c + 1))
                gate_and_up_products(pe, xfT, c, split[b][0:2], (gp[:, c % 2], up[:, c % 2])).then_inc(gu_ready, 1)

            def down(f, b, c):
                pe.wait_ge(hid_split, f * NQ + (c + 1))
                for t in range(QT):
                    pe.wait_ge(down_used, f * (NQ * QT) + (c * QT + t + 1))
                    for part, (of_w, of_h) in enumerate(PRODUCTS):
                        last = pe.matmul(dp[:, t], hid[:, c % 2, of_h, t * P:(t + 1) * P], wd[b][:, of_w],
                                         start=(part == 0), stop=(part == 2))
                    last.then_inc(down_ready, 1)

            def tile(f, b, last=False):
                for c in range(NQ):
                    if c < NQ - 1:
                        gate_and_up(f, b, c + 1)
                    elif not last:
                        gate_and_up(f + 1, 1 - b, 0)
                    down(f, b, c)

            pe.sem_inc(gu_ready, 1)
            with pe.Fori(0, NFS // 2) as i:
                for b in range(2):
                    tile(i * 2 + b, b)
            tile(LAST, 0, last=True)

        @block.scalar
        def _(act):
            def split_weights(b, i):
                act.wait_ge(w_in[b], i * 48 + 1)
                for of_raw, of_split in zip(raw[b], split[b]):
                    act.copy(of_split[:, 0], of_raw[:]).then_inc(w_hi, 1)

            def hidden(f, c):
                act.wait_ge(gu_ready, f * NQ + (c + 1))
                act.activation(silu[:, c % 2], gp[:, c % 2], ACT.Silu).then_inc(silu_done, 1)
                act.wait_ge(hid_done, f * NQ + (c + 3))
                act.copy(hid[:, c % 2, 0], hid_full[:, c % 2]).then_inc(hid_hi, 1)

            act.sem_inc(w_hi, 3)
            with act.Fori(0, NFS // 2) as i:
                for b in range(2):
                    for c in range(NQ):
                        hidden(i * 2 + b, c)
                        if c == 1:
                            split_weights(1 - b, i + b)
            for c in range(NQ):
                hidden(LAST, c)

        @block.vector
        def _(dve):
            dve.memset(zero_ids[:], 0).then_inc(zeros_set, 1)
            dve.memset(zero_row[:], 0.0).then_inc(zeros_set, 1)
            dve.sem_inc(hid_done, 2)
            dve.sem_inc(down_used, QT)
            dve.sem_inc(w_split, 3)
            for b in range(2):
                dve.sem_inc(w_in[b], 1)

            def split_weights(b, f):
                for n, (of_raw, of_split) in enumerate(zip(raw[b], split[b])):
                    dve.wait_ge(w_hi, f * 3 + (n + 1))
                    dve.tensor_tensor(of_split[:, 1], of_raw[:], of_split[:, 0], ALU.subtract).then_inc(w_split, 1)

            def hidden_full(f, c):
                dve.wait_ge(silu_done, f * NQ + (c + 1))
                dve.tensor_tensor(hid_full[:, c % 2], up[:, c % 2], silu[:, c % 2], ALU.mult).then_inc(hid_done, 1)

            def hidden_lo(f, c):
                dve.wait_ge(hid_hi, f * NQ + (c + 1))
                dve.tensor_tensor(hid[:, c % 2, 1], hid_full[:, c % 2], hid[:, c % 2, 0],
                                  ALU.subtract).then_inc(hid_split, 1)

            def accumulate(f, c, tiles):
                for t in tiles:
                    n = c * QT + t
                    dve.wait_ge(down_ready, f * (NQ * QT) + (n + 1))
                    acc_t = acc[:, n * C:(n + 1) * C]
                    dve.scalar_tensor_tensor(out=acc_t, in0=dp[:, t], scalar=shared_gate[:, n:n + 1], in1=acc_t,
                                             op0=ALU.mult, op1=ALU.add).then_inc(down_used, 1)

            def tile(f, b, last=False):
                for c in range(NQ):
                    following = (f, c + 1) if c < NQ - 1 else None if last else (f + 1, 0)
                    if following:
                        hidden_full(*following)
                    accumulate(f, c, range(0, QT // 2))
                    if following:
                        hidden_lo(*following)
                    accumulate(f, c, range(QT // 2, QT))
                    if c == 1 and not last:
                        split_weights(1 - b, f + 1)

            hidden_full(0, 0)
            hidden_lo(0, 0)
            with dve.Fori(0, NFS // 2) as i:
                for b in range(2):
                    tile(i * 2 + b, b)
            tile(LAST, 0, last=True)


def experts(nc, w_gate, w_up, w_down, tokens_dram, y_dram, ident, ids, first):
    NF = len(FT)
    KH = KC // 2
    with ExitStack() as ctx:
        m = Mem(nc, ctx)
        wg_raw, wu_raw = ([first[n], m.sb(f"e_{n}_raw1", [P, KC, F])] for n in ("wg", "wu"))
        wd_raw = [first["wd"], m.sb("e_wd_raw1", [P, NF, C])]
        wg, wu = ([m.sb(f"e_{n}{b}", [P, 2, KC, F], F32R) for b in range(2)] for n in ("wg", "wu"))
        wd = [m.sb(f"e_wd{b}", [P, 2, NF, C], F32R) for b in range(2)]
        ids_now = [first["ids"], m.sb("e_ids_now1", [P, ST], I32)]
        xg = [first["xg"], m.sb("e_xg1", [P, ST, C])]
        xgT = m.sb("e_xgT", [P, 2, KC, CAP], F32R)
        silu, hid_full = m.sb("e_silu", [P, NF, CAP]), m.sb("e_hid_full", [P, NF, CAP])
        hid = m.sb("e_hid", [P, 2, NF, CAP], F32R)
        y = [m.sb(f"e_y{b}", [P, ST, C]) for b in range(2)]
        tp = m.ps("e_tp", [P, ST, KC, P])
        gu = m.ps("e_gu", [P, NF, 2, CAP])
        dp = m.ps("e_d", [P, ST, C])
        ids_copied, held = m.sem("e_ids_copied"), m.sem("e_held")
        gate_in = [m.sem(f"e_gate_in{b}") for b in range(2)]
        up_in = [m.sem(f"e_up_in{b}") for b in range(2)]
        down_in = [m.sem(f"e_down_in{b}") for b in range(2)]
        w_hi = m.sem("e_w_hi")
        gate_split, up_split, down_split = m.sem("e_gate_split"), m.sem("e_up_split"), m.sem("e_down_split")
        xg_in = [m.sem(f"e_xg_in{b}") for b in range(2)]
        turned, xg_hi, xg_split = m.sem("e_turned"), m.sem("e_xg_hi"), m.sem("e_xg_split")
        gu_ready, silu_done = m.sem("e_gu_ready"), m.sem("e_silu_done")
        hid_done = m.sem("e_hid_done")
        hid_hi, hid_split = m.sem("e_hid_hi"), m.sem("e_hid_split")
        down_ready = m.sem("e_down_ready")
        y_copied = m.sem("e_y_copied")
        y_stored = [m.sem(f"e_y_stored{b}") for b in range(2)]
        block = ctx.enter_context(nc.Block())
        N_HI = 2 + 2 + NF

        def gate_up_parts(b, raw, split):
            return [(raw[b][:, h * KH:(h + 1) * KH], split[b][:, 0, h * KH:(h + 1) * KH],
                     split[b][:, 1, h * KH:(h + 1) * KH]) for h in range(2)]

        def down_parts(b):
            return [(wd_raw[b][0:w, n], wd[b][0:w, 0, n], wd[b][0:w, 1, n]) for n, (f0, w) in enumerate(FT)]

        @block.sync
        def _(sp):
            def load_gate_up(b, row):
                for raw, w_dram, loaded in ((wg_raw, w_gate, gate_in), (wu_raw, w_up, up_in)):
                    sp.dma_start(raw[b][:], w_dram[ds(row, C), :].rearrange("(k p) f -> p k f", p=P))\
                        .then_inc(loaded[b], 16)

            def load_down(b, frow, frow_rest):
                sp.dma_start(wd_raw[b][:, 0:2], w_down[ds(frow, 2 * P), :].rearrange("(f p) n -> p f n", p=P))\
                    .then_inc(down_in[b], 16)
                sp.dma_start(wd_raw[b][0:FT[2][1], 2], w_down[ds(frow_rest, FT[2][1]), :])\
                    .then_inc(down_in[b], 16)

            load_gate_up(1, C)
            load_down(1, F, F + FT[2][0])
            with sp.Fori(0, E // 2 - 1) as i:
                row = [sp.snap(i * (2 * C) + (b + 2) * C) for b in range(2)]
                frow = [sp.snap(i * (2 * F) + (b + 2) * F) for b in range(2)]
                frow_rest = [sp.snap(i * (2 * F) + ((b + 2) * F + FT[2][0])) for b in range(2)]
                for b in range(2):
                    sp.wait_ge(gate_split, i * 4 + 2 * (b + 1))
                    sp.wait_ge(up_split, i * 4 + 2 * (b + 1))
                    load_gate_up(b, row[b])
                    sp.wait_ge(down_split, i * (2 * NF) + NF * (b + 1))
                    load_down(b, frow[b], frow_rest[b])

        @block.gpsimd
        def _(pool):
            def gather(b, col, e):
                pool.tensor_copy(ids_now[b][:], ids[:, ds(col, ST)]).then_inc(ids_copied, 1)
                pool.wait_ge(ids_copied, e)
                hold(pool, held)
                for t in range(ST):
                    pool.indirect_dma_start(
                        xg[b][:, t], None, tokens_dram,
                        bass.IndirectOffsetOnAxis(ap=ids_now[b][:, t:t + 1].bitcast(U32), axis=0))\
                        .then_inc(xg_in[b], 16)

            def split_up_down(b, e):
                for n, (raw, hi, lo) in enumerate(gate_up_parts(b, wu_raw, wu)):
                    pool.wait_ge(w_hi, e * N_HI + (3 + n))
                    hold(pool, held)
                    pool.tensor_tensor(lo, raw, hi, ALU.subtract).then_inc(up_split, 1)
                for n, (raw, hi, lo) in enumerate(down_parts(b)):
                    pool.wait_ge(w_hi, e * N_HI + (5 + n))
                    hold(pool, held)
                    pool.tensor_tensor(lo, raw, hi, ALU.subtract).then_inc(down_split, 1)

            gather(1, ST, 1)
            split_up_down(0, 0)
            with pool.Fori(0, E // 2 - 1) as i:
                for b in range(2):
                    pool.wait_ge(turned, i * (2 * ST) + ST * (b + 1))
                    hold(pool, held)
                    gather(b, i * (2 * ST) + ST * (b + 2), i * 2 + (b + 2))
                    split_up_down(1 - b, i * 2 + (b + 1))
            split_up_down(1, E - 1)

        @block.tensor
        def _(pe):
            def turn(b, i, in_place=False):
                if not in_place:
                    pe.wait_ge(xg_in[b], i * (16 * ST) + (16 * ST if b else 0))
                for t in range(ST):
                    for k in range(KC):
                        last = pe.transpose(tp[:, t, k], xg[b][:, t, k * P:(k + 1) * P], ident[:])
                    last.then_inc(turned, 1)

            def gate_and_up(b, e):
                pe.wait_ge(xg_split, e * ST + ST)
                pe.wait_ge(gate_split, e * 2 + 2)
                pe.wait_ge(up_split, e * 2 + 2)
                for n, (f0, w) in enumerate(FT):
                    pe.wait_ge(hid_done, e * NF + (n + 1))
                    for s, weights in enumerate((wg, wu)):
                        for k in range(KC):
                            for part, (of_w, of_x) in enumerate(PRODUCTS):
                                last = pe.matmul(gu[0:w, n, s], weights[b][:, of_w, k, f0:f0 + w], xgT[:, of_x, k],
                                                 start=(k == 0 and part == 0), stop=(k == KC - 1 and part == 2))
                    last.then_inc(gu_ready, 1)

            def down(b, e):
                pe.wait_ge(y_copied, e * ST + ST)
                pe.wait_ge(down_split, e * NF + NF)
                for n, (f0, w) in enumerate(FT):
                    pe.wait_ge(hid_split, e * NF + (n + 1))
                    for t in range(ST):
                        for part, (of_w, of_h) in enumerate(PRODUCTS):
                            last = pe.matmul(dp[:, t], hid[0:w, of_h, n, t * P:(t + 1) * P], wd[b][0:w, of_w, n],
                                             start=(n == 0 and part == 0), stop=(n == NF - 1 and part == 2))
                        if n == NF - 1:
                            last.then_inc(down_ready, 1)

            turn(0, 0, in_place=True)
            with pe.Fori(0, E // 2 - 1) as i:
                for b in range(2):
                    gate_and_up(b, i * 2 + b)
                    turn(1 - b, i + b)
                    down(b, i * 2 + b)
            gate_and_up(0, E - 2)
            turn(1, E // 2 - 1)
            down(0, E - 2)
            gate_and_up(1, E - 1)
            down(1, E - 1)

        @block.scalar
        def _(act):
            act.sem_inc(y_copied, ST)
            for b in range(2):
                act.sem_inc(y_stored[b], 1)

            def arrived(b, i, per):
                return i * per + (per if b else 0)

            def split_hi(parts, loaded, count):
                if count is not None:
                    act.wait_ge(loaded, count)
                for raw, hi, _ in parts:
                    act.copy(hi, raw).then_inc(w_hi, 1)

            def split_gate(b, i):
                split_hi(gate_up_parts(b, wg_raw, wg), gate_in[b], arrived(b, i, 16))

            def split_up(b, i):
                split_hi(gate_up_parts(b, wu_raw, wu), up_in[b], arrived(b, i, 16))

            def split_down(b, i):
                split_hi(down_parts(b), down_in[b], arrived(b, i, 32))

            def tokens_hi(e):
                for t in range(ST):
                    act.wait_ge(turned, e * ST + (t + 1))
                    act.copy(xgT[:, 0, :, t * P:(t + 1) * P], tp[:, t]).then_inc(xg_hi, 1)

            def hidden(e, n):
                w = FT[n][1]
                act.wait_ge(gu_ready, e * NF + (n + 1))
                act.activation(silu[0:w, n], gu[0:w, n, 0], ACT.Silu).then_inc(silu_done, 1)
                act.wait_ge(hid_done, e * NF + (n + 1 + NF))
                act.copy(hid[0:w, 0, n], hid_full[0:w, n]).then_inc(hid_hi, 1)

            def results(b, e, i, y_row):
                for t in range(ST):
                    act.wait_ge(down_ready, e * ST + (t + 1))
                    act.wait_ge(y_stored[b], i * 16 + 1)
                    act.copy(y[b][:, t], dp[:, t]).then_inc(y_copied, 1)
                act.wait_ge(y_copied, e * ST + 2 * ST)
                act.dma_start(y_dram[0:SLOTS, :].rearrange("(p n) c -> p n c", p=P)[:, ds(y_row, ST)], y[b][:])\
                    .then_inc(y_stored[b], 16)

            def expert(b, i, y_row, last=False):
                e = i * 2 + b
                if not last:
                    split_gate(1 - b, i + b)
                hidden(e, 0)
                if not last:
                    split_up(1 - b, i + b)
                hidden(e, 1)
                if not last:
                    split_down(1 - b, i + b)
                hidden(e, 2)
                if not last:
                    tokens_hi(e + 1)
                results(b, e, i, y_row)

            split_hi(gate_up_parts(0, wg_raw, wg), None, None)
            tokens_hi(0)
            split_hi(gate_up_parts(0, wu_raw, wu), None, None)
            split_hi(down_parts(0), None, None)
            with act.Fori(0, E // 2 - 1) as i:
                y_row = [act.snap(i * (2 * ST) + b * ST) for b in range(2)]
                for b in range(2):
                    expert(b, i, y_row[b])
            expert(0, E // 2 - 1, (E - 2) * ST)
            expert(1, E // 2 - 1, (E - 1) * ST, last=True)
            for b in range(2):
                act.wait_ge(y_stored[b], 16 * E // 2 + 1)

        @block.vector
        def _(dve):
            dve.sem_inc(hid_done, NF)

            def split_gate(b, e):
                for n, (raw, hi, lo) in enumerate(gate_up_parts(b, wg_raw, wg)):
                    dve.wait_ge(w_hi, e * N_HI + (n + 1))
                    dve.tensor_tensor(lo, raw, hi, ALU.subtract).then_inc(gate_split, 1)

            def tokens_lo(e):
                for t in range(ST):
                    dve.wait_ge(xg_hi, e * ST + (t + 1))
                    dve.tensor_tensor(xgT[:, 1, :, t * P:(t + 1) * P], tp[:, t], xgT[:, 0, :, t * P:(t + 1) * P],
                                      ALU.subtract).then_inc(xg_split, 1)

            def hidden(e):
                for n, (f0, w) in enumerate(FT):
                    dve.wait_ge(silu_done, e * NF + (n + 1))
                    dve.tensor_tensor(hid_full[0:w, n], gu[0:w, n, 1], silu[0:w, n], ALU.mult).then_inc(hid_done, 1)
                    dve.wait_ge(hid_hi, e * NF + (n + 1))
                    dve.tensor_tensor(hid[0:w, 1, n], hid_full[0:w, n], hid[0:w, 0, n],
                                      ALU.subtract).then_inc(hid_split, 1)

            split_gate(0, 0)
            tokens_lo(0)
            with dve.Fori(0, E // 2 - 1) as i:
                for b in range(2):
                    split_gate(1 - b, i * 2 + (b + 1))
                    hidden(i * 2 + b)
                    tokens_lo(i * 2 + (b + 1))
            split_gate(1, E - 1)
            hidden(E - 2)
            tokens_lo(E - 1)
            hidden(E - 1)


def combine(nc, y_dram, out_dram, x1, acc, best, slots, neg_half):
    NB, PAIRS = 4, NT // 2
    with ExitStack() as ctx:
        m = Mem(nc, ctx)
        slot4 = [m.sb(f"f_slot4{h}", [P, 2 * K], I32) for h in range(2)]
        yk = [m.sb(f"f_y{b}", [P, K, C]) for b in range(NB)]
        total, centred = m.sb("f_total", [P, NB, C]), m.sb("f_centred", [P, NB, C])
        o = m.sb("f_out", [P, NB, C])
        stats, mv = m.sb("f_stats", [P, NB, 6]), m.sb("f_mv", [P, NB, 2])
        negmean = m.sb("f_negmean", [P, NB])
        veps, rstd = m.sb("f_veps", [P, NB]), m.sb("f_rstd", [P, NB])
        held = m.sem("f_held")
        slot4_set = m.sem("f_slot4_set")
        y_in = [m.sem(f"f_y_in{b}") for b in range(NB)]
        y_used = m.sem("f_y_used")
        mean_ready, var_ready, rstd_ready = m.sem("f_mean_ready"), m.sem("f_var_ready"), m.sem("f_rstd_ready")
        centred_done, out_ready = m.sem("f_centred_done"), m.sem("f_out_ready")
        out_stored = [m.sem(f"f_out_stored{b}") for b in range(NB)]
        chain = m.sem("f_chain")
        block = ctx.enter_context(nc.Block())

        @block.gpsimd
        def _(pool):
            def gather(pair, h):
                pool.wait_ge(y_used, pair)
                hold(pool, held)
                pool.tensor_copy(slot4[h][:], slots[:, ds(pair * (2 * K), 2 * K)]).then_inc(slot4_set, 1)
                pool.wait_ge(slot4_set, pair + 1)
                hold(pool, held)
                for b in range(2):
                    for k in range(K):
                        n = b * K + k
                        pool.indirect_dma_start(
                            yk[2 * h + b][:, k], None, y_dram,
                            bass.IndirectOffsetOnAxis(ap=slot4[h][:, n:n + 1].bitcast(U32), axis=0))\
                            .then_inc(y_in[2 * h + b], 16)

            def deviation(pair, h):
                pool.wait_ge(var_ready, pair * 2 + 2)
                hold(pool, held)
                for b in range(2 * h, 2 * h + 2):
                    last = pool.tensor_tensor(rstd[:, b:b + 1], veps[:, b:b + 1], neg_half[:], ALU.pow)
                last.then_inc(rstd_ready, 1)

            pool.tensor_copy(slot4[0][:], slots[:, 0:2 * K]).then_inc(slot4_set, 1)
            pool.wait_ge(slot4_set, 1)
            for b in range(2):
                for k in range(K):
                    n = b * K + k
                    pool.indirect_dma_start(
                        yk[b][:, k], None, y_dram,
                        bass.IndirectOffsetOnAxis(ap=slot4[0][:, n:n + 1].bitcast(U32), axis=0))\
                        .then_inc(y_in[b], 16)
            with pool.Fori(0, NT // NB - 1) as i:
                for h in range(2):
                    gather(i * 2 + (h + 1), 1 - h)
                    deviation(i * 2 + h, h)
            gather(PAIRS - 1, 1)
            deviation(PAIRS - 2, 0)
            deviation(PAIRS - 1, 1)

        @block.vector
        def _(dve):
            dve.sem_inc(y_used, 1)
            for b in range(NB):
                dve.sem_inc(out_stored[b], 1)
            PER_PAIR = 2 * K + 4

            def sums(pair, h, i):
                at = pair * PER_PAIR
                for k in range(K):
                    for b in range(2):
                        bb = 2 * h + b
                        if k == 0:
                            dve.wait_ge(y_in[bb], i * (16 * K) + 16 * K)
                            so_far = acc[:, ds(pair * (2 * C) + b * C, C)]
                        else:
                            dve.wait_ge(chain, at + (2 * (k - 1) + b + 1))
                            so_far = total[:, bb]
                        dve.scalar_tensor_tensor(
                            out=total[:, bb], in0=yk[bb][:, k], scalar=best[:, ds(pair * (2 * K) + (b * K + k), 1)],
                            in1=so_far, op0=ALU.mult, op1=ALU.add).then_inc(chain, 1)
                dve.sem_inc(y_used, 1)
                for b in range(2):
                    bb = 2 * h + b
                    dve.wait_ge(chain, at + (2 * (K - 1) + b + 1))
                    dve.bn_stats(stats[:, bb], total[:, bb]).then_inc(chain, 1)
                for b in range(2):
                    bb = 2 * h + b
                    dve.wait_ge(chain, at + (2 * K + b + 1))
                    hold(dve, held)
                    dve.bn_aggr(mv[:, bb], stats[:, bb]).then_inc(chain, 1)
                for b in range(2):
                    bb = 2 * h + b
                    dve.wait_ge(chain, at + (2 * K + 2 + b + 1))
                    dve.tensor_scalar(veps[:, bb:bb + 1], mv[:, bb, 1:2], LN_EPS, None,
                                      ALU.add).then_inc(var_ready, 1)
                    dve.tensor_scalar(negmean[:, bb:bb + 1], mv[:, bb, 0:1], -1.0, None,
                                      ALU.mult).then_inc(mean_ready, 1)

            def finish(pair, h, i):
                dve.wait_ge(rstd_ready, pair + 1)
                for b in range(2):
                    bb = 2 * h + b
                    dve.wait_ge(centred_done, pair * 2 + (b + 1))
                    dve.wait_ge(out_stored[bb], i * 16 + 1)
                    dve.scalar_tensor_tensor(out=o[:, bb], in0=centred[:, bb], scalar=rstd[:, bb:bb + 1],
                                             in1=x1[:, ds(pair * (2 * C) + b * C, C)], op0=ALU.mult,
                                             op1=ALU.add).then_inc(out_ready, 1)

            sums(0, 0, 0)
            with dve.Fori(0, NT // NB - 1) as i:
                for h in range(2):
                    sums(i * 2 + (h + 1), 1 - h, i + h)
                    finish(i * 2 + h, h, i)
            sums(PAIRS - 1, 1, NT // NB - 1)
            finish(PAIRS - 2, 0, NT // NB - 1)
            finish(PAIRS - 1, 1, NT // NB - 1)

        @block.scalar
        def _(act):
            act.sem_inc(out_ready, NB)
            with act.Fori(0, NT // NB) as i:
                for b in range(NB):
                    act.wait_ge(mean_ready, i * NB + (b + 1))
                    act.wait_ge(out_ready, i * NB + (b + 1))
                    act.activation(centred[:, b], total[:, b], ACT.Identity, bias=negmean[:, b:b + 1])\
                        .then_inc(centred_done, 1)

        @block.sync
        def _(sp):
            with sp.Fori(0, NT // NB) as i:
                row = [sp.snap(i * (NB * P) + b * P) for b in range(NB)]
                for b in range(NB):
                    sp.wait_ge(out_ready, i * NB + (b + 1 + NB))
                    sp.dma_start(out_dram[ds(row[b], P), :], o[:, b]).then_inc(out_stored[b], 16)
            for b in range(NB):
                sp.wait_ge(out_stored[b], 16 * NT // NB + 1)


def sandwich(nc, a, out):
    x_rows = a["x"]
    ctx_dram = nc.dram_tensor("ctx_scratch", [C, T], F32).ap()
    tokens_dram = nc.dram_tensor("tokens_scratch", [T, C], F32).ap()
    ids_dram = nc.dram_tensor("ids_scratch", [SLOTS + P, 1], I32).ap()
    y_dram = nc.dram_tensor("y_scratch", [SLOTS + P, C], F32).ap()
    with ExitStack() as ctx:
        m = Mem(nc, ctx)
        ident, neg_half = m.sb("ident", [P, P]), m.sb("neg_half", [P, 1])
        with ExitStack() as part:
            xnT = Mem(nc, part).sb("xnT", [P, KC, T])
            p = Mem(nc, part)
            cos, sin, rotate = p.sb("rope_cos", [P, T]), p.sb("rope_sin", [P, T]), p.sb("rope_rotate", [P, P])
            wq, wk, wv = (p.sb(f"{n}_g", [P, KC, P]) for n in ("wq", "wk", "wv"))
            first_group = slice(0, P)
            tables = [(wq[:], head_columns(a["wq_t"], first_group)), (wk[:], head_columns(a["wk_t"], first_group)),
                      (wv[:], head_columns(a["wv_t"], first_group)), (rotate[:], a["rope_rotate"]),
                      (cos[:], a["rope_cos"]), (sin[:], a["rope_sin"])]
            norm_and_transpose(nc, x_rows, a["identity"], tables, ident, neg_half, xnT)
            attention(nc, a["wq_t"], a["wk_t"], a["wv_t"], ctx_dram, ident, xnT, cos, sin, rotate, wq, wk, wv)
        x1, acc = m.sb("x1", [P, NT * C]), m.sb("acc", [P, NT * C])
        best, slots = m.sb("best", [P, NT * K]), m.sb("slots", [P, NT * K], I32)
        shared_gate = m.sb("shared_gate", [P, NT])
        first = {"wg": m.sb("e_wg_raw0", [P, KC, F]), "wu": m.sb("e_wu_raw0", [P, KC, F]),
                 "wd": m.sb("e_wd_raw0", [P, len(FT), C]), "ids": m.sb("e_ids_now0", [P, ST], I32),
                 "xg": m.sb("e_xg0", [P, ST, C])}
        ids = m.sb("e_ids", [P, E * ST], I32)
        tables = [(first["wg"][:], a["w_gate"][0:C, :].rearrange("(k p) f -> p k f", p=P)),
                  (first["wu"][:], a["w_up"][0:C, :].rearrange("(k p) f -> p k f", p=P)),
                  *((first["wd"][0:w, n], a["w_down"][f0:f0 + w, :]) for n, (f0, w) in enumerate(FT))]
        with ExitStack() as part:
            xfT = Mem(nc, part).sb("xfT", [P, 2, KC, T], F32R)
            logits = Mem(nc, part).sb("logits", [P, NT * (E + 1)])
            layer_norms(nc, x_rows, ctx_dram, a["wo_t"], a["w_norm"], a["w_router"], a["w_shared_gate"],
                        tokens_dram, ident, neg_half, x1, acc, xfT, logits)
            shared_weights = a["sw_gate"], a["sw_up"], a["sw_down"]
            p = Mem(nc, part)
            raw = [[p.sb(f"s_wg_raw{b}", [P, KC, P]), p.sb(f"s_wu_raw{b}", [P, KC, P]), p.sb(f"s_wd_raw{b}", [P, C])]
                   for b in range(2)]
            split = [p.sb("s_wg0", [P, 2, KC, P], F32R), p.sb("s_wu0", [P, 2, KC, P], F32R),
                     p.sb("s_wd0", [P, 2, C], F32R)]
            gp, up = p.ps("s_g", [P, 2, QC]), p.ps("s_u", [P, 2, QC])
            route(nc, a["before"], logits, best, slots, shared_gate,
                  [(place[:], array) for b in range(2)
                   for place, array in zip(raw[b], shared_tile(*shared_weights, b * P))],
                  [(of_raw[:], of_split[:, 0], of_split[:, 1]) for of_raw, of_split in zip(raw[0], split)],
                  xfT, split[0:2], (gp[:, 0], up[:, 0]))
            shared_expert(nc, *shared_weights, raw, split, gp, up, ids_dram, y_dram, xfT, slots,
                          shared_gate, acc, tables, tokens_dram, ids, first["ids"], first["xg"])
        experts(nc, a["w_gate"], a["w_up"], a["w_down"], tokens_dram, y_dram, ident, ids, first)
        combine(nc, y_dram, out, x1, acc, best, slots, neg_half)


def shape_constants():
    import numpy as np

    f32 = np.float32
    inv_freq = (f32(1.0) / f32(10000.0) ** (np.arange(0, D, 2, dtype=f32) / f32(D))).astype(f32)
    freqs = np.outer(np.arange(T, dtype=f32), inv_freq).astype(f32)
    angles = np.concatenate([freqs, freqs], axis=-1).T
    rotate = np.zeros((P, P), f32)
    for j in range(HG):
        for d in range(D // 2):
            rotate[j * D + d + D // 2, j * D + d] = -1.0
            rotate[j * D + d, j * D + d + D // 2] = 1.0
    return {
        "identity": np.eye(P, dtype=f32),
        "rope_cos": np.ascontiguousarray(np.tile(np.cos(angles), (HG, 1))),
        "rope_sin": np.ascontiguousarray(np.tile(np.sin(angles), (HG, 1))),
        "rope_rotate": rotate,
        "before": np.triu(np.ones((P, P), f32), 1),
    }


def kernel(**inputs):
    import numpy as np
    import concourse.bacc as bacc
    from concourse.bass_utils import run_bass_kernel_spmd

    def plain(name):
        return np.ascontiguousarray(inputs[name])

    def turned(name):
        return np.ascontiguousarray(np.asarray(inputs[name]).T)

    arrays = {
        "x": plain("L0_attn_x").reshape(T, C),
        "wq_t": turned("L0_attn_w_q"), "wk_t": turned("L0_attn_w_k"),
        "wv_t": turned("L0_attn_w_v"), "wo_t": turned("L0_attn_w_o"),
        "w_norm": plain("L0_ffn_w_norm").reshape(1, C),
        "w_router": plain("L0_ffn_w_router"),
        "w_shared_gate": plain("L0_ffn_w_shared_gate"),
        "w_gate": plain("L0_ffn_w_gate").reshape(E * C, F),
        "w_up": plain("L0_ffn_w_up").reshape(E * C, F),
        "w_down": plain("L0_ffn_w_down").reshape(E * F, C),
        "sw_gate": plain("L0_ffn_sw_gate"), "sw_up": plain("L0_ffn_sw_up"), "sw_down": plain("L0_ffn_sw_down"),
        **shape_constants(),
    }
    nc = bacc.Bacc("TRN2", target_bir_lowering=False, num_devices=1)
    handles = {n: nc.dram_tensor(f"in_{n}", v.shape, mybir.dt.from_np(v.dtype), kind="ExternalInput").ap()
               for n, v in arrays.items()}
    out = nc.dram_tensor("out", (T, C), F32, kind="ExternalOutput").ap()
    sandwich(nc, handles, out)
    r = run_bass_kernel_spmd(nc, [{f"in_{n}": v for n, v in arrays.items()}], core_ids=[0])
    return r.results[0]["out"].reshape(1, T, C)
```
